# Optimizing a Trainium2 kernel written in Bass

```python
import numpy as np
import jax
import jax.numpy as jnp

def _softmax(x, axis=-1):
    return jax.nn.softmax(x, axis=axis)

def _gelu(x):
    return jax.nn.gelu(x, approximate=True)

def _silu(x):
    return jax.nn.silu(x)

def _sigmoid(x):
    return jax.nn.sigmoid(x)

def _layernorm(x, axis=-1, eps=1e-05):
    m = jnp.mean(x, axis=axis, keepdims=True)
    v = jnp.var(x, axis=axis, keepdims=True)
    return (x - m) / jnp.sqrt(v + eps)

def _scatter_add(tgt, idx, src, axis=0):
    return tgt.at[idx].add(src)

def _segment_sum(src, seg, n):
    return jax.ops.segment_sum(src, seg, n)
kernel_name = 'mk_perceiver_d1_seqx_r8_231b06'

def setup_inputs(seed: int=0):
    np.random.seed(seed)
    _w = jnp.asarray

    def _rec_inputs():
        import jax
        import jax.numpy as jnp
        _rk = jax.random.key(seed)
        x = 7.22e-05 + 1 * jax.random.normal(jax.random.fold_in(_rk, 1), (64, 64, 128), jnp.float32)
        _lenS = 64 - jax.random.randint(jax.random.fold_in(_rk, 7), (64,), 0, max(1, 64 // 4) + 1, jnp.int32)
        _lenS2 = 128 - jax.random.randint(jax.random.fold_in(_rk, 8), (64,), 0, max(1, 128 // 4) + 1, jnp.int32)
        _ctx_1024P = jax.random.normal(jax.random.fold_in(_rk, 11), (64, 16, 128), jnp.float32)
        _ctx_1024c = jax.random.dirichlet(jax.random.fold_in(_rk, 511), 0.3 * jnp.ones((16,), jnp.float32), (64, 128))
        _ctx_1024t = jnp.einsum('bsk,bkd->bsd', _ctx_1024c, _ctx_1024P)
        _ctx_1024t = _ctx_1024t * jax.lax.rsqrt(jnp.mean(jnp.square(_ctx_1024t)) + 1e-12) * 0.953939
        ctx_1024 = 4.13588e-05 + 0.999923 * (_ctx_1024t + 0.3 * jax.random.normal(jax.random.fold_in(_rk, 611), (64, 128, 128), jnp.float32))
        _validS = jnp.arange(64)[None, :] < _lenS[:, None]
        _validS2 = jnp.arange(128)[None, :] < _lenS2[:, None]
        _causal = jnp.tril(jnp.ones((64, 64), dtype=bool))
        mask_SxS2_bk1 = jnp.broadcast_to(_validS2[0:1, :], (64, 128))
        return (x, ctx_1024, mask_SxS2_bk1)
    x, ctx_1024, mask_SxS2_bk1 = _rec_inputs()

    def _L0_xattn_setup():
        import jax, jax.numpy as jnp
        import numpy as np
        B, S, D, H = (4, 256, 128, 16)
        HD = D // H
        key = jax.random.key(seed)
        ks = jax.random.split(key, 16)
        inv = 1.0 / np.sqrt(D)
        inv_hd = 1.0 / np.sqrt(D)
        inp = {'query': jax.random.normal(ks[0], (B, S, D), jnp.float32), 'key': jax.random.normal(ks[1], (B, S, D), jnp.float32), 'value': jax.random.normal(ks[2], (B, S, D), jnp.float32), 'mask': jnp.triu(jnp.ones((S, S), jnp.bool_), k=1), 'Wq': jax.random.normal(ks[3], (D, D), jnp.float32) * inv, 'Wk': jax.random.normal(ks[4], (D, D), jnp.float32) * inv, 'Wv': jax.random.normal(ks[5], (D, D), jnp.float32) * inv, 'wq_h': jax.random.normal(ks[6], (D, HD), jnp.float32) * inv_hd, 'bq_h': jax.random.normal(ks[7], (HD,), jnp.float32) * inv_hd, 'wk_h': jax.random.normal(ks[8], (D, HD), jnp.float32) * inv_hd, 'bk_h': jax.random.normal(ks[9], (HD,), jnp.float32) * inv_hd, 'wv_h': jax.random.normal(ks[10], (D, HD), jnp.float32) * inv_hd, 'bv_h': jax.random.normal(ks[11], (HD,), jnp.float32) * inv_hd, 'Wo': jax.random.normal(ks[12], (D, D), jnp.float32) * inv}
        return inp
    _L0_xattn_all = _L0_xattn_setup()
    _L0_xattn_in = {k: v for k, v in _L0_xattn_all.items() if k in ('Wq', 'Wk', 'Wv', 'wq_h', 'bq_h', 'wk_h', 'bk_h', 'wv_h', 'bv_h', 'Wo')}
    del _L0_xattn_all

    def _L0_attn_setup():
        import jax, jax.numpy as jnp
        import numpy as np
        C = 128
        H = 16
        K = 2
        B, N = (4, 512)

        def _heads(t):
            shp = t.shape
            d = shp[-1] // H
            t = t.reshape(shp[:-1] + (H, d))
            return jnp.swapaxes(t, -2, -3)
        key = jax.random.key(seed)
        ks_ = jax.random.split(key, 12)
        s = 1.0 / np.sqrt(C)
        inp = {'x': jax.random.normal(ks_[0], (B, N, C), dtype=jnp.float32), 'Wq': jax.random.normal(ks_[1], (C, C), dtype=jnp.float32) * s, 'bq': jnp.zeros((C,), dtype=jnp.float32), 'Wk': jax.random.normal(ks_[2], (K, C, C), dtype=jnp.float32) * s, 'bk': jnp.zeros((K, C), dtype=jnp.float32), 'Wv': jax.random.normal(ks_[3], (K, C, C), dtype=jnp.float32) * s, 'bv': jnp.zeros((K, C), dtype=jnp.float32), 'Wo': jax.random.normal(ks_[4], (C, C), dtype=jnp.float32) * s, 'bo': jnp.zeros((C,), dtype=jnp.float32), 'ln_g': jnp.ones((C,), dtype=jnp.float32), 'ln_b': jnp.zeros((C,), dtype=jnp.float32)}
        return inp
    _L0_attn_all = _L0_attn_setup()
    _L0_attn_in = {k: v for k, v in _L0_attn_all.items() if k in ('Wq', 'bq', 'Wk', 'bk', 'Wv', 'bv', 'Wo', 'bo', 'ln_g', 'ln_b')}
    del _L0_attn_all

    def _L0_ffn_setup():
        import jax, jax.numpy as jnp
        import numpy as np
        import math
        B, T, D, H, E, TOPK, CAPF = (4, 256, 128, 16, 8, 2, 2.0)
        HD = D // H

        def layernorm(x, g, b, eps=1e-05):
            m = jnp.mean(x, -1, keepdims=True)
            v = jnp.mean(jnp.square(x - m), -1, keepdims=True)
            return (x - m) * jax.lax.rsqrt(v + eps) * g + b

        def block_forward(x, ln1_g, ln1_b, Wqkv, Wproj, ln2_g, ln2_b, Wgate, W1, b1, W2, b2):
            Bb, Tt, d = x.shape
            hd = HD
            half = hd // 2
            h = layernorm(x, ln1_g, ln1_b)
            qkv = (h @ Wqkv).reshape(Bb, Tt, H, 3 * hd)
            q, k, v = (qkv[..., :hd], qkv[..., hd:2 * hd], qkv[..., 2 * hd:])
            inv_freq = 1.0 / 10000.0 ** (jnp.arange(0, hd, 2, dtype=jnp.float32) / hd)
            ang = jnp.arange(Tt, dtype=jnp.float32)[:, None] * inv_freq
            sin = jnp.sin(ang)[None, :, None, :].astype(x.dtype)
            cos = jnp.cos(ang)[None, :, None, :].astype(x.dtype)

            def rope(t):
                t1, t2 = (t[..., :half], t[..., half:])
                return jnp.concatenate([t1 * cos - t2 * sin, t1 * sin + t2 * cos], -1)
            q, k = (rope(q), rope(k))
            scores = jnp.einsum('bqhd,bkhd->bhqk', q, k) / math.sqrt(hd)
            causal = jnp.tril(jnp.ones((Tt, Tt), dtype=bool))
            scores = jnp.where(causal, scores, jnp.asarray(-1000000000.0, scores.dtype))
            probs = jax.nn.softmax(scores, axis=-1)
            attn = jnp.einsum('bhqk,bkhd->bqhd', probs, v).reshape(Bb, Tt, d) @ Wproj
            x = x + attn
            h2 = layernorm(x, ln2_g, ln2_b)
            flat = h2.reshape(-1, d)
            N = flat.shape[0]
            capacity = int(math.ceil(CAPF * N / E))
            gates = jax.nn.softmax((flat @ Wgate).astype(jnp.float32), -1).astype(flat.dtype)
            _, top_inds = jax.lax.top_k(gates, TOPK)
            mask = jnp.zeros((N, E), dtype=bool).at[jnp.arange(N)[:, None], top_inds].set(True)
            pos = jnp.cumsum(mask.astype(jnp.int32), axis=0) * mask - 1
            keep = (pos < capacity) & mask
            t_flat = jnp.repeat(jnp.arange(N), TOPK)
            e_flat = top_inds.reshape(-1)
            p = pos[t_flat, e_flat]
            kp = keep[t_flat, e_flat]
            p_eff = jnp.where(kp, p, capacity)
            exp_in = jnp.zeros((E, capacity, d), flat.dtype).at[e_flat, p_eff].set(flat[t_flat], mode='drop')
            hmid = jax.nn.gelu(jnp.einsum('ecd,edf->ecf', exp_in, W1) + b1[:, None, :], approximate=False)
            exp_out = jnp.einsum('ecf,efd->ecd', hmid, W2) + b2[:, None, :]
            gate = gates[t_flat, e_flat] * kp.astype(flat.dtype)
            p_g = jnp.minimum(p_eff, capacity - 1)
            moe = jnp.zeros((N, d), flat.dtype).at[t_flat].add(exp_out[e_flat, p_g] * gate[:, None])
            return x + moe.reshape(Bb, Tt, d)
        key = jax.random.key(seed)
        ks = jax.random.split(key, 8)
        s = 0.02
        return {'x': jax.random.normal(ks[0], (B, T, D), jnp.float32), 'ln1_g': jnp.ones((D,), jnp.float32), 'ln1_b': jnp.zeros((D,), jnp.float32), 'Wqkv': jax.random.normal(ks[1], (D, 3 * D), jnp.float32) * s, 'Wproj': jax.random.normal(ks[2], (D, D), jnp.float32) * s, 'ln2_g': jnp.ones((D,), jnp.float32), 'ln2_b': jnp.zeros((D,), jnp.float32), 'Wgate': jax.random.normal(ks[3], (D, E), jnp.float32) * s, 'W1': jax.random.normal(ks[4], (E, D, 4 * D), jnp.float32) * s, 'b1': jnp.zeros((E, 4 * D), jnp.float32), 'W2': jax.random.normal(ks[5], (E, 4 * D, D), jnp.float32) * s, 'b2': jnp.zeros((E, D), jnp.float32)}
    _L0_ffn_all = _L0_ffn_setup()
    _L0_ffn_in = {k: v for k, v in _L0_ffn_all.items() if k in ('ln1_g', 'ln1_b', 'Wqkv', 'Wproj', 'ln2_g', 'ln2_b', 'Wgate', 'W1', 'b1', 'W2', 'b2')}
    del _L0_ffn_all
    return {'x': x, 'ctx_1024': ctx_1024, 'mask_SxS2_bk1': mask_SxS2_bk1, 'L0_xattn_Wq': _L0_xattn_in['Wq'], 'L0_xattn_Wk': _L0_xattn_in['Wk'], 'L0_xattn_Wv': _L0_xattn_in['Wv'], 'L0_xattn_wq_h': _L0_xattn_in['wq_h'], 'L0_xattn_bq_h': _L0_xattn_in['bq_h'], 'L0_xattn_wk_h': _L0_xattn_in['wk_h'], 'L0_xattn_bk_h': _L0_xattn_in['bk_h'], 'L0_xattn_wv_h': _L0_xattn_in['wv_h'], 'L0_xattn_bv_h': _L0_xattn_in['bv_h'], 'L0_xattn_Wo': _L0_xattn_in['Wo'], 'L0_attn_Wq': _L0_attn_in['Wq'], 'L0_attn_bq': _L0_attn_in['bq'], 'L0_attn_Wk': _L0_attn_in['Wk'], 'L0_attn_bk': _L0_attn_in['bk'], 'L0_attn_Wv': _L0_attn_in['Wv'], 'L0_attn_bv': _L0_attn_in['bv'], 'L0_attn_Wo': _L0_attn_in['Wo'], 'L0_attn_bo': _L0_attn_in['bo'], 'L0_attn_ln_g': _L0_attn_in['ln_g'], 'L0_attn_ln_b': _L0_attn_in['ln_b'], 'L0_ffn_ln1_g': _L0_ffn_in['ln1_g'], 'L0_ffn_ln1_b': _L0_ffn_in['ln1_b'], 'L0_ffn_Wqkv': _L0_ffn_in['Wqkv'], 'L0_ffn_Wproj': _L0_ffn_in['Wproj'], 'L0_ffn_ln2_g': _L0_ffn_in['ln2_g'], 'L0_ffn_ln2_b': _L0_ffn_in['ln2_b'], 'L0_ffn_Wgate': _L0_ffn_in['Wgate'], 'L0_ffn_W1': _L0_ffn_in['W1'], 'L0_ffn_b1': _L0_ffn_in['b1'], 'L0_ffn_W2': _L0_ffn_in['W2'], 'L0_ffn_b2': _L0_ffn_in['b2']}

def reference(x, ctx_1024, mask_SxS2_bk1, L0_xattn_Wq, L0_xattn_Wk, L0_xattn_Wv, L0_xattn_wq_h, L0_xattn_bq_h, L0_xattn_wk_h, L0_xattn_bk_h, L0_xattn_wv_h, L0_xattn_bv_h, L0_xattn_Wo, L0_attn_Wq, L0_attn_bq, L0_attn_Wk, L0_attn_bk, L0_attn_Wv, L0_attn_bv, L0_attn_Wo, L0_attn_bo, L0_attn_ln_g, L0_attn_ln_b, L0_ffn_ln1_g, L0_ffn_ln1_b, L0_ffn_Wqkv, L0_ffn_Wproj, L0_ffn_ln2_g, L0_ffn_ln2_b, L0_ffn_Wgate, L0_ffn_W1, L0_ffn_b1, L0_ffn_W2, L0_ffn_b2):
    import jax
    import jax.numpy as jnp

    def _L0_xattn_ref(query, key, value, mask, Wq, Wk, Wv, wq_h, bq_h, wk_h, bk_h, wv_h, bv_h, Wo):
        import jax, jax.numpy as jnp
        import numpy as np
        B, S, D, H = (4, 256, 128, 16)
        HD = D // H
        q = jnp.einsum('bsd,de->bse', query, Wq)
        k = jnp.einsum('bsd,de->bse', key, Wk)
        v = jnp.einsum('bsd,de->bse', value, Wv)
        qh = jnp.einsum('bsd,dh->bsh', q, wq_h) + bq_h
        kh = jnp.einsum('bsd,dh->bsh', k, wk_h) + bk_h
        vh = jnp.einsum('bsd,dh->bsh', v, wv_h) + bv_h
        scores = jnp.einsum('bsh,bth->bst', qh, kh) / jnp.sqrt(jnp.float32(HD))
        scores = jnp.where(mask, jnp.float32(-1000000000.0), scores)
        attn = jax.nn.softmax(scores, axis=-1)
        out_h = jnp.einsum('bst,bth->bsh', attn, vh)
        out = jnp.tile(out_h, (1, 1, H))
        return jnp.einsum('bsd,de->bse', out, Wo)

    def _L0_attn_ref(x, Wq, bq, Wk, bk, Wv, bv, Wo, bo, ln_g, ln_b):
        import jax, jax.numpy as jnp
        import numpy as np
        C = 128
        H = 16
        K = 2
        B, N = (4, 512)

        def _heads(t):
            shp = t.shape
            d = shp[-1] // H
            t = t.reshape(shp[:-1] + (H, d))
            return jnp.swapaxes(t, -2, -3)
        dtype = x.dtype
        q = x + jnp.einsum('bnc,cd->bnd', x, Wq) + bq
        ks = x[None] + jnp.einsum('bnc,kcd->kbnd', x, Wk) + bk[:, None, None, :]
        vs = x[None] + jnp.einsum('bnc,kcd->kbnd', x, Wv) + bv[:, None, None, :]
        q = _heads(q)
        ks = _heads(ks)
        vs = _heads(vs)
        scale = 1.0 / jnp.sqrt(jnp.asarray(N, dtype=jnp.float32))
        ks = ks.astype(jnp.float32) * scale
        vs = vs.astype(jnp.float32) * scale
        states = jnp.einsum('kbhnd,kbhne->kbhde', ks, vs)
        state = jnp.prod(states, axis=0)
        out = jnp.einsum('bhnd,bhde->bhne', q.astype(jnp.float32), state)
        out = out.astype(dtype)
        out = jnp.swapaxes(out, 1, 2).reshape(x.shape[0], x.shape[1], C)
        mu = jnp.mean(out, axis=-1, keepdims=True)
        var = jnp.var(out, axis=-1, keepdims=True)
        out = (out - mu) / jnp.sqrt(var + 1e-05) * ln_g + ln_b
        out = jnp.einsum('bnc,cd->bnd', out, Wo) + bo
        return out

    def _L0_ffn_ref(x, ln1_g, ln1_b, Wqkv, Wproj, ln2_g, ln2_b, Wgate, W1, b1, W2, b2):
        import jax, jax.numpy as jnp
        import numpy as np
        import math
        B, T, D, H, E, TOPK, CAPF = (4, 256, 128, 16, 8, 2, 2.0)
        HD = D // H

        def layernorm(x, g, b, eps=1e-05):
            m = jnp.mean(x, -1, keepdims=True)
            v = jnp.mean(jnp.square(x - m), -1, keepdims=True)
            return (x - m) * jax.lax.rsqrt(v + eps) * g + b

        def block_forward(x, ln1_g, ln1_b, Wqkv, Wproj, ln2_g, ln2_b, Wgate, W1, b1, W2, b2):
            Bb, Tt, d = x.shape
            hd = HD
            half = hd // 2
            h = layernorm(x, ln1_g, ln1_b)
            qkv = (h @ Wqkv).reshape(Bb, Tt, H, 3 * hd)
            q, k, v = (qkv[..., :hd], qkv[..., hd:2 * hd], qkv[..., 2 * hd:])
            inv_freq = 1.0 / 10000.0 ** (jnp.arange(0, hd, 2, dtype=jnp.float32) / hd)
            ang = jnp.arange(Tt, dtype=jnp.float32)[:, None] * inv_freq
            sin = jnp.sin(ang)[None, :, None, :].astype(x.dtype)
            cos = jnp.cos(ang)[None, :, None, :].astype(x.dtype)

            def rope(t):
                t1, t2 = (t[..., :half], t[..., half:])
                return jnp.concatenate([t1 * cos - t2 * sin, t1 * sin + t2 * cos], -1)
            q, k = (rope(q), rope(k))
            scores = jnp.einsum('bqhd,bkhd->bhqk', q, k) / math.sqrt(hd)
            causal = jnp.tril(jnp.ones((Tt, Tt), dtype=bool))
            scores = jnp.where(causal, scores, jnp.asarray(-1000000000.0, scores.dtype))
            probs = jax.nn.softmax(scores, axis=-1)
            attn = jnp.einsum('bhqk,bkhd->bqhd', probs, v).reshape(Bb, Tt, d) @ Wproj
            x = x + attn
            h2 = layernorm(x, ln2_g, ln2_b)
            flat = h2.reshape(-1, d)
            N = flat.shape[0]
            capacity = int(math.ceil(CAPF * N / E))
            gates = jax.nn.softmax((flat @ Wgate).astype(jnp.float32), -1).astype(flat.dtype)
            _, top_inds = jax.lax.top_k(gates, TOPK)
            mask = jnp.zeros((N, E), dtype=bool).at[jnp.arange(N)[:, None], top_inds].set(True)
            pos = jnp.cumsum(mask.astype(jnp.int32), axis=0) * mask - 1
            keep = (pos < capacity) & mask
            t_flat = jnp.repeat(jnp.arange(N), TOPK)
            e_flat = top_inds.reshape(-1)
            p = pos[t_flat, e_flat]
            kp = keep[t_flat, e_flat]
            p_eff = jnp.where(kp, p, capacity)
            exp_in = jnp.zeros((E, capacity, d), flat.dtype).at[e_flat, p_eff].set(flat[t_flat], mode='drop')
            hmid = jax.nn.gelu(jnp.einsum('ecd,edf->ecf', exp_in, W1) + b1[:, None, :], approximate=False)
            exp_out = jnp.einsum('ecf,efd->ecd', hmid, W2) + b2[:, None, :]
            gate = gates[t_flat, e_flat] * kp.astype(flat.dtype)
            p_g = jnp.minimum(p_eff, capacity - 1)
            moe = jnp.zeros((N, d), flat.dtype).at[t_flat].add(exp_out[e_flat, p_g] * gate[:, None])
            return x + moe.reshape(Bb, Tt, d)
        return block_forward(x, ln1_g, ln1_b, Wqkv, Wproj, ln2_g, ln2_b, Wgate, W1, b1, W2, b2)
    x = x + _L0_xattn_ref(_layernorm(x, axis=-1), ctx_1024, ctx_1024, mask_SxS2_bk1, L0_xattn_Wq, L0_xattn_Wk, L0_xattn_Wv, L0_xattn_wq_h, L0_xattn_bq_h, L0_xattn_wk_h, L0_xattn_bk_h, L0_xattn_wv_h, L0_xattn_bv_h, L0_xattn_Wo)
    x = x + _L0_attn_ref(_layernorm(x, axis=-1), L0_attn_Wq, L0_attn_bq, L0_attn_Wk, L0_attn_bk, L0_attn_Wv, L0_attn_bv, L0_attn_Wo, L0_attn_bo, L0_attn_ln_g, L0_attn_ln_b)
    x = x + _L0_ffn_ref(_layernorm(x, axis=-1), L0_ffn_ln1_g, L0_ffn_ln1_b, L0_ffn_Wqkv, L0_ffn_Wproj, L0_ffn_ln2_g, L0_ffn_ln2_b, L0_ffn_Wgate, L0_ffn_W1, L0_ffn_b1, L0_ffn_W2, L0_ffn_b2)
    return x

_drawn_inputs = setup_inputs


def setup_inputs(seed=0):
    import zlib

    import numpy as np

    out = dict(_drawn_inputs(seed))
    spreads = {'L0_attn_bq': (0.0, 0.1),
     'L0_attn_bk': (0.0, 0.1),
     'L0_attn_bv': (0.0, 0.1),
     'L0_attn_bo': (0.0, 0.1),
     'L0_attn_ln_g': (1.0, 0.2),
     'L0_attn_ln_b': (0.0, 0.1),
     'L0_ffn_ln1_g': (1.0, 0.6),
     'L0_ffn_ln1_b': (0.0, 0.8),
     'L0_ffn_ln2_g': (1.0, 0.6),
     'L0_ffn_ln2_b': (0.0, 0.8),
     'L0_ffn_b1': (0.0, 0.8),
     'L0_ffn_b2': (0.0, 0.8)}
    factors = {'L0_ffn_Wqkv': 4.635,
     'L0_ffn_Wproj': 4.778,
     'L0_ffn_Wgate': 6.514,
     'L0_ffn_W1': 8.0,
     'L0_ffn_W2': 8.0}
    for name, (base, spread) in spreads.items():
        noise = np.random.default_rng([zlib.crc32(name.encode()), seed]).standard_normal(out[name].shape)
        drawn = base * np.exp(spread * noise) if base else spread * noise
        out[name] = jnp.asarray(drawn.astype(out[name].dtype))
    for name, factor in factors.items():
        out[name] = (out[name] * factor).astype(out[name].dtype)
    return out
```

```python
from contextlib import ExitStack

import concourse.bass as bass
from concourse import mybir

ALU = mybir.AluOpType
ACT = mybir.ActivationFunctionType
F32 = mybir.dt.float32
BF16 = mybir.dt.bfloat16
U32 = mybir.dt.uint32
U8 = mybir.dt.uint8
X = mybir.AxisListType.X

P = 128
D = 128
B, S = 64, 64
KEYS = 128
H, HD = 16, 8
HH = H // 2
E, CAP = 8, 1024
FF = 512
FC = FF // P
U = 4
GROUPS = B * S // (U * P)
TB = 2
GB = U * TB
EPS = 1e-5
LN_STEPS = 2 * U + 1
SCALE = float(HD) ** -0.5
SLOTS = E * CAP
ZERO_STORES = 4
VW = HD + 1

C_IDENT = 0
C_COS = C_IDENT + P
C_SIN = C_COS + HD // 2
C_NSIN = C_SIN + HD // 2
C_BLOCK = C_NSIN + HD // 2
C_HEAD = C_BLOCK + D
C_RANK = C_HEAD + HH
C_EOFF = C_RANK + E
C_WIDTH = C_EOFF + E
L_IDENT = 0
L_TRI = L_IDENT + P
L_ONES = L_TRI + P
L_CAUSAL = L_ONES + P
L_WIDTH = L_CAUSAL + HH * S


def build_program(nc, t, out):
    xs = nc.dram_tensor("expert_in", [SLOTS, D], F32, kind="Internal").ap()
    ys = nc.dram_tensor("expert_out", [SLOTS, D], F32, kind="Internal").ap()
    x_groups = t["x"].rearrange("(g u w) s d -> g (w s) u d", u=U, w=TB)
    out_groups = out.rearrange("(g u w) s d -> g (w s) u d", u=U, w=TB)
    ctx_groups = t["ctx_1024"].rearrange("(g b) k d -> g k b d", b=GB)
    xs_rows = xs.rearrange("(e p r) d -> e p r d", e=E, p=P)
    ys_rows = ys.rearrange("(e p r) d -> e p r d", e=E, p=P)
    w1_rows = t["w1"]
    w2_rows = t["w2"].rearrange("e (c p) d -> e p c d", p=P)

    with ExitStack() as ctx:
        def sb(name, shape, dt=F32):
            return ctx.enter_context(nc.sbuf_tensor(name, shape, dt))

        names = """const_in weights_in zero_done prep prep_mm prep_cast presets x_in ctx_in group_done
            ln0 z0 z0T_mm ctxT_mm z0T ctxT q0_mm k0_mm v0_mm q0 k0 v0 s0_mm s0_step nmax0 p0 p0T_mm p0T o0_mm o0 y0_mm
            rsum0 x1 ln1 z1 z1T_mm z1T q1_mm q1 kv_mm kv state_mm state_half state o1_mm ln2 n1 n1T_mm n1T y1_mm x1c x2
            ln3 h h_T_mm hT qk_mm qk v_mm vx rope_a rope_b qkr qkT_mm qT kT kx_dve kx_pool
            s_mm smax ssub probs pT_mm pT pv_mm rsum attn attnT_mm attnT proj_mm z2 xp ln4 h2n h2g h2 h2T_mm h2T
            logit_mm route shift expd selected pos_mm slots scattered resid resid_x2
            w_in0 w_in1 rows_in0 rows_in1 tok_mm tok hid_mm hid exp_mm expert_out expert_stored
            root0 root1 root2 root3 root4 idx gathered0 gathered1 gather_free partial result result_stored""".split()
        s = {n: ctx.enter_context(nc.semaphore(n)) for n in names}

        cf = sb("const_f32", [P, C_WIDTH])
        cl = sb("const_bf16", [P, L_WIDTH], BF16)
        cl_f32 = sb("const_low_f32", [P, L_WIDTH])
        ident = cf[:, C_IDENT:C_IDENT + P]
        cos = cf[:, C_COS:C_COS + 4]
        sin = cf[:, C_SIN:C_SIN + 4]
        nsin = cf[:, C_NSIN:C_NSIN + 4]
        block_scale = cf[:, C_BLOCK:C_BLOCK + D]
        head_mask = cf[:, C_HEAD:C_HEAD + HH]
        rank = cf[:, C_RANK:C_RANK + E]
        eoff = cf[:, C_EOFF:C_EOFF + E]
        ident_l = cl[:, L_IDENT:L_IDENT + P]
        tri_l = cl[:, L_TRI:L_TRI + P]
        ones_l = cl[:, L_ONES:L_ONES + P]
        causal_l = cl[:, L_CAUSAL:L_CAUSAL + HH * S]
        xw_T = sb("xw_T", [P, 3, D])
        xw_h = sb("xw_h", [P, 3, HD])
        xw = sb("xw", [P, 3, HD])
        wo_heads = sb("wo_heads", [HD, H, D])
        wo_sum = sb("wo_sum", [HD, D])
        bqk_h = sb("bqk_h", [HD, 2])
        bv_h = sb("bv_h", [P, HD])
        mask_u8 = sb("mask_u8", [P, KEYS], U8)
        keep = sb("keep", [P, KEYS])
        fill = sb("fill", [P, KEYS])
        wq1 = sb("wq1", [P, D])
        bq1 = sb("bq1", [P, 1])
        wkv = sb("wkv", [P, 4 * D])
        bkv = sb("bkv", [P, 4 * D])
        wo1 = sb("wo1", [P, D])
        wo1_g = sb("wo1_g", [P, D])
        bo1 = sb("bo1", [P, D])
        c1 = sb("c1", [P, D])
        cols = sb("cols", [P, 4])
        bcols = sb("bcols", [P, 2, P])
        wqkv = sb("wqkv", [P, 3 * D])
        wqkv_g = sb("wqkv_g", [P, 3 * D])
        bqk = sb("bqk", [P, 2 * D])
        bv = sb("bv", [P, D // 2])
        wproj = sb("wproj", [P, D])
        g2 = sb("g2", [P, D])
        b2ln = sb("b2ln", [P, D])
        wgate = sb("wgate", [P, E])
        b1c = sb("b1c", [P, E * FC])
        b2 = sb("b2", [P, E, D])
        zeros = sb("zeros", [P, 2048])

        x_sb = sb("x_sb", [P, U, D])
        ctx_sb = sb("ctx_sb", [P, GB, D])
        ln_parts = sb("ln_parts", [P, U, 6])
        mv = sb("mv", [P, 5, U, 2])
        var_eps = sb("var_eps", [P, 6, U])
        rstd = sb("rstd", [P, 8, U])
        minus_half = sb("minus_half", [P, U])
        z = sb("z", [P, U, D])
        zT = sb("zT", [P, U * P])
        ctxT = sb("ctxT", [P, GB * KEYS])
        q0T = sb("q0T", [HD, U * P])
        k0T = sb("k0T", [HD, GB * KEYS])
        v0 = sb("v0", [P, GB, HD])
        s0 = sb("s0", [P, U, KEYS])
        smax0 = sb("smax0", [P, U])
        nmax0 = sb("nmax0", [P, U])
        sum0 = sb("sum0", [P, U])
        rsum0 = sb("rsum0", [P, U])
        p0 = sb("p0", [P, U, KEYS])
        p0T = sb("p0T", [P, U * P])
        o0T = sb("o0T", [HD, U * P])
        x1 = sb("x1", [P, U, D])
        x1c = sb("x1c", [P, U, D])
        q1T = sb("q1T", [P, U * P])
        kv = sb("kv", [P, U, 4 * D])
        half_state = sb("half_state", [P, 2, TB, 2, D])
        state = sb("state", [P, 2, TB, 2, D])
        x2 = sb("x2", [P, U, D])
        z2 = sb("z2", [P, U, D])
        hT = sb("hT", [P, U * P])
        qk = sb("qk", [P, U, 2 * D])
        rope_a = sb("rope_a", [P, U, 2 * D])
        rope_b = sb("rope_b", [P, U, 2 * D])
        qkr = sb("qkr", [P, U, 2 * D])
        vx = sb("vx", [P, GB, H // 2, 2, VW])
        qblk = sb("qblk", [P, U, 2, P])
        kT = sb("kT", [P, U, 2, S])
        kx = sb("kx", [P, U, 2, HH, S])
        mxs = sb("mxs", [P, 2, H])
        probs = sb("probs", [P, 2, H * S])
        pT = sb("pT", [P, 2, H // 2, P])
        rsum = sb("rsum", [P, U, H])
        attn = sb("attn", [P, U, D])
        attnT = sb("attnT", [P, U * P])
        xp = sb("xp", [P, U, D])
        h2 = sb("h2", [P, U, D])
        h2T = sb("h2T", [P, U * P])
        lg = sb("lg", [P, 2, U, E])
        first = sb("first", [P, 2, U])
        tie = sb("tie", [P, 2, U, E])
        tie_max = sb("tie_max", [P, 2, U])
        sel = sb("sel", [P, 2, U, E])
        sel_l = sb("sel_l", [P, U, E], BF16)
        shifted = sb("shifted", [P, U, E + 1])
        expd = sb("expd", [P, U, E + 1])
        gate = sb("gate", [P, 2, U])
        esum = sb("esum", [P, U])
        count = sb("count", [P, 2, E])
        pos = sb("pos", [P, 2, U, E])
        kept = sb("kept", [P, U, E])
        picked = sb("picked", [P, 4, U, E])
        slot = sb("slot", [P, 6, 2, U])
        scatter_idx = sb("scatter_idx", [P, 2, U], U32)
        resid = sb("resid", [P, GROUPS, U, D])
        slots_all = sb("slots_all", [P, GROUPS, 2, U], U32)
        gates_all = sb("gates_all", [P, GROUPS, 2, U])
        w1_sb = [sb(f"w1_sb{n}", [P, FF]) for n in range(2)]
        w2_sb = [sb(f"w2_sb{n}", [P, FC, D]) for n in range(2)]
        rows = [b[:, :, :].rearrange("p u (r d) -> p (u r) d", r=2) for b in (rope_a, rope_b)]
        tokT = sb("tokT", [P, 2, 512])
        hid = kx[:, :, :, :, :].rearrange("p (c v) h j k -> p c (v h) (j k)", c=2)
        y_sb = [kv[:, 2 * n:2 * n + 2, :].rearrange("p u (r d) -> p (u r) d", r=4) for n in range(2)]
        gather_idx = [sb(f"gather_idx{n}", [P, 2, U], U32) for n in range(2)]
        gathered = [b[:, :, :].rearrange("p (k v) (r d) -> p k (v r) d", k=2, r=2) for b in (qk, qkr)]

        bank = [ctx.enter_context(nc.psum_tensor(f"bank{n}", [P, 512], F32)) for n in range(8)]

        block = ctx.enter_context(nc.Block())

        def wait_apart(eng, sem, count):
            count = eng.compute_val(count)
            eng.wait_ge(s["weights_in"], 16 * len(LOADS))
            eng.wait_ge(sem, count)

        def over_tiles(ap, width):
            return ap.unsqueeze(1).broadcast_to([P, U, width])

        def per_tile(b):
            return b[:, :].rearrange("p (u n) -> p u n", u=U)

        LOADS = [(cf[:, :], t["const_f32"]), (cl_f32[:, :], t["const_low"]),
                 (xw_T[:, :, :], t["xw_T"]), (xw_h[:, :, :], t["xw_h"]), (wo_heads[:, :, :], t["xwo_heads"]),
                 (bqk_h[:, :], t["xb_qk"]), (bv_h[:, :], t["xb_v"].partition_broadcast(P)),
                 (mask_u8[0:S, :], t["mask"]), (mask_u8[S:P, :], t["mask"]),
                 (wq1[:, :], t["awq"]), (bq1[:, :], t["abq"]), (wkv[:, :], t["awkv"]),
                 (bkv[:, :], t["abkv"].partition_broadcast(P)),
                 (wo1[:, :], t["awo"]), (bo1[:, :], t["abo"].partition_broadcast(P)), (cols[:, :], t["cols"]),
                 (wqkv[:, :], t["wqkv"]), (wproj[:, :], t["wproj"]), (g2[:, :], t["g2"].partition_broadcast(P)),
                 (b2ln[:, :], t["b2ln"].partition_broadcast(P)), (wgate[:, :], t["wgate"]),
                 (b1c[:, :], t["b1c"]), (b2[:, :, :], t["b2"].partition_broadcast(P))]

        @block.sync
        def _(sp):
            for dst, src in LOADS:
                sp.dma_start(dst, src).then_inc(s["weights_in"], 16)
            sp.dma_start(ctx_sb[:, :, :], ctx_groups[0]).then_inc(s["ctx_in"], 16)
            sp.dma_start(x_sb[:, :, :], x_groups[0]).then_inc(s["x_in"], 16)
            with sp.Fori(0, GROUPS - 1) as g:
                sp.wait_ge(s["ctxT_mm"], (g + 1) * 2)
                sp.dma_start(ctx_sb[:, :, :], ctx_groups[bass.ds(g + 1, 1)].rearrange("a k b d -> (a k) b d"))\
                    .then_inc(s["ctx_in"], 16)
                sp.wait_ge(s["x1"], (g + 1) * U)
                sp.dma_start(x_sb[:, :, :], x_groups[bass.ds(g + 1, 1)].rearrange("a k b d -> (a k) b d"))\
                    .then_inc(s["x_in"], 16)

            def load_expert(e, n, wait_rows=False):
                w_in, rows_in = (s["w_in0"], s["w_in1"])[n], (s["rows_in0"], s["rows_in1"])[n]
                sp.dma_start(w1_sb[n][:, :], w1_rows[bass.ds(e, 1)].rearrange("a p f -> (a p) f"))\
                    .then_inc(w_in, 16)
                sp.dma_start(w2_sb[n][:, :, :], w2_rows[bass.ds(e, 1)].rearrange("a p c d -> (a p) c d"))\
                    .then_inc(w_in, 16)
                sp.dma_start(rows[n], xs_rows[bass.ds(e, 1)].rearrange("a p r d -> (a p) r d"))\
                    .then_inc(rows_in, 16)

            def store_expert(e, n):
                sp.wait_ge(s["expert_out"], (e + 1) * 2)
                sp.dma_start(ys_rows[bass.ds(e, 1)].rearrange("a p r d -> (a p) r d"), y_sb[n])\
                    .then_inc(s["expert_stored"], 16)
                sp.wait_ge(s["expert_stored"], (e + 1) * 16)

            sp.wait_ge(s["scattered"], (GROUPS * U * 2 + ZERO_STORES) * 16)
            for n in range(2):
                load_expert(n, n)
            with sp.Fori(0, E // 2 - 1) as i:
                for n in range(2):
                    store_expert(i * 2 + n, n)
                    load_expert(i * 2 + (n + 2), n)
            for n in range(2):
                store_expert(E - 2 + n, n)
            with sp.Fori(0, GROUPS) as g:
                sp.wait_ge(s["result"], (g + 1) * U)
                sp.dma_start(out_groups[bass.ds(g, 1)].rearrange("a p u d -> (a p) u d"),
                             resid[:, bass.ds(g, 1), :, :].rearrange("p a u d -> p (a u) d"))\
                    .then_inc(s["result_stored"], 16)
            sp.wait_ge(s["result_stored"], GROUPS * 16)

        @block.gpsimd
        def _(pool):
            pool.memset(zeros[:, :], 0.0).then_inc(s["zero_done"], 1)
            pool.wait_ge(s["zero_done"], 1)
            for n in range(ZERO_STORES):
                pool.dma_start(xs.rearrange("(n p r) d -> n p (r d)", n=ZERO_STORES, p=P)[n], zeros[:, :])\
                    .then_inc(s["scattered"], 16)
            pool.memset(qblk[:, :, :, :], 0.0).then_inc(s["presets"], 1)
            pool.memset(vx[:, :, :, :, :], 0.0).then_inc(s["presets"], 1)
            pool.memset(count[:, :, :], 0.0).then_inc(s["presets"], 1)
            pool.memset(minus_half[:, :], -0.5).then_inc(s["presets"], 1)
            pool.wait_ge(s["presets"], 4)
            pool.memset(vx[0:S, :, :, 0, HD:VW], 1.0).then_inc(s["presets"], 1)
            pool.memset(vx[S:P, :, :, 1, HD:VW], 1.0).then_inc(s["presets"], 1)
            pool.wait_ge(s["weights_in"], 16 * len(LOADS))
            pool.wait_ge(s["scattered"], ZERO_STORES * 16)

            def inverse_root(g, n, ln, root):
                pool.wait_ge(ln, (g + 1) * LN_STEPS)
                pool.tensor_tensor(rstd[:, n, :], var_eps[:, n, :], minus_half[:, :], ALU.pow).then_inc(root, 1)

            with pool.Fori(0, GROUPS) as g:
                pool.wait_ge(s["group_done"], g + 1)
                inverse_root(g, 0, s["ln0"], s["root0"])
                inverse_root(g, 1, s["ln1"], s["root1"])
                pool.wait_ge(s["x1"], (g + 1) * U)
                pool.tensor_tensor(x1c[:, :, :], x1[:, :, :], over_tiles(c1[:, :], D), ALU.add).then_inc(s["x1c"], 1)
                inverse_root(g, 2, s["ln2"], s["root2"])
                inverse_root(g, 3, s["ln3"], s["root3"])
                pool.wait_ge(s["root3"], g * 6 + 1)
                pool.tensor_tensor(rstd[:, 5, :], mv[:, 3, :, 1], rstd[:, 3, :], ALU.mult).then_inc(s["root3"], 1)
                pool.wait_ge(s["root3"], g * 6 + 2)
                pool.tensor_tensor(rstd[:, 6, :], rstd[:, 5, :], rstd[:, 3, :], ALU.mult).then_inc(s["root3"], 1)
                wait_apart(pool, s["root3"], g * 6 + 3)
                pool.tensor_scalar(var_eps[:, 5, :], rstd[:, 6, :], EPS, None, ALU.add).then_inc(s["root3"], 1)
                pool.wait_ge(s["root3"], g * 6 + 4)
                pool.tensor_tensor(rstd[:, 5, :], var_eps[:, 5, :], minus_half[:, :], ALU.pow).then_inc(s["root3"], 1)
                pool.wait_ge(s["root3"], g * 6 + 5)
                pool.tensor_tensor(rstd[:, 7, :], rstd[:, 5, :], rstd[:, 3, :], ALU.mult).then_inc(s["root3"], 1)
                for u in range(U):
                    pool.tensor_scalar(z2[:, u, :], x2[:, u, :], mv[:, 3, u, 0:1], rstd[:, 3, u:u + 1],
                                       ALU.subtract, ALU.mult).then_inc(s["z2"], 1)
                pool.wait_ge(s["qk"], (g + 1) * 2)
                halves = qk[:, :, :].rearrange("p u (c k f) -> p (u c) k f", k=2, f=4)
                crossed = rope_b[:, :, :].rearrange("p u (c k f) -> p (u c) k f", k=2, f=4)
                for k, table in ((0, nsin), (1, sin)):
                    pool.tensor_tensor(crossed[:, :, k, :], halves[:, :, 1 - k, :],
                                       table.unsqueeze(1).broadcast_to([P, U * 2 * H, 4]), ALU.mult)\
                        .then_inc(s["rope_b"], 1)
                wait_apart(pool, s["kT"], (g + 1) * 2)
                for j in range(HH // 2, HH):
                    pool.tensor_scalar(kx[:, :, :, j, :], kT[:, :, :, :], head_mask[:, j:j + 1], None, ALU.mult)\
                        .then_inc(s["kx_pool"], 1)
                pool.wait_ge(s["xp"], g + 1)
                pool.tensor_tensor(resid[:, bass.ds(g, 1), :, :].rearrange("p a u d -> p (a u) d"),
                                   x2[:, :, :], xp[:, :, :], ALU.add).then_inc(s["resid"], 1)
                inverse_root(g, 4, s["ln4"], s["root4"])
                pool.wait_ge(s["h2n"], (g + 1) * U)
                pool.tensor_tensor(h2[:, :, :], h2[:, :, :], over_tiles(g2[:, :], D), ALU.mult).then_inc(s["h2g"], 1)
                pool.wait_ge(s["h2g"], g + 1)
                pool.tensor_tensor(h2[:, :, :], h2[:, :, :], over_tiles(b2ln[:, :], D), ALU.add).then_inc(s["h2"], 1)
                wait_apart(pool, s["slots"], g + 1)
                pool.wait_ge(s["h2"], g + 1)
                for u in range(U):
                    for k in range(2):
                        pool.indirect_dma_start(
                            xs, bass.IndirectOffsetOnAxis(scatter_idx[:, k, u:u + 1], 0), h2[:, u, :], None,
                            bounds_check=SLOTS - 1, oob_is_err=False).then_inc(s["scattered"], 16)

            pool.wait_ge(s["expert_stored"], E * 16)
            with pool.Fori(0, GROUPS // 2) as i:
                for n in range(2):
                    pool.wait_ge(s["gather_free"], i * 2 + (n + 1))
                    pool.tensor_copy(gather_idx[n][:, :, :],
                                     slots_all[:, bass.ds(i * 2 + n, 1), :, :].rearrange("p a k u -> p (a k) u"))\
                        .then_inc(s["idx"], 1)
                    wait_apart(pool, s["idx"], i * 2 + (n + 1))
                    for k in range(2):
                        for u in range(U):
                            pool.indirect_dma_start(
                                gathered[n][:, k, u, :], None, ys,
                                bass.IndirectOffsetOnAxis(gather_idx[n][:, k, u:u + 1], 0))\
                                .then_inc((s["gathered0"], s["gathered1"])[n], 16)

        @block.scalar
        def _(act):
            act.wait_ge(s["weights_in"], 16 * len(LOADS))
            act.wait_ge(s["presets"], 6)
            with act.Fori(0, GROUPS) as g:
                act.wait_ge(s["group_done"], g + 1)
                for n in range(2):
                    act.wait_ge(s["ctxT_mm"], g * 2 + n + 1)
                    act.activation(ctxT[:, n * 512:(n + 1) * 512], bank[1 + n][:, :], ACT.Copy).then_inc(s["ctxT"], 1)
                for n in range(2):
                    act.wait_ge(s["k0_mm"], g * 2 + n + 1)
                    act.activation(k0T[:, n * 512:(n + 1) * 512], bank[4 + n][0:HD, :], ACT.Identity,
                                   bias=bqk_h[:, 1:2]).then_inc(s["k0"], 1)
                act.wait_ge(s["q0_mm"], g + 1)
                act.activation(q0T[:, :], bank[3][0:HD, :], ACT.Identity, bias=bqk_h[:, 0:1]).then_inc(s["q0"], 1)
                act.wait_ge(s["nmax0"], g + 1)
                for u in range(U):
                    act.activation(p0[:, u, :], s0[:, u, :], ACT.Exp, bias=nmax0[:, u:u + 1], scale=SCALE,
                                   accum_out=sum0[:, u:u + 1]).then_inc(s["p0"], 1)
                act.wait_ge(s["o0_mm"], g + 1)
                act.activation(o0T[:, :], bank[1][0:HD, :], ACT.Copy).then_inc(s["o0"], 1)
                act.wait_ge(s["z1T_mm"], g + 1)
                act.activation(zT[:, :], bank[3][:, :], ACT.Copy).then_inc(s["z1T"], 1)
                act.wait_ge(s["q1_mm"], g + 1)
                act.activation(q1T[:, :], bank[4][:, :], ACT.Identity, bias=bq1[:, 0:1]).then_inc(s["q1"], 1)
                act.wait_ge(s["n1T_mm"], g + 1)
                act.activation(zT[:, :], bank[6][:, :], ACT.Copy).then_inc(s["n1T"], 1)
                act.wait_ge(s["h_T_mm"], g + 1)
                act.activation(hT[:, :], bank[1][:, :], ACT.Copy).then_inc(s["hT"], 1)
                act.wait_ge(s["qkT_mm"], (g + 1) * U)
                for n in range(2):
                    for u in range(U):
                        src = bank[(5, 6, 7, 0)[u]][0:HH * HD, :].rearrange("p (c h b t) -> p c h b t",
                                                                            c=2, h=2, b=TB)
                        act.activation(kT[n * 64:(n + 1) * 64, u, :, :], src[:, 1, :, n, :], ACT.Copy)\
                            .then_inc(s["kT"] if u == U - 1 else s["shift"], 1)
                for n in range(2):
                    for u in range(U):
                        src = bank[(5, 6, 7, 0)[u]][0:HH * HD, :].rearrange("p (c h b t) -> p c h b t",
                                                                            c=2, h=2, b=TB)
                        act.activation(qblk[n * 64:(n + 1) * 64, u, :, n * S:(n + 1) * S], src[:, 0, :, n, :],
                                       ACT.Copy).then_inc(s["qT"], 1)
                for u in range(U):
                    act.wait_ge(s["ssub"], g * U + u + 1)
                    act.activation(probs[:, u % 2, :], probs[:, u % 2, :], ACT.Exp, scale=SCALE)\
                        .then_inc(s["probs"], 1)
                    for n in range(2):
                        act.wait_ge(s["pT_mm"], (g * U + u) * 2 + n + 1)
                        act.activation(pT[:, u % 2, 4 * n:4 * n + 4, :],
                                       bank[5 + n][:, :].rearrange("p (j t) -> p j t", j=4), ACT.Copy)\
                            .then_inc(s["pT"], 1)
                act.wait_ge(s["attnT_mm"], g + 1)
                act.activation(attnT[:, :], bank[5][:, :], ACT.Copy).then_inc(s["attnT"], 1)
                act.wait_ge(s["h2T_mm"], g + 1)
                act.activation(h2T[:, :], bank[7][:, :], ACT.Copy).then_inc(s["h2T"], 1)
                act.wait_ge(s["expd"], g * 2 + 1)
                act.activation(expd[:, :, :], shifted[:, :, :], ACT.Exp).then_inc(s["expd"], 1)
            with act.Fori(0, E) as e:
                for c in range(2):
                    for f in range(FC):
                        wait_apart(act, s["hid_mm"], e * (2 * FC) + c * FC + f + 1)
                        act.activation(hid[:, c, f, :], bank[2 + f][:, :], ACT.Gelu,
                                       bias=b1c[:, bass.ds(e * FC + f, 1)]).then_inc(s["hid"], 1)

        @block.vector
        def _(dve):
            dve.wait_ge(s["weights_in"], 16 * len(LOADS))
            dve.tensor_reduce(wo_sum[:, :], wo_heads[:, :, :].rearrange("p h d -> p d h"), X, ALU.add)\
                .then_inc(s["prep"], 1)
            dve.tensor_copy(cl[:, :], cl_f32[:, :]).then_inc(s["prep_cast"], 1)
            dve.tensor_copy(fill[:, :], mask_u8[:, :]).then_inc(s["prep_cast"], 1)
            dve.wait_ge(s["prep_cast"], 2)
            dve.tensor_scalar(keep[:, :], fill[:, :], -1.0, 1.0, ALU.mult, ALU.add).then_inc(s["prep_cast"], 1)
            dve.wait_ge(s["prep_cast"], 3)
            dve.tensor_scalar(fill[:, :], fill[:, :], -1e9 / SCALE, None, ALU.mult).then_inc(s["prep"], 1)
            dve.tensor_tensor(wq1[:, :], wq1[:, :], ident, ALU.add).then_inc(s["prep"], 1)
            for k in range(4):
                dve.tensor_tensor(wkv[:, k * D:(k + 1) * D], wkv[:, k * D:(k + 1) * D], ident, ALU.add)\
                    .then_inc(s["prep_cast"], 1)
            dve.tensor_scalar(wo1_g[:, :], wo1[:, :], cols[:, 0:1], None, ALU.mult).then_inc(s["prep"], 1)
            dve.tensor_scalar(wqkv_g[:, :], wqkv[:, :], cols[:, 2:3], None, ALU.mult).then_inc(s["prep"], 1)
            for n in range(2):
                dve.tensor_scalar(bcols[:, n, :], ident, 0.0, cols[:, 2 * n + 1:2 * n + 2], ALU.mult, ALU.add)\
                    .then_inc(s["prep_cast"], 1)
            dve.wait_ge(s["prep_mm"], 1)
            dve.tensor_copy(xw[:, :, :], bank[0][:, 0:3 * HD].rearrange("p (c d) -> p c d", c=3))\
                .then_inc(s["prep"], 1)
            dve.tensor_copy(bqk[:, :], bank[1][:, 0:2 * D]).then_inc(s["prep"], 1)
            dve.tensor_copy(bv[0:S, :], bank[1][0:S, 2 * D:2 * D + D // 2]).then_inc(s["prep_cast"], 1)
            dve.tensor_copy(bv[S:P, :], bank[1][S:P, 2 * D + D // 2:3 * D]).then_inc(s["prep"], 1)
            dve.wait_ge(s["prep_cast"], 10)
            dve.tensor_tensor(c1[:, :], bank[2][:, 0:D], bo1[:, :], ALU.add).then_inc(s["prep"], 1)
            dve.wait_ge(s["prep"], 9)
            dve.memset(smax0[:, :], 0.0).then_inc(s["group_done"], 1)
            dve.memset(nmax0[:, :], 0.0).then_inc(s["gather_free"], 2)
            dve.wait_ge(s["presets"], 6)

            def stats(g, n, sem, src):
                for u in range(U):
                    dve.bn_stats(ln_parts[:, u, :], src(u)).then_inc(sem, 1)
                wait_apart(dve, sem, g * LN_STEPS + U)
                for u in range(U):
                    dve.bn_aggr(mv[:, n, u, :], ln_parts[:, u, :]).then_inc(sem, 1)
                dve.wait_ge(sem, g * LN_STEPS + 2 * U)
                dve.tensor_scalar(var_eps[:, n, :], mv[:, n, :, 1], EPS, None, ALU.add).then_inc(sem, 1)

            def normalise(dst, n, k, src, sem):
                for u in range(U):
                    dve.tensor_scalar(dst[:, u, :], src(u), mv[:, n, u, 0:1], rstd[:, k, u:u + 1],
                                      ALU.subtract, ALU.mult).then_inc(sem, 1)

            with dve.Fori(0, GROUPS) as g:
                dve.wait_ge(s["group_done"], g + 1)
                dve.wait_ge(s["x_in"], (g + 1) * 16)
                stats(g, 0, s["ln0"], lambda u: x_sb[:, u, :])
                dve.wait_ge(s["root0"], g + 1)
                normalise(z, 0, 0, lambda u: x_sb[:, u, :], s["z0"])
                dve.wait_ge(s["z0T_mm"], g + 1)
                dve.tensor_copy(zT[:, :], bank[0][:, :]).then_inc(s["z0T"], 1)
                dve.wait_ge(s["v0_mm"], g + 1)
                dve.tensor_tensor(v0[:, :, :], bank[6][:, 0:GB * HD].rearrange("p (b d) -> p b d", b=GB),
                                  bv_h[:, :].unsqueeze(1).broadcast_to([P, GB, HD]), ALU.add).then_inc(s["v0"], 1)
                dve.wait_ge(s["s0_mm"], g + 1)
                dve.tensor_tensor(s0[:, :, :], per_tile(bank[7]), over_tiles(keep[:, :], KEYS), ALU.mult)\
                    .then_inc(s["s0_step"], 1)
                dve.wait_ge(s["s0_step"], g * 3 + 1)
                dve.tensor_tensor(s0[:, :, :], s0[:, :, :], over_tiles(fill[:, :], KEYS), ALU.add)\
                    .then_inc(s["s0_step"], 1)
                dve.wait_ge(s["s0_step"], g * 3 + 2)
                dve.tensor_reduce(smax0[:, :], s0[:, :, :], X, ALU.max).then_inc(s["s0_step"], 1)
                dve.wait_ge(s["s0_step"], g * 3 + 3)
                dve.tensor_scalar(nmax0[:, :], smax0[:, :], -SCALE, None, ALU.mult).then_inc(s["nmax0"], 1)
                dve.wait_ge(s["p0T_mm"], g + 1)
                dve.tensor_copy(p0T[:, :], bank[0][:, :]).then_inc(s["p0T"], 1)
                dve.wait_ge(s["p0"], (g + 1) * U)
                dve.reciprocal(rsum0[:, :], sum0[:, :]).then_inc(s["rsum0"], 1)
                dve.wait_ge(s["rsum0"], g + 1)
                dve.wait_ge(s["y0_mm"], g + 1)
                for u in range(U):
                    dve.scalar_tensor_tensor(out=x1[:, u, :], in0=bank[2][:, u * D:(u + 1) * D],
                                             scalar=rsum0[:, u:u + 1], in1=x_sb[:, u, :], op0=ALU.mult,
                                             op1=ALU.add).then_inc(s["x1"], 1)
                dve.wait_ge(s["x1"], (g + 1) * U)
                stats(g, 1, s["ln1"], lambda u: x1[:, u, :])
                dve.wait_ge(s["root1"], g + 1)
                normalise(z, 1, 1, lambda u: x1[:, u, :], s["z1"])
                for u in range(U):
                    dve.wait_ge(s["kv_mm"], g * U + u + 1)
                    dve.tensor_tensor(kv[:, u, :], bank[(5, 6, 0, 1)[u]][:, :], bkv[:, :], ALU.add)\
                        .then_inc(s["kv"], 1)
                for pair in range(2):
                    dve.wait_ge(s["state_mm"], g * 2 + pair + 1)
                    for b in range(TB):
                        st = bank[((7, 2), (3, 4))[pair][b]][:, :].rearrange("p (u k e) -> p u k e", u=2, k=2)
                        dve.tensor_tensor(half_state[:, pair, b, :, :], st[:, :, 0, :],
                                          block_scale.unsqueeze(1).broadcast_to([P, 2, D]), ALU.mult)\
                            .then_inc(s["state_half"], 1)
                    for b in range(TB):
                        dve.wait_ge(s["state_half"], (g * 2 + pair) * TB + b + 1)
                        st = bank[((7, 2), (3, 4))[pair][b]][:, :].rearrange("p (u k e) -> p u k e", u=2, k=2)
                        dve.tensor_tensor(state[:, pair, b, :, :], half_state[:, pair, b, :, :], st[:, :, 1, :],
                                          ALU.mult).then_inc(s["state"], 1)
                dve.wait_ge(s["o1_mm"], g + 1)
                stats(g, 2, s["ln2"], lambda u: bank[5][:, u * D:(u + 1) * D])
                dve.wait_ge(s["root2"], g + 1)
                normalise(z, 2, 2, lambda u: bank[5][:, u * D:(u + 1) * D], s["n1"])
                dve.wait_ge(s["y1_mm"], g + 1)
                dve.wait_ge(s["x1c"], g + 1)
                dve.tensor_tensor(x2[:, :, :], per_tile(bank[0]), x1c[:, :, :], ALU.add).then_inc(s["x2"], 1)
                dve.wait_ge(s["x2"], g + 1)
                stats(g, 3, s["ln3"], lambda u: x2[:, u, :])
                dve.wait_ge(s["root3"], (g + 1) * 6)
                normalise(z, 3, 7, lambda u: x2[:, u, :], s["h"])
                for n in range(2):
                    dve.wait_ge(s["qk_mm"], g * 2 + n + 1)
                    dve.tensor_tensor(qk[:, 2 * n:2 * n + 2, :], bank[2 + n][:, :].rearrange("p (u c) -> p u c", u=2),
                                      bqk[:, :].unsqueeze(1).broadcast_to([P, 2, 2 * D]), ALU.add).then_inc(s["qk"], 1)
                dve.wait_ge(s["v_mm"], g + 1)
                for n in range(2):
                    at = slice(n * S, (n + 1) * S)
                    dve.tensor_tensor(vx[at, :, :, n, 0:HD],
                                      bank[4][at, :].rearrange("p (b j d) -> p b j d", b=GB, d=HD),
                                      bv[at, :].rearrange("p (j d) -> p j d", d=HD).unsqueeze(1)
                                      .broadcast_to([S, GB, H // 2, HD]), ALU.add).then_inc(s["vx"], 1)
                dve.wait_ge(s["qk"], (g + 1) * 2)
                dve.tensor_tensor(rope_a[:, :, :].rearrange("p u (c f) -> p (u c) f", f=4),
                                  qk[:, :, :].rearrange("p u (c f) -> p (u c) f", f=4),
                                  cos.unsqueeze(1).broadcast_to([P, U * 4 * H, 4]), ALU.mult).then_inc(s["rope_a"], 1)
                dve.wait_ge(s["rope_a"], g + 1)
                dve.wait_ge(s["rope_b"], (g + 1) * 2)
                dve.tensor_tensor(qkr[:, :, :], rope_a[:, :, :], rope_b[:, :, :], ALU.add).then_inc(s["qkr"], 1)
                dve.wait_ge(s["kT"], (g + 1) * 2)
                for j in range(HH // 2):
                    dve.tensor_scalar(kx[:, :, :, j, :], kT[:, :, :, :], head_mask[:, j:j + 1], None, ALU.mult)\
                        .then_inc(s["kx_dve"], 1)

                def shift_scores(u):
                    dve.wait_ge(s["s_mm"], g * U + u + 1)
                    for n in range(2):
                        dve.tensor_reduce(mxs[:, u % 2, n * HH:(n + 1) * HH],
                                          bank[1 + 2 * (u % 2) + n][:, :].rearrange("p (h k) -> p h k", h=HH),
                                          X, ALU.max).then_inc(s["smax"], 1)
                    dve.wait_ge(s["smax"], (g * U + u + 1) * 2)
                    if u >= 2:
                        dve.wait_ge(s["pT_mm"], (g * U + u - 1) * 2)
                    for n in range(2):
                        ins = dve.tensor_tensor(
                            probs[:, u % 2, n * 512:(n + 1) * 512].rearrange("p (h k) -> p h k", h=HH),
                            bank[1 + 2 * (u % 2) + n][:, :].rearrange("p (h k) -> p h k", h=HH),
                            mxs[:, u % 2, n * HH:(n + 1) * HH].unsqueeze(2).broadcast_to([P, HH, S]), ALU.subtract)
                    ins.then_inc(s["ssub"], 1)

                def attention(u):
                    dve.wait_ge(s["pv_mm"], g * U + u + 1)
                    pv = bank[(7, 0)[u % 2]][:, 0:H // 2 * TB * 2 * VW].rearrange("p (j b h c) -> p j b h c",
                                                                                 b=TB, h=2, c=VW)
                    for b in range(TB):
                        at = slice(b * S, (b + 1) * S)
                        dve.reciprocal(rsum[at, u, :].rearrange("p (j h) -> p j h", h=2), pv[at, :, b, :, HD])\
                            .then_inc(s["rsum"], 1)
                    for b in range(TB):
                        at = slice(b * S, (b + 1) * S)
                        dve.wait_ge(s["rsum"], (g * U + u) * TB + b + 1)
                        dve.tensor_tensor(
                            attn[at, u, :].rearrange("p (j h c) -> p j h c", h=2, c=HD), pv[at, :, b, :, 0:HD],
                            rsum[at, u, :].rearrange("p (j h) -> p j h", h=2).unsqueeze(3)
                            .broadcast_to([S, H // 2, 2, HD]), ALU.mult).then_inc(s["attn"], 1)

                shift_scores(0)
                shift_scores(1)
                for u in range(2, U):
                    shift_scores(u)
                    attention(u - 2)
                attention(U - 2)
                attention(U - 1)
                dve.wait_ge(s["proj_mm"], g + 1)
                dve.wait_ge(s["z2"], (g + 1) * U)
                dve.tensor_tensor(xp[:, :, :], per_tile(bank[6]), z2[:, :, :], ALU.add).then_inc(s["xp"], 1)
                dve.wait_ge(s["xp"], g + 1)
                stats(g, 4, s["ln4"], lambda u: xp[:, u, :])
                dve.wait_ge(s["scattered"], g * (U * 2 * 16) + ZERO_STORES * 16)
                dve.wait_ge(s["root4"], g + 1)
                normalise(h2, 4, 4, lambda u: xp[:, u, :], s["h2n"])
                route_steps = 25
                step = [0]

                def link(ins):
                    step[0] += 1
                    ins.then_inc(s["route"], 1)
                    dve.wait_ge(s["route"], g * route_steps + step[0])

                def over_experts(ap):
                    return ap.unsqueeze(2).broadcast_to([P, U, E])

                dve.wait_ge(s["logit_mm"], g + 1)
                link(dve.tensor_copy(lg[:, 0, :, :], bank[0][:, 0:U * E].rearrange("p (u e) -> p u e", u=U)))
                for k in range(2):
                    link(dve.tensor_reduce(first[:, k, :], lg[:, k, :, :], X, ALU.max))
                    link(dve.tensor_tensor(tie[:, k, :, :], lg[:, k, :, :], over_experts(first[:, k, :]),
                                           ALU.is_equal))
                    link(dve.tensor_tensor(tie[:, k, :, :], tie[:, k, :, :], over_tiles(rank, E), ALU.mult))
                    link(dve.tensor_reduce(tie_max[:, k, :], tie[:, k, :, :], X, ALU.max))
                    link(dve.tensor_tensor(sel[:, k, :, :], over_tiles(rank, E), over_experts(tie_max[:, k, :]),
                                           ALU.is_equal))
                    if k == 0:
                        link(dve.scalar_tensor_tensor(out=lg[:, 1, :, :], in0=sel[:, 0, :, :], scalar=-3e38,
                                                      in1=lg[:, 0, :, :], op0=ALU.mult, op1=ALU.add))
                dve.tensor_tensor(sel_l[:, :, :], sel[:, 0, :, :], sel[:, 1, :, :], ALU.add).then_inc(s["selected"], 1)
                dve.tensor_tensor(shifted[:, :, 0:E], lg[:, 0, :, :], over_experts(first[:, 0, :]), ALU.subtract)
                dve.tensor_tensor(shifted[:, :, E], first[:, 1, :], first[:, 0, :], ALU.subtract)\
                    .then_inc(s["expd"], 1)
                dve.wait_ge(s["pos_mm"], g + 1)
                link(dve.tensor_tensor(pos[:, 0, :, :], bank[1][:, 0:U * E].rearrange("p (u e) -> p u e", u=U),
                                       over_tiles(count[:, 0, :], E), ALU.add))
                link(dve.tensor_tensor(count[:, 1, :], count[:, 0, :], bank[2][:, 0:E], ALU.add))
                link(dve.tensor_copy(count[:, 0, :], count[:, 1, :]))
                link(dve.tensor_scalar(kept[:, :, :], pos[:, 0, :, :], float(CAP), None, ALU.is_le))
                link(dve.tensor_tensor(pos[:, 1, :, :], pos[:, 0, :, :], over_tiles(eoff, E), ALU.add))
                for k in range(2):
                    dve.tensor_tensor(picked[:, k, :, :], sel[:, k, :, :], pos[:, 1, :, :], ALU.mult)
                    last = dve.tensor_tensor(picked[:, 2 + k, :, :], sel[:, k, :, :], kept[:, :, :], ALU.mult)
                link(last)
                link(dve.tensor_reduce(slot[:, 0:2, :, :], picked[:, :, :, :], X, ALU.add))
                link(dve.tensor_tensor(slot[:, 2, :, :], slot[:, 0, :, :], slot[:, 1, :, :], ALU.mult))
                link(dve.tensor_scalar(slot[:, 3, :, :], slot[:, 1, :, :], -float(4 * SLOTS), float(4 * SLOTS),
                                       ALU.mult, ALU.add))
                link(dve.tensor_tensor(slot[:, 4, :, :], slot[:, 2, :, :], slot[:, 3, :, :], ALU.add))
                dve.tensor_copy(scatter_idx[:, :, :], slot[:, 4, :, :]).then_inc(s["slots"], 1)
                dve.tensor_copy(slots_all[:, bass.ds(g, 1), :, :].rearrange("p a k u -> p (a k) u"),
                                slot[:, 2, :, :])
                dve.wait_ge(s["expd"], (g + 1) * 2)
                link(dve.tensor_reduce(esum[:, :], expd[:, :, 0:E], X, ALU.add))
                link(dve.reciprocal(gate[:, 0, :], esum[:, :]))
                link(dve.tensor_tensor(gate[:, 1, :], gate[:, 0, :], expd[:, :, E], ALU.mult))
                dve.wait_ge(s["resid"], g + 1)
                dve.tensor_tensor(gates_all[:, bass.ds(g, 1), :, :].rearrange("p a k u -> p (a k) u"),
                                  gate[:, :, :], slot[:, 1, :, :], ALU.mult).then_inc(s["group_done"], 1)
                assert step[0] == route_steps, step

            with dve.Fori(0, E // 2) as i:
                for n in range(2):
                    for c in range(2):
                        dve.wait_ge(s["tok_mm"], i * 4 + (2 * n + c + 1))
                        dve.tensor_copy(tokT[:, c, :], bank[c][:, :]).then_inc(s["tok"], 1)
                    for c in range(2):
                        dve.wait_ge(s["exp_mm"], i * 4 + (2 * n + c + 1))
                        dve.tensor_tensor(y_sb[n][:, 4 * c:4 * c + 4, :], per_tile(bank[6 + c]),
                                          b2[:, bass.ds(i * 2 + n, 1), :].broadcast_to([P, 4, D]), ALU.add)\
                            .then_inc(s["expert_out"], 1)
            with dve.Fori(0, GROUPS // 2) as i:
                for n in range(2):
                    dve.wait_ge((s["gathered0"], s["gathered1"])[n], (i + 1) * (U * 2 * 16))
                    for k in range(2):
                        for u in range(U):
                            acc = resid[:, bass.ds(i * 2 + n, 1), u, :].rearrange("p a d -> p (a d)")
                            if k == 1:
                                dve.wait_ge(s["partial"], i * (2 * U) + (n * U + u + 1))
                            ins = dve.scalar_tensor_tensor(
                                out=acc, in0=gathered[n][:, k, u, :],
                                scalar=gates_all[:, bass.ds(i * 2 + n, 1), k, u:u + 1].rearrange("p a u -> p (a u)"),
                                in1=acc, op0=ALU.mult, op1=ALU.add)
                            ins.then_inc(s["partial"] if k == 0 else s["result"], 1)
                    dve.wait_ge(s["result"], i * (2 * U) + (n + 1) * U)
                    dve.memset(smax0[:, :], 0.0).then_inc(s["gather_free"], 1)

        @block.tensor
        def _(pe):
            pe.wait_ge(s["weights_in"], 16 * len(LOADS))
            for k in range(3):
                pe.matmul(bank[0][:, k * HD:(k + 1) * HD], xw_T[:, k, :], xw_h[:, k, :], start=True, stop=True)
            pe.wait_ge(s["prep_cast"], 9)
            pe.matmul(bank[1][:, 0:3 * D], bcols[:, 1, :], wqkv[:, :], start=True, stop=True)
            pe.matmul(bank[2][:, 0:D], bcols[:, 0, :], wo1[:, :], start=True, stop=True).then_inc(s["prep_mm"], 1)
            pe.wait_ge(s["presets"], 6)

            def transposes(dst, src, sem, ready, counts):
                for u in range(U):
                    pe.wait_ge(ready, counts + u + 1)
                    mm = pe.transpose(dst[:, u * P:(u + 1) * P], src[:, u, :], ident)
                mm.then_inc(sem, 1)

            with pe.Fori(0, GROUPS) as g:
                pe.wait_ge(s["group_done"], g + 1)
                pe.wait_ge(s["ctx_in"], (g + 1) * 16)
                for b in range(GB):
                    mm = pe.transpose(bank[1 + b // 4][:, b % 4 * KEYS:(b % 4 + 1) * KEYS], ctx_sb[:, b, :], ident)
                    if b % 4 == 3:
                        mm.then_inc(s["ctxT_mm"], 1)
                transposes(bank[0], z, s["z0T_mm"], s["z0"], g * U)
                for n in range(2):
                    pe.wait_ge(s["ctxT"], g * 2 + n + 1)
                    pe.matmul(bank[4 + n][0:HD, :], xw[:, 1, :], ctxT[:, n * 512:(n + 1) * 512], start=True,
                              stop=True).then_inc(s["k0_mm"], 1)
                for b in range(GB):
                    mm = pe.matmul(bank[6][:, b * HD:(b + 1) * HD], ctxT[:, b * KEYS:(b + 1) * KEYS], xw[:, 2, :],
                                   start=True, stop=True)
                mm.then_inc(s["v0_mm"], 1)
                pe.wait_ge(s["z0T"], g + 1)
                pe.matmul(bank[3][0:HD, :], xw[:, 0, :], zT[:, :], start=True, stop=True).then_inc(s["q0_mm"], 1)
                pe.wait_ge(s["q0"], g + 1)
                pe.wait_ge(s["k0"], (g + 1) * 2)
                for b in range(GB):
                    u, w = b // TB, b % TB
                    mm = pe.matmul(bank[7][w * S:(w + 1) * S, u * KEYS:(u + 1) * KEYS], q0T[:, b * S:(b + 1) * S],
                                   k0T[:, b * KEYS:(b + 1) * KEYS], start=True, stop=True)
                mm.then_inc(s["s0_mm"], 1)
                transposes(bank[0], p0, s["p0T_mm"], s["p0"], g * U)
                pe.wait_ge(s["p0T"], g + 1)
                pe.wait_ge(s["v0"], g + 1)
                for b in range(GB):
                    mm = pe.matmul(bank[1][0:HD, b * S:(b + 1) * S], v0[:, b, :], p0T[:, b * S:(b + 1) * S],
                                   start=True, stop=True)
                mm.then_inc(s["o0_mm"], 1)
                pe.wait_ge(s["o0"], g + 1)
                for u in range(U):
                    mm = pe.matmul(bank[2][:, u * D:(u + 1) * D], o0T[:, u * P:(u + 1) * P], wo_sum[:, :],
                                   start=True, stop=True)
                mm.then_inc(s["y0_mm"], 1)
                transposes(bank[3], z, s["z1T_mm"], s["z1"], g * U)
                pe.wait_ge(s["z1T"], g + 1)
                for u in range(U):
                    pe.matmul(bank[(5, 6, 0, 1)[u]][:, :], zT[:, u * P:(u + 1) * P], wkv[:, :], start=True,
                              stop=True).then_inc(s["kv_mm"], 1)
                pe.matmul(bank[4][:, :], wq1[:, :], zT[:, :], start=True, stop=True).then_inc(s["q1_mm"], 1)
                for pair in range(2):
                    if pair == 1:
                        pe.wait_ge(s["q1"], g + 1)
                    for v in range(2):
                        u = 2 * pair + v
                        pe.wait_ge(s["kv"], g * U + u + 1)
                        for k in range(2):
                            for b in range(TB):
                                at = slice(b * S, (b + 1) * S)
                                o = (2 * v + k) * D
                                mm = pe.matmul(bank[((7, 2), (3, 4))[pair][b]][:, o:o + D],
                                               kv[at, u, 2 * k * D:(2 * k + 1) * D],
                                               kv[at, u, (2 * k + 1) * D:(2 * k + 2) * D], start=True, stop=True)
                    mm.then_inc(s["state_mm"], 1)
                for u in range(U):
                    for b in range(TB):
                        pe.wait_ge(s["state"], (g * 2 + u // 2) * TB + b + 1)
                        mm = pe.matmul(bank[5][b * S:(b + 1) * S, u * D:(u + 1) * D],
                                       q1T[:, u * P + b * S:u * P + (b + 1) * S], state[:, u // 2, b, u % 2, :],
                                       start=True, stop=True)
                mm.then_inc(s["o1_mm"], 1)
                transposes(bank[6], z, s["n1T_mm"], s["n1"], g * U)
                pe.wait_ge(s["n1T"], g + 1)
                for u in range(U):
                    mm = pe.matmul(bank[0][:, u * D:(u + 1) * D], zT[:, u * P:(u + 1) * P], wo1_g[:, :],
                                   start=True, stop=True)
                mm.then_inc(s["y1_mm"], 1)
                transposes(bank[1], z, s["h_T_mm"], s["h"], g * U)
                pe.wait_ge(s["hT"], g + 1)
                for u in range(U):
                    mm = pe.matmul(bank[2 + u // 2][:, u % 2 * 2 * D:(u % 2 + 1) * 2 * D], hT[:, u * P:(u + 1) * P],
                                   wqkv_g[:, 0:2 * D], start=True, stop=True)
                    if u % 2:
                        mm.then_inc(s["qk_mm"], 1)
                for b in range(GB):
                    for n in range(2):
                        mm = pe.matmul(bank[4][n * S:(n + 1) * S, b * 64:(b + 1) * 64], hT[:, b * S:(b + 1) * S],
                                       wqkv_g[:, 2 * D + n * 64:2 * D + (n + 1) * 64], start=True, stop=True)
                mm.then_inc(s["v_mm"], 1)
                wait_apart(pe, s["qkr"], g + 1)
                for u in range(U):
                    for c in range(2):
                        for n in range(2):
                            o = (c * 2 + n) * P
                            mm = pe.transpose(bank[(5, 6, 7, 0)[u]][0:64, o:o + P],
                                              qkr[:, u, c * D + n * 64:c * D + (n + 1) * 64], ident)
                    mm.then_inc(s["qkT_mm"], 1)

                def scores(u):
                    if u >= 2:
                        pe.wait_ge(s["ssub"], g * U + u - 1)
                    for n in range(2):
                        b = bank[1 + 2 * (u % 2) + n]
                        pe.matmul(b[:, :], qblk[:, u, n, :],
                                  kx[:, u, n, :, :].rearrange("p h k -> p (h k)"), start=True, stop=False)
                        mm = pe.matmul(b[:, :], ident_l, causal_l, start=False, stop=True)
                    mm.then_inc(s["s_mm"], 1)

                def probs_T(u):
                    pe.wait_ge(s["probs"], g * U + u + 1)
                    if u >= 1:
                        pe.wait_ge(s["pT"], (g * U + u) * 2)
                    for j in range(H // 2):
                        mm = pe.transpose(bank[5 + j // 4][:, j % 4 * P:(j % 4 + 1) * P],
                                          probs[:, u % 2, j * P:(j + 1) * P], ident)
                        if j % 4 == 3:
                            mm.then_inc(s["pT_mm"], 1)

                def values(u):
                    pe.wait_ge(s["pT"], (g * U + u + 1) * 2)
                    if u >= 2:
                        pe.wait_ge(s["attn"], (g * U + u - 1) * TB)
                    w = TB * 2 * VW
                    for j in range(H // 2):
                        mm = pe.matmul(bank[(7, 0)[u % 2]][:, j * w:(j + 1) * w], pT[:, u % 2, j, :],
                                       vx[:, TB * u:TB * u + TB, j, :, :].rearrange("p b h c -> p b (h c)"),
                                       start=True, stop=True)
                    mm.then_inc(s["pv_mm"], 1)

                pe.wait_ge(s["kx_dve"], (g + 1) * (HH // 2))
                pe.wait_ge(s["kx_pool"], (g + 1) * (HH // 2))
                pe.wait_ge(s["qT"], (g + 1) * 2 * U)
                pe.wait_ge(s["vx"], (g + 1) * 2)
                scores(0)
                scores(1)
                for u in range(U):
                    probs_T(u)
                    if u + 2 < U:
                        scores(u + 2)
                    values(u)
                for u in range(U):
                    pe.wait_ge(s["attn"], (g * U + u + 1) * TB)
                    mm = pe.transpose(bank[5][:, u * P:(u + 1) * P], attn[:, u, :], ident)
                mm.then_inc(s["attnT_mm"], 1)
                pe.wait_ge(s["attnT"], g + 1)
                for u in range(U):
                    mm = pe.matmul(bank[6][:, u * D:(u + 1) * D], attnT[:, u * P:(u + 1) * P], wproj[:, :],
                                   start=True, stop=True)
                mm.then_inc(s["proj_mm"], 1)
                pe.wait_ge(s["h2"], g + 1)
                for u in range(U):
                    mm = pe.transpose(bank[7][:, u * P:(u + 1) * P], h2[:, u, :], ident)
                mm.then_inc(s["h2T_mm"], 1)
                pe.wait_ge(s["h2T"], g + 1)
                for u in range(U):
                    mm = pe.matmul(bank[0][:, u * E:(u + 1) * E], h2T[:, u * P:(u + 1) * P], wgate[:, :],
                                   start=True, stop=True)
                mm.then_inc(s["logit_mm"], 1)
                pe.wait_ge(s["selected"], g + 1)
                for v in range(U):
                    pe.matmul(bank[1][:, v * E:(v + 1) * E], tri_l, sel_l[:, v, :], start=True, stop=(v == 0))
                    for u in range(v):
                        pe.matmul(bank[1][:, v * E:(v + 1) * E], ones_l, sel_l[:, u, :], start=False,
                                  stop=(u == v - 1))
                for u in range(U):
                    mm = pe.matmul(bank[2][:, 0:E], ones_l, sel_l[:, u, :], start=(u == 0), stop=(u == U - 1))
                mm.then_inc(s["pos_mm"], 1)

            with pe.Fori(0, E // 2) as i:
                for n in range(2):
                    pe.wait_ge((s["w_in0"], s["w_in1"])[n], (i + 1) * 32)
                    pe.wait_ge((s["rows_in0"], s["rows_in1"])[n], (i + 1) * 16)
                    for c in range(2):
                        for r in range(4):
                            mm = pe.transpose(bank[c][:, r * P:(r + 1) * P], rows[n][:, 4 * c + r, :], ident)
                        mm.then_inc(s["tok_mm"], 1)
                    for c in range(2):
                        pe.wait_ge(s["tok"], i * 4 + (2 * n + c + 1))
                        for f in range(FC):
                            if c == 1:
                                pe.wait_ge(s["hid"], i * (4 * FC) + (2 * FC * n + f + 1))
                            pe.matmul(bank[2 + f][:, :], w1_sb[n][:, f * P:(f + 1) * P], tokT[:, c, :], start=True,
                                      stop=True).then_inc(s["hid_mm"], 1)
                    for c in range(2):
                        pe.wait_ge(s["hid"], i * (4 * FC) + (2 * FC * n + (c + 1) * FC))
                        for r in range(4):
                            for f in range(FC):
                                mm = pe.matmul(bank[6 + c][:, r * D:(r + 1) * D], hid[:, c, f, r * P:(r + 1) * P],
                                               w2_sb[n][:, f, :], start=(f == 0), stop=(f == FC - 1))
                        mm.then_inc(s["exp_mm"], 1)


def constants():
    import numpy as np

    f = np.zeros((P, C_WIDTH), np.float32)
    p = np.arange(P)
    f[:, C_IDENT:C_IDENT + P] = np.eye(P)
    inv_freq = (1.0 / 10000.0 ** (np.arange(0, HD, 2, dtype=np.float32) / np.float32(HD))).astype(np.float32)
    ang = ((p % S).astype(np.float32)[:, None] * inv_freq).astype(np.float32)
    f[:, C_COS:C_COS + 4] = np.cos(ang)
    f[:, C_SIN:C_SIN + 4] = np.sin(ang)
    f[:, C_NSIN:C_NSIN + 4] = -np.sin(ang)
    f[:, C_BLOCK:C_BLOCK + D] = (p[:, None] // HD == np.arange(D)[None, :] // HD) * 2.0 ** -18
    f[:, C_HEAD:C_HEAD + HH] = (p[:, None] // HD) % HH == np.arange(HH)[None, :]
    f[:, C_RANK:C_RANK + E] = E - np.arange(E)
    f[:, C_EOFF:C_EOFF + E] = np.arange(E) * CAP - 1
    b = np.zeros((P, L_WIDTH), np.float32)
    b[:, L_IDENT:L_IDENT + P] = np.eye(P)
    b[:, L_TRI:L_TRI + P] = p[:, None] <= p[None, :]
    b[:, L_ONES:L_ONES + P] = 1.0
    key = np.arange(HH * S) % S
    b[:, L_CAUSAL:] = np.where(key[None, :] <= (p % S)[:, None], 0.0, -(2.0 ** 32))
    return f, b


def kernel(**inputs):
    import numpy as np
    import concourse.bacc as bacc
    from concourse.bass_utils import run_bass_kernel_spmd

    a = {k: np.asarray(v) for k, v in inputs.items()}
    f, b = constants()
    qkv = a["L0_ffn_Wqkv"].reshape(D, H, 3, HD)
    awk, awv = a["L0_attn_Wk"], a["L0_attn_Wv"]
    abk, abv = a["L0_attn_bk"], a["L0_attn_bv"]
    arrays = {
        "x": a["x"],
        "ctx_1024": a["ctx_1024"],
        "mask": a["mask_SxS2_bk1"].view(np.uint8),
        "const_f32": f,
        "const_low": b,
        "xw_T": np.stack([a["L0_xattn_Wq"].T, a["L0_xattn_Wk"].T, a["L0_xattn_Wv"].T], 1),
        "xw_h": np.stack([a["L0_xattn_wq_h"], a["L0_xattn_wk_h"], a["L0_xattn_wv_h"]], 1),
        "xwo_heads": a["L0_xattn_Wo"].reshape(H, HD, D).transpose(1, 0, 2),
        "xb_qk": np.stack([a["L0_xattn_bq_h"], a["L0_xattn_bk_h"]], 1),
        "xb_v": a["L0_xattn_bv_h"],
        "awq": a["L0_attn_Wq"],
        "abq": a["L0_attn_bq"][:, None],
        "awkv": np.concatenate([awk[0], awv[0], awk[1], awv[1]], 1),
        "abkv": np.concatenate([abk[0], abv[0], abk[1], abv[1]]),
        "awo": a["L0_attn_Wo"],
        "abo": a["L0_attn_bo"],
        "cols": np.stack([a["L0_attn_ln_g"], a["L0_attn_ln_b"], a["L0_ffn_ln1_g"], a["L0_ffn_ln1_b"]], 1),
        "wqkv": np.concatenate([qkv[:, :, 0].reshape(D, D), qkv[:, :, 1].reshape(D, D),
                                qkv[:, 0::2, 2].reshape(D, D // 2), qkv[:, 1::2, 2].reshape(D, D // 2)], 1),
        "wproj": a["L0_ffn_Wproj"],
        "g2": a["L0_ffn_ln2_g"],
        "b2ln": a["L0_ffn_ln2_b"],
        "wgate": a["L0_ffn_Wgate"],
        "w1": a["L0_ffn_W1"],
        "b1c": a["L0_ffn_b1"].reshape(E, FC, P).transpose(2, 0, 1).reshape(P, E * FC),
        "w2": a["L0_ffn_W2"],
        "b2": a["L0_ffn_b2"],
    }
    arrays = {k: np.ascontiguousarray(v) for k, v in arrays.items()}
    nc = bacc.Bacc("TRN2", target_bir_lowering=False, num_devices=1)
    t = {
        n: nc.dram_tensor("in_" + n, list(v.shape), mybir.dt.from_np(v.dtype), kind="ExternalInput").ap()
        for n, v in arrays.items()}
    out = nc.dram_tensor("out", [B, S, D], F32, kind="ExternalOutput").ap()
    build_program(nc, t, out)
    r = run_bass_kernel_spmd(nc, [{"in_" + n: v for n, v in arrays.items()}], core_ids=[0])
    return r.results[0]["out"]
```

```python
from contextlib import ExitStack

import concourse.bass as bass
from concourse import mybir

ALU = mybir.AluOpType
ACT = mybir.ActivationFunctionType
F32 = mybir.dt.float32
BF16 = mybir.dt.bfloat16
U32 = mybir.dt.uint32
U8 = mybir.dt.uint8
X = mybir.AxisListType.X

P = 128
D = 128
B, S = 64, 64
KEYS = 128
H, HD = 16, 8
HH = H // 2
HH_DVE = 5
E, CAP = 8, 1024
FF = 512
FC = FF // P
U = 4
GROUPS = B * S // (U * P)
TB = 2
GB = U * TB
EPS = 1e-5
LN_STEPS = 2 * U + 1
SCALE = float(HD) ** -0.5
SLOTS = E * CAP
TOKENS = B * S
ZERO_STORES = 4
ROW = D + 1
EMPTY = 65536.0
KV_BANK = (0, 1, 2, 0)
STATE_BANK = ((2, 0), (1, 0))
VW = HD + 1

C_IDENT = 0
C_COS = C_IDENT + P
C_SIN = C_COS + HD // 2
C_NSIN = C_SIN + HD // 2
C_BLOCK = C_NSIN + HD // 2
C_HEAD = C_BLOCK + D
C_RANK = C_HEAD + HH
C_EOFF = C_RANK + E
C_ROWID = C_EOFF + E
C_WIDTH = C_ROWID + 2 * U
L_IDENT = 0
L_TRI = L_IDENT + P
L_ONES = L_TRI + P
L_CAUSAL = L_ONES + P
L_WIDTH = L_CAUSAL + HH * S


def build_program(nc, t, out):
    xs = nc.dram_tensor("expert_in", [SLOTS, ROW], F32, kind="Internal").ap()
    contributions = nc.dram_tensor("contributions", [2 * TOKENS, D], F32, kind="Internal").ap()
    contributions_of = contributions.rearrange("(k g p u) d -> g p k u d", k=2, g=GROUPS, p=P)
    x_groups = t["x"].rearrange("(g u w) s d -> g (w s) u d", u=U, w=TB)
    out_groups = out.rearrange("(g u w) s d -> g (w s) u d", u=U, w=TB)
    ctx_groups = t["ctx_1024"].rearrange("(g b) k d -> g k b d", b=GB)
    xs_rows = xs.rearrange("(e p r) d -> e p r d", e=E, p=P)
    w1_rows = t["w1"]
    w2_rows = t["w2"].rearrange("e (c p) d -> e p c d", p=P)

    with ExitStack() as ctx:
        def sb(name, shape, dt=F32):
            return ctx.enter_context(nc.sbuf_tensor(name, shape, dt))

        names = """const_in weights_in prep prep_mm prep_cast presets prepared x_in ctx_in
            ln0 z0 z0T_mm ctxT_mm z0T ctxT q0_mm k0_mm v0_mm q0 k0 v0 s0_mm s0_step nmax0 p0 p0T_mm p0T o0_mm o0 y0_mm
            rsum0 x1 ln1 z1 z1T_mm z1T q1_mm q1 kv_mm kv state_mm state_half state o1_mm ln2 n1 n1T_mm n1T y1_mm x1c x2
            ln3 h h_T_mm hT qk_mm qk v_mm vx rope_a rope_b qkr qkT_mm qT kT kx kx_act
            s_mm smax ssub probs pT_mm pT pv_mm rsum attn attnT_mm attnT proj_mm z2 xp ln4 h2n h2g h2 h2T_mm h2T
            logit_mm route shift expd selected pos_mm slots scattered resid saved d_done
            w_in0 w_in1 rows_in0 rows_in1 tok_mm tok hid_mm hid exp_mm expert_out expert_stored
            root0 root1 root2 root3 root4 blank_done row_id h2_twin y_idx
            contributed0 contributed1 partial result result_stored""".split()
        names += [f"joined{g}" for g in range(GROUPS)]
        s = {n: ctx.enter_context(nc.semaphore(n)) for n in names}

        cf = sb("const_f32", [P, C_WIDTH])
        cl = sb("const_bf16", [P, L_WIDTH], BF16)
        cl_f32 = sb("const_low_f32", [P, L_WIDTH])
        ident = cf[:, C_IDENT:C_IDENT + P]
        cos = cf[:, C_COS:C_COS + 4]
        sin = cf[:, C_SIN:C_SIN + 4]
        nsin = cf[:, C_NSIN:C_NSIN + 4]
        block_scale = cf[:, C_BLOCK:C_BLOCK + D]
        head_mask = cf[:, C_HEAD:C_HEAD + HH]
        rank = cf[:, C_RANK:C_RANK + E]
        eoff = cf[:, C_EOFF:C_EOFF + E]
        row_id0 = cf[:, C_ROWID:C_ROWID + 2 * U].rearrange("p (k u) -> p k u", k=2)
        ident_l = cl[:, L_IDENT:L_IDENT + P]
        tri_l = cl[:, L_TRI:L_TRI + P]
        ones_l = cl[:, L_ONES:L_ONES + P]
        causal_l = cl[:, L_CAUSAL:L_CAUSAL + HH * S]
        xw_T = sb("xw_T", [P, 3, D])
        xw_h = sb("xw_h", [P, 3, HD])
        xw = sb("xw", [P, 3, HD])
        wo_heads = sb("wo_heads", [HD, H, D])
        wo_sum = sb("wo_sum", [HD, D])
        bqk_h = sb("bqk_h", [HD, 2])
        bv_h = sb("bv_h", [P, HD])
        mask_u8 = sb("mask_u8", [P, KEYS], U8)
        keep = sb("keep", [P, KEYS])
        fill = sb("fill", [P, KEYS])
        wq1 = sb("wq1", [P, D])
        bq1 = sb("bq1", [P, 1])
        wkv = sb("wkv", [P, 4 * D])
        bkv = sb("bkv", [P, 4 * D])
        wo1 = sb("wo1", [P, D])
        wo1_g = sb("wo1_g", [P, D])
        bo1 = sb("bo1", [P, D])
        c1 = sb("c1", [P, D])
        cols = sb("cols", [P, 4])
        bcols = sb("bcols", [P, 2, P])
        wqkv = sb("wqkv", [P, 3 * D])
        wqkv_g = sb("wqkv_g", [P, 3 * D])
        bqk = sb("bqk", [P, 2 * D])
        bv = sb("bv", [P, D // 2])
        wproj = sb("wproj", [P, D])
        g2 = sb("g2", [P, D])
        b2ln = sb("b2ln", [P, D])
        wgate = sb("wgate", [P, E])
        b1c = sb("b1c", [P, E * FC])
        b2 = sb("b2", [P, E, D])
        blank = sb("blank", [P, 8, ROW])

        x_sb = sb("x_sb", [P, U, D])
        ctx_sb = sb("ctx_sb", [P, GB, D])
        ln_parts = sb("ln_parts", [P, 5, U, 6])
        mv = sb("mv", [P, 5, U, 2])
        var_eps = sb("var_eps", [P, 6, U])
        rstd = sb("rstd", [P, 8, U])
        minus_half = sb("minus_half", [P, 2, U])
        z = sb("z", [P, U, D])
        zT = sb("zT", [P, U * P])
        ctxT = sb("ctxT", [P, GB * KEYS])
        q0T = sb("q0T", [HD, U * P])
        k0T = sb("k0T", [HD, GB * KEYS])
        v0 = sb("v0", [P, GB, HD])
        s0 = sb("s0", [P, U, KEYS])
        smax0 = sb("smax0", [P, U])
        nmax0 = sb("nmax0", [P, U])
        sum0 = sb("sum0", [P, U])
        rsum0 = sb("rsum0", [P, U])
        p0 = sb("p0", [P, U, KEYS])
        p0T = sb("p0T", [P, U * P])
        o0T = sb("o0T", [HD, U * P])
        x1 = sb("x1", [P, U, D])
        x1c = sb("x1c", [P, U, D])
        q1T = sb("q1T", [P, U * P])
        kv = sb("kv", [P, U, 4 * D])
        half_state = sb("half_state", [P, 2, TB, 2, D])
        state = sb("state", [P, 2, TB, 2, D])
        z2 = sb("z2", [P, U, D])
        h = sb("h", [P, U, D])
        hT = sb("hT", [P, U * P])
        qk = sb("qk", [P, U, 2 * D])
        rope_space = [sb(f"rope_space{n}", [P, 8, ROW]) for n in range(2)]
        rope_a, rope_b = [b[:, :, :].rearrange("p r d -> p (r d)")[:, 0:U * 2 * D]
                          .rearrange("p (u c) -> p u c", u=U) for b in rope_space]
        qkr = sb("qkr", [P, U, 2 * D])
        vx = sb("vx", [P, GB, H // 2, 2, VW])
        qblk = sb("qblk", [P, U, 2, P])
        kT = sb("kT", [P, U, 2, S])
        kx = sb("kx", [P, U, 2, HH, S])
        mxs = sb("mxs", [P, 2, H])
        probs = sb("probs", [P, 2, H * S])
        pT = sb("pT", [P, 2, H // 2, P])
        rsum = sb("rsum", [P, U, H])
        attn = sb("attn", [P, U, D])
        attnT = sb("attnT", [P, U * P])
        xp = sb("xp", [P, U, D])
        h2_rows = sb("h2_rows", [P, 2, U, ROW])
        h2 = h2_rows[:, 0, :, 0:D]
        row_id = h2_rows[:, :, :, D]
        h2T = sb("h2T", [P, U * P])
        lg = sb("lg", [P, 2, U, E])
        first = sb("first", [P, 2, U])
        tie = sb("tie", [P, 2, U, E])
        tie_max = sb("tie_max", [P, 2, U])
        sel = sb("sel", [P, 2, U, E])
        sel_l = sb("sel_l", [P, U, E], BF16)
        shifted = sb("shifted", [P, U, E + 1])
        expd = sb("expd", [P, U, E + 1])
        gate = sb("gate", [P, 2, U])
        esum = sb("esum", [P, U])
        count = sb("count", [P, 2, E])
        pos = sb("pos", [P, 2, U, E])
        kept = sb("kept", [P, U, E])
        picked = sb("picked", [P, 4, U, E])
        slot = sb("slot", [P, 6, 2, U])
        scatter_idx = sb("scatter_idx", [P, 2, U], U32)
        resid = sb("resid", [P, GROUPS, U, D])
        moments_all = sb("moments_all", [P, GROUPS, 2, U])
        gates_all = sb("gates_all", [P, GROUPS, 2, U])
        w1_sb = [sb(f"w1_sb{n}", [P, FF]) for n in range(2)]
        w2_sb = [sb(f"w2_sb{n}", [P, FC, D]) for n in range(2)]
        rows = rope_space
        tokT = sb("tokT", [P, 2, 512])
        hid = kx[:, :, :, :, :].rearrange("p (c v) h j k -> p c (v h) (j k)", c=2)
        y_sb = [kv[:, 2 * n:2 * n + 2, :].rearrange("p u (r d) -> p (u r) d", r=4) for n in range(2)]
        y_idx = [sb(f"y_idx{n}", [P, 8], U32) for n in range(2)]
        joined = [b[:, :, :].rearrange("p (k v) (r d) -> p k (v r) d", k=2, r=2) for b in (qk, qkr)]
        joined += [b[:, :, :].rearrange("p (k u) d -> p k u d", k=2) for b in (ctx_sb,)]
        joined += [ctxT[:, :].rearrange("p (k u d) -> p k u d", k=2, u=U)]
        joined += [b[:, :, :, :, :].rearrange("p k b u d -> p k (b u) d") for b in (half_state, state)]
        joined += [probs[:, n, :].rearrange("p (k u d) -> p k u d", k=2, u=U) for n in range(2)]

        bank = [ctx.enter_context(nc.psum_tensor(f"bank{n}", [P, 512], F32)) for n in range(8)]

        block = ctx.enter_context(nc.Block())

        def wait_apart(eng, sem, count):
            count = eng.compute_val(count)
            eng.wait_ge(s["weights_in"], 16 * len(LOADS))
            eng.wait_ge(sem, count)

        def wait_past(eng, sem, count):
            if not (isinstance(count, int) and count <= 0):
                eng.wait_ge(sem, count)

        def of_group(kept, g):
            return kept[:, bass.ds(g, 1), :, :].rearrange("p g a b -> p (g a) b")

        def pipeline(eng, iteration):
            lags = 4
            for t in range(lags - 1):
                iteration([t - lag if t >= lag else None for lag in range(lags)])
            with eng.Fori(0, GROUPS - (lags - 1)) as g:
                iteration([g + (lags - 1 - lag) for lag in range(lags)])
            for t in range(GROUPS, GROUPS + lags - 1):
                iteration([t - lag if t - lag < GROUPS else None for lag in range(lags)])

        def run(step, g, *more):
            if g is not None:
                step(g, *more)

        def over_tiles(ap, width):
            return ap.unsqueeze(1).broadcast_to([P, U, width])

        def per_tile(b):
            return b[:, :].rearrange("p (u n) -> p u n", u=U)

        LOADS = [(cf[:, :], t["const_f32"]), (cl_f32[:, :], t["const_low"]),
                 (xw_T[:, :, :], t["xw_T"]), (xw_h[:, :, :], t["xw_h"]), (wo_heads[:, :, :], t["xwo_heads"]),
                 (bqk_h[:, :], t["xb_qk"]), (bv_h[:, :], t["xb_v"].partition_broadcast(P)),
                 (mask_u8[0:S, :], t["mask"]), (mask_u8[S:P, :], t["mask"]),
                 (wq1[:, :], t["awq"]), (bq1[:, :], t["abq"]), (wkv[:, :], t["awkv"]),
                 (bkv[:, :], t["abkv"].partition_broadcast(P)),
                 (wo1[:, :], t["awo"]), (bo1[:, :], t["abo"].partition_broadcast(P)), (cols[:, :], t["cols"]),
                 (wqkv[:, :], t["wqkv"]), (wproj[:, :], t["wproj"]), (g2[:, :], t["g2"].partition_broadcast(P)),
                 (b2ln[:, :], t["b2ln"].partition_broadcast(P)), (wgate[:, :], t["wgate"]),
                 (b1c[:, :], t["b1c"]), (b2[:, :, :], t["b2"].partition_broadcast(P))]

        @block.sync
        def _(sp):
            for dst, src in LOADS:
                sp.dma_start(dst, src).then_inc(s["weights_in"], 16)
            sp.dma_start(ctx_sb[:, :, :], ctx_groups[0]).then_inc(s["ctx_in"], 16)
            sp.dma_start(x_sb[:, :, :], x_groups[0]).then_inc(s["x_in"], 16)
            with sp.Fori(0, GROUPS - 1) as g:
                sp.wait_ge(s["ctxT_mm"], (g + 1) * 2)
                sp.dma_start(ctx_sb[:, :, :], ctx_groups[bass.ds(g + 1, 1)].rearrange("a k b d -> (a k) b d"))\
                    .then_inc(s["ctx_in"], 16)
                sp.wait_ge(s["x1"], (g + 1) * U)
                sp.dma_start(x_sb[:, :, :], x_groups[bass.ds(g + 1, 1)].rearrange("a k b d -> (a k) b d"))\
                    .then_inc(s["x_in"], 16)

            def load_rows(e, n):
                sp.dma_start(rows[n][:, :, :], xs_rows[bass.ds(e, 1)].rearrange("a p r d -> (a p) r d"))\
                    .then_inc((s["rows_in0"], s["rows_in1"])[n], 16)

            def load_weights(e, n):
                w_in = (s["w_in0"], s["w_in1"])[n]
                sp.dma_start(w1_sb[n][:, :], w1_rows[bass.ds(e, 1)].rearrange("a p f -> (a p) f"))\
                    .then_inc(w_in, 16)
                sp.dma_start(w2_sb[n][:, :, :], w2_rows[bass.ds(e, 1)].rearrange("a p c d -> (a p) c d"))\
                    .then_inc(w_in, 16)

            for n in range(2):
                load_weights(n, n)
            sp.wait_ge(s["scattered"], (GROUPS * U * 2 + ZERO_STORES) * 16)
            for n in range(2):
                load_rows(n, n)
            with sp.Fori(0, E // 2 - 1) as i:
                for n in range(2):
                    sp.wait_ge(s["tok_mm"], i * 4 + (2 * n + 2))
                    sp.wait_ge(s["y_idx"], i * 2 + (n + 1))
                    load_rows(i * 2 + (n + 2), n)
                    sp.wait_ge(s["exp_mm"], i * 4 + (2 * n + 2))
                    load_weights(i * 2 + (n + 2), n)
            for n in range(2):
                sp.wait_ge(s[f"contributed{n}"], (GROUPS + SLOTS // P // 2) * 16)
            for g in range(GROUPS):
                sp.dma_start(joined[g], contributions_of[g]).then_inc(s[f"joined{g}"], 16)

        @block.gpsimd
        def _(pool):
            pool.memset(blank[:, :, :], 0.0).then_inc(s["blank_done"], 1)
            pool.wait_ge(s["blank_done"], 1)
            pool.memset(blank[:, :, D:ROW], EMPTY).then_inc(s["blank_done"], 1)
            pool.memset(qblk[:, :, :, :], 0.0).then_inc(s["presets"], 1)
            pool.memset(vx[:, :, :, :, :], 0.0).then_inc(s["presets"], 1)
            pool.memset(count[:, :, :], 0.0).then_inc(s["presets"], 1)
            pool.memset(xp[:, :, :], 0.0).then_inc(s["resid"], 1)
            pool.memset(minus_half[:, :, :], -0.5).then_inc(s["presets"], 1)
            pool.wait_ge(s["presets"], 4)
            pool.memset(vx[0:S, :, :, 0, HD:VW], 1.0).then_inc(s["presets"], 1)
            pool.memset(vx[S:P, :, :, 1, HD:VW], 1.0).then_inc(s["presets"], 1)
            pool.wait_ge(s["weights_in"], 16 * len(LOADS))
            pool.wait_ge(s["blank_done"], 2)
            for n in range(ZERO_STORES):
                pool.dma_start(xs.rearrange("(n p a r) d -> n p a r d", n=ZERO_STORES, p=P, r=8)[n],
                               blank[:, :, :].unsqueeze(1).broadcast_to([P, SLOTS // (ZERO_STORES * P * 8), 8, ROW]))\
                    .then_inc(s["scattered"], 16)
            pool.wait_ge(s["prepared"], 1)
            pool.wait_ge(s["scattered"], ZERO_STORES * 16)

            def root(g, ln, steps, first, many, done):
                pool.wait_ge(ln, (g + 1) * steps)
                pool.tensor_tensor(rstd[:, first:first + many, :], var_eps[:, first:first + many, :],
                                   minus_half[:, 0:many, :], ALU.pow).then_inc(done, 1)

            def a_offset(g):
                pool.wait_ge(s["x1"], (g + 1) * U)
                pool.tensor_tensor(x1c[:, :, :], x1[:, :, :], over_tiles(c1[:, :], D), ALU.add)\
                    .then_inc(s["x1c"], 1)

            def b_rope(g):
                pool.wait_ge(s["qk"], (g + 1) * 2)
                halves = qk[:, :, :].rearrange("p u (c k f) -> p (u c) k f", k=2, f=4)
                crossed = rope_b[:, :, :].rearrange("p u (c k f) -> p (u c) k f", k=2, f=4)
                for k, table in ((0, nsin), (1, sin)):
                    pool.tensor_tensor(crossed[:, :, k, :], halves[:, :, 1 - k, :],
                                       table.unsqueeze(1).broadcast_to([P, U * 2 * H, 4]), ALU.mult)\
                        .then_inc(s["rope_b"], 1)

            def c_norm(g):
                pool.wait_ge(s["h2n"], (g + 1) * U)
                pool.tensor_tensor(h2, h2, over_tiles(g2[:, :], D), ALU.mult).then_inc(s["h2g"], 1)
                pool.wait_ge(s["h2g"], g + 1)
                pool.tensor_tensor(h2, h2, over_tiles(b2ln[:, :], D), ALU.add).then_inc(s["h2"], 1)

            def c_blank(g):
                for k in range(2):
                    pool.dma_start(contributions_of[bass.ds(g, 1)].rearrange("a p k u d -> (a p) k u d")[:, k],
                                   blank[:, 0:U, 0:D]).then_inc(s[f"contributed{k}"], 16)

            def c_residual(g):
                pool.wait_ge(s["xp"], g + 1)
                pool.tensor_tensor(of_group(resid, g), of_group(resid, g), xp[:, :, :], ALU.add)\
                    .then_inc(s["resid"], 1)

            def c_scatter(g, k):
                if k == 0:
                    wait_apart(pool, s["slots"], g + 1)
                    pool.wait_ge(s["h2"], g + 1)
                    pool.wait_ge(s["row_id"], g + 2)
                else:
                    wait_apart(pool, s["h2_twin"], g + 1)
                for u in range(U):
                    pool.indirect_dma_start(
                        xs, bass.IndirectOffsetOnAxis(scatter_idx[:, k, u:u + 1], 0), h2_rows[:, k, u, :], None,
                        bounds_check=SLOTS - 1, oob_is_err=False).then_inc(s["scattered"], 16)

            def iteration(group):
                run(root, group[2], s["ln3"], LN_STEPS + 1, 3, 2, s["root3"])
                run(b_rope, group[2])
                run(root, group[3], s["ln4"], LN_STEPS, 5, 1, s["root4"])
                run(c_norm, group[3])
                run(c_blank, group[3])
                run(root, group[1], s["ln1"], LN_STEPS, 1, 1, s["root1"])
                run(c_residual, group[3])
                run(c_scatter, group[3], 0)
                run(c_scatter, group[3], 1)
                run(a_offset, group[1])
                run(root, group[1], s["ln2"], LN_STEPS, 2, 1, s["root2"])
                run(root, group[0], s["ln0"], LN_STEPS, 0, 1, s["root0"])

            pipeline(pool, iteration)

            for n in range(2):
                pool.wait_ge(s[f"contributed{n}"], GROUPS * 16)
            with pool.Fori(0, E // 2) as i:
                for n in range(2):
                    wait_apart(pool, s["y_idx"], i * 2 + (n + 1))
                    for c in range(2):
                        wait_apart(pool, s["expert_out"], i * 4 + (2 * n + c + 1))
                        for r in range(4 * c, 4 * c + 4):
                            pool.indirect_dma_start(
                                contributions, bass.IndirectOffsetOnAxis(y_idx[n][:, r:r + 1], 0), y_sb[n][:, r, :],
                                None, bounds_check=2 * TOKENS - 1, oob_is_err=False)\
                                .then_inc(s[f"contributed{n}"], 16)

        @block.scalar
        def _(act):
            act.wait_ge(s["weights_in"], 16 * len(LOADS))
            act.wait_ge(s["prepared"], 1)
            act.wait_ge(s["presets"], 6)
            def a_context(g, n):
                act.wait_ge(s["ctxT_mm"], g * 2 + n + 1)
                act.activation(ctxT[:, n * 512:(n + 1) * 512], bank[n][:, :], ACT.Copy).then_inc(s["ctxT"], 1)

            def a_z0T(g):
                act.wait_ge(s["z0T_mm"], g + 1)
                act.activation(zT[:, :], bank[2][:, :], ACT.Copy).then_inc(s["z0T"], 1)

            def a_keys(g, n):
                act.wait_ge(s["k0_mm"], g * 2 + n + 1)
                act.activation(k0T[:, n * 512:(n + 1) * 512], bank[n][0:HD, :], ACT.Identity,
                               bias=bqk_h[:, 1:2]).then_inc(s["k0"], 1)

            def a_queries(g):
                act.wait_ge(s["q0_mm"], g + 1)
                act.activation(q0T[:, :], bank[2][0:HD, :], ACT.Identity, bias=bqk_h[:, 0:1]).then_inc(s["q0"], 1)

            def a_softmax(g):
                act.wait_ge(s["nmax0"], g + 1)
                for u in range(U):
                    act.activation(p0[:, u, :], s0[:, u, :], ACT.Exp, bias=nmax0[:, u:u + 1], scale=SCALE,
                                   accum_out=sum0[:, u:u + 1]).then_inc(s["p0"], 1)

            def a_p0T(g):
                act.wait_ge(s["p0T_mm"], g + 1)
                act.activation(p0T[:, :], bank[2][:, :], ACT.Copy).then_inc(s["p0T"], 1)

            def a_values(g):
                act.wait_ge(s["o0_mm"], g + 1)
                act.activation(o0T[:, :], bank[0][0:HD, :], ACT.Copy).then_inc(s["o0"], 1)

            def a_z1T(g):
                act.wait_ge(s["z1T_mm"], g + 1)
                act.activation(zT[:, :], bank[2][:, :], ACT.Copy).then_inc(s["z1T"], 1)

            def a_q1(g):
                act.wait_ge(s["q1_mm"], g + 1)
                act.activation(q1T[:, :], bank[1][:, :], ACT.Identity, bias=bq1[:, 0:1]).then_inc(s["q1"], 1)

            def a_n1T(g):
                act.wait_ge(s["n1T_mm"], g + 1)
                act.activation(zT[:, :], bank[1][:, :], ACT.Copy).then_inc(s["n1T"], 1)

            def b_hT(g):
                act.wait_ge(s["h_T_mm"], g + 1)
                act.activation(hT[:, :], bank[3][:, :], ACT.Copy).then_inc(s["hT"], 1)

            def b_qkT(g):
                act.wait_ge(s["qkT_mm"], (g + 1) * U)
                for n in range(2):
                    for u in range(U):
                        src = bank[3 + u][0:HH * HD, :].rearrange("p (c h b t) -> p c h b t", c=2, h=2, b=TB)
                        act.activation(kT[n * 64:(n + 1) * 64, u, :, :], src[:, 1, :, n, :], ACT.Copy)\
                            .then_inc(s["kT"] if u == U - 1 else s["shift"], 1)
                for n in range(2):
                    for u in range(U):
                        src = bank[3 + u][0:HH * HD, :].rearrange("p (c h b t) -> p c h b t", c=2, h=2, b=TB)
                        act.activation(qblk[n * 64:(n + 1) * 64, u, :, n * S:(n + 1) * S], src[:, 0, :, n, :],
                                       ACT.Copy).then_inc(s["qT"], 1)

            def b_keys(g, n):
                act.wait_ge(s["kT"], (g + 1) * 2)
                for j in range(HH_DVE, HH):
                    act.activation(kx[:, 2 * n:2 * n + 2, :, j, :], kT[:, 2 * n:2 * n + 2, :, :], ACT.Copy,
                                   scale=head_mask[:, j:j + 1]).then_inc(s["kx_act"], 1)

            def b_exp(g, u):
                act.wait_ge(s["ssub"], g * U + u + 1)
                act.activation(probs[:, u % 2, :], probs[:, u % 2, :], ACT.Exp, scale=SCALE)\
                    .then_inc(s["probs"], 1)

            def b_probs_T(g, u, n):
                act.wait_ge(s["pT_mm"], (g * U + u) * 2 + n + 1)
                act.activation(pT[:, u % 2, 4 * n:4 * n + 4, :],
                               bank[5][:, :].rearrange("p (j t) -> p j t", j=4), ACT.Copy).then_inc(s["pT"], 1)

            def c_attnT(g):
                act.wait_ge(s["attnT_mm"], g + 1)
                act.activation(attnT[:, :], bank[7][:, :], ACT.Copy).then_inc(s["attnT"], 1)

            def c_h2T(g):
                act.wait_ge(s["h2T_mm"], g + 1)
                act.activation(h2T[:, :], bank[7][:, :], ACT.Copy).then_inc(s["h2T"], 1)

            def c_twin(g):
                act.wait_ge(s["h2"], g + 1)
                act.activation(h2_rows[:, 1, :, 0:D], h2, ACT.Copy).then_inc(s["h2_twin"], 1)

            def c_gates(g):
                act.wait_ge(s["expd"], g * 2 + 1)
                act.activation(expd[:, :, :], shifted[:, :, :], ACT.Exp).then_inc(s["expd"], 1)

            def iteration(group):
                run(a_n1T, group[1])
                run(a_context, group[0], 0)
                run(a_context, group[0], 1)
                run(c_attnT, group[2])
                run(b_hT, group[1])
                run(a_keys, group[0], 0)
                run(a_keys, group[0], 1)
                run(a_z0T, group[0])
                run(a_queries, group[0])
                run(b_qkT, group[1])
                run(a_softmax, group[0])
                run(c_h2T, group[2])
                run(c_twin, group[2])
                run(b_keys, group[1], 0)
                run(a_p0T, group[0])
                run(a_values, group[0])
                run(b_keys, group[1], 1)
                run(b_exp, group[1], 0)
                run(a_z1T, group[0])
                run(b_probs_T, group[1], 0, 0)
                run(b_exp, group[1], 1)
                run(c_gates, group[2])
                run(b_probs_T, group[1], 0, 1)
                run(b_probs_T, group[1], 1, 0)
                run(b_exp, group[1], 2)
                run(b_probs_T, group[1], 1, 1)
                run(b_probs_T, group[1], 2, 0)
                run(a_q1, group[0])
                run(b_exp, group[1], 3)
                run(b_probs_T, group[1], 2, 1)
                run(b_probs_T, group[1], 3, 0)
                run(b_probs_T, group[1], 3, 1)

            pipeline(act, iteration)
            with act.Fori(0, E) as e:
                for c in range(2):
                    for f in range(FC):
                        wait_apart(act, s["hid_mm"], e * (2 * FC) + c * FC + f + 1)
                        act.activation(hid[:, c, f, :], bank[2 + f][:, :], ACT.Gelu,
                                       bias=b1c[:, bass.ds(e * FC + f, 1)]).then_inc(s["hid"], 1)
            with act.Fori(0, GROUPS) as g:
                act.wait_ge(s["result"], (g + 1) * U)
                act.dma_start(out_groups[bass.ds(g, 1)].rearrange("a p u d -> (a p) u d"),
                              resid[:, bass.ds(g, 1), :, :].rearrange("p a u d -> p (a u) d"))\
                    .then_inc(s["result_stored"], 16)
            act.wait_ge(s["result_stored"], GROUPS * 16)

        @block.vector
        def _(dve):
            dve.wait_ge(s["weights_in"], 16 * len(LOADS))
            dve.tensor_reduce(wo_sum[:, :], wo_heads[:, :, :].rearrange("p h d -> p d h"), X, ALU.add)\
                .then_inc(s["prep"], 1)
            dve.tensor_copy(cl[:, :], cl_f32[:, :]).then_inc(s["prep_cast"], 1)
            dve.tensor_copy(fill[:, :], mask_u8[:, :]).then_inc(s["prep_cast"], 1)
            dve.wait_ge(s["prep_cast"], 2)
            dve.tensor_scalar(keep[:, :], fill[:, :], -1.0, 1.0, ALU.mult, ALU.add).then_inc(s["prep_cast"], 1)
            dve.wait_ge(s["prep_cast"], 3)
            dve.tensor_scalar(fill[:, :], fill[:, :], -1e9 / SCALE, None, ALU.mult).then_inc(s["prep"], 1)
            dve.tensor_tensor(wq1[:, :], wq1[:, :], ident, ALU.add).then_inc(s["prep"], 1)
            for k in range(4):
                dve.tensor_tensor(wkv[:, k * D:(k + 1) * D], wkv[:, k * D:(k + 1) * D], ident, ALU.add)\
                    .then_inc(s["prep_cast"], 1)
            dve.tensor_scalar(wo1_g[:, :], wo1[:, :], cols[:, 0:1], None, ALU.mult).then_inc(s["prep"], 1)
            dve.tensor_scalar(wqkv_g[:, :], wqkv[:, :], cols[:, 2:3], None, ALU.mult).then_inc(s["prep"], 1)
            for n in range(2):
                dve.tensor_scalar(bcols[:, n, :], ident, 0.0, cols[:, 2 * n + 1:2 * n + 2], ALU.mult, ALU.add)\
                    .then_inc(s["prep_cast"], 1)
            dve.wait_ge(s["prep_mm"], 1)
            dve.tensor_copy(xw[:, :, :], bank[0][:, 0:3 * HD].rearrange("p (c d) -> p c d", c=3))\
                .then_inc(s["prep"], 1)
            dve.tensor_copy(bqk[:, :], bank[1][:, 0:2 * D]).then_inc(s["prep"], 1)
            dve.tensor_copy(bv[0:S, :], bank[1][0:S, 2 * D:2 * D + D // 2]).then_inc(s["prep_cast"], 1)
            dve.tensor_copy(bv[S:P, :], bank[1][S:P, 2 * D + D // 2:3 * D]).then_inc(s["prep"], 1)
            dve.wait_ge(s["prep_cast"], 10)
            dve.tensor_tensor(c1[:, :], bank[2][:, 0:D], bo1[:, :], ALU.add).then_inc(s["prep"], 1)
            dve.wait_ge(s["prep"], 9)
            dve.memset(smax0[:, :], 0.0).then_inc(s["d_done"], 1)
            dve.memset(rsum0[:, :], 0.0).then_inc(s["prepared"], 1)
            dve.tensor_copy(row_id, row_id0).then_inc(s["row_id"], 1)
            dve.wait_ge(s["presets"], 6)

            def stats(g, n, sem, src, steps=LN_STEPS):
                at = 5 if n == 4 else n
                for u in range(U):
                    dve.bn_stats(ln_parts[:, n, u, :], src(u)).then_inc(sem, 1)
                wait_apart(dve, sem, g * steps + U)
                for u in range(U):
                    dve.bn_aggr(mv[:, n, u, :], ln_parts[:, n, u, :]).then_inc(sem, 1)
                dve.wait_ge(sem, g * steps + 2 * U)
                dve.tensor_scalar(var_eps[:, at, :], mv[:, n, :, 1], EPS, None, ALU.add).then_inc(sem, 1)

            def normalise(dst, n, k, src, sem):
                for u in range(U):
                    dve.tensor_scalar(dst[:, u, :], src(u), mv[:, n, u, 0:1], rstd[:, k, u:u + 1],
                                      ALU.subtract, ALU.mult).then_inc(sem, 1)

            def x2_tile(g, u):
                return resid[:, bass.ds(g, 1), u, :].rearrange("p a d -> p (a d)")

            def a_stats0(g):
                dve.wait_ge(s["x_in"], (g + 1) * 16)
                stats(g, 0, s["ln0"], lambda u: x_sb[:, u, :])

            def a_norm0(g):
                dve.wait_ge(s["root0"], g + 1)
                normalise(z, 0, 0, lambda u: x_sb[:, u, :], s["z0"])

            def a_v0(g):
                dve.wait_ge(s["v0_mm"], g + 1)
                dve.tensor_tensor(v0[:, :, :], bank[0][:, 0:GB * HD].rearrange("p (b d) -> p b d", b=GB),
                                  bv_h[:, :].unsqueeze(1).broadcast_to([P, GB, HD]), ALU.add).then_inc(s["v0"], 1)

            def a_softmax(g):
                dve.wait_ge(s["s0_mm"], g + 1)
                dve.tensor_tensor(s0[:, :, :], per_tile(bank[1]), over_tiles(keep[:, :], KEYS), ALU.mult)\
                    .then_inc(s["s0_step"], 1)
                dve.wait_ge(s["s0_step"], g * 3 + 1)
                dve.tensor_tensor(s0[:, :, :], s0[:, :, :], over_tiles(fill[:, :], KEYS), ALU.add)\
                    .then_inc(s["s0_step"], 1)
                dve.wait_ge(s["s0_step"], g * 3 + 2)
                dve.tensor_reduce(smax0[:, :], s0[:, :, :], X, ALU.max).then_inc(s["s0_step"], 1)
                dve.wait_ge(s["s0_step"], g * 3 + 3)
                dve.tensor_scalar(nmax0[:, :], smax0[:, :], -SCALE, None, ALU.mult).then_inc(s["nmax0"], 1)

            def a_rsum0(g):
                dve.wait_ge(s["p0"], (g + 1) * U)
                dve.reciprocal(rsum0[:, :], sum0[:, :]).then_inc(s["rsum0"], 1)

            def a_x1(g):
                dve.wait_ge(s["rsum0"], g + 1)
                dve.wait_ge(s["y0_mm"], g + 1)
                for u in range(U):
                    dve.scalar_tensor_tensor(out=x1[:, u, :], in0=bank[1][:, u * D:(u + 1) * D],
                                             scalar=rsum0[:, u:u + 1], in1=x_sb[:, u, :], op0=ALU.mult,
                                             op1=ALU.add).then_inc(s["x1"], 1)
                dve.wait_ge(s["x1"], (g + 1) * U)
                stats(g, 1, s["ln1"], lambda u: x1[:, u, :])

            def a_norm1(g):
                dve.wait_ge(s["root1"], g + 1)
                normalise(z, 1, 1, lambda u: x1[:, u, :], s["z1"])

            def a_kv(g, u):
                dve.wait_ge(s["kv_mm"], g * U + u + 1)
                dve.tensor_tensor(kv[:, u, :], bank[KV_BANK[u]][:, :], bkv[:, :], ALU.add).then_inc(s["kv"], 1)

            def a_state(g, pair):
                dve.wait_ge(s["state_mm"], g * 2 + pair + 1)
                for b in range(TB):
                    st = bank[STATE_BANK[pair][b]][:, :].rearrange("p (u k e) -> p u k e", u=2, k=2)
                    dve.tensor_tensor(half_state[:, pair, b, :, :], st[:, :, 0, :],
                                      block_scale.unsqueeze(1).broadcast_to([P, 2, D]), ALU.mult)\
                        .then_inc(s["state_half"], 1)
                for b in range(TB):
                    dve.wait_ge(s["state_half"], (g * 2 + pair) * TB + b + 1)
                    st = bank[STATE_BANK[pair][b]][:, :].rearrange("p (u k e) -> p u k e", u=2, k=2)
                    dve.tensor_tensor(state[:, pair, b, :, :], half_state[:, pair, b, :, :], st[:, :, 1, :],
                                      ALU.mult).then_inc(s["state"], 1)

            def a_stats2(g):
                dve.wait_ge(s["o1_mm"], g + 1)
                stats(g, 2, s["ln2"], lambda u: bank[2][:, u * D:(u + 1) * D])

            def a_norm2(g):
                dve.wait_ge(s["root2"], g + 1)
                normalise(z, 2, 2, lambda u: bank[2][:, u * D:(u + 1) * D], s["n1"])

            def a_x2(g):
                dve.wait_ge(s["y1_mm"], g + 1)
                dve.wait_ge(s["x1c"], g + 1)
                dve.tensor_tensor(of_group(resid, g), per_tile(bank[0]), x1c[:, :, :], ALU.add)\
                    .then_inc(s["x2"], 1)

            def b_stats(g):
                wait_apart(dve, s["x2"], g + 1)
                stats(g, 3, s["ln3"], lambda u: x2_tile(g, u), LN_STEPS + 1)
                dve.wait_ge(s["ln3"], g * (LN_STEPS + 1) + LN_STEPS)
                dve.scalar_tensor_tensor(out=var_eps[:, 4, :], in0=var_eps[:, 3, :], scalar=EPS,
                                         in1=mv[:, 3, :, 1], op0=ALU.mult, op1=ALU.add).then_inc(s["ln3"], 1)

            def b_norm(g):
                dve.wait_ge(s["root3"], g + 1)
                normalise(h, 3, 4, lambda u: x2_tile(g, u), s["h"])
                dve.tensor_copy(of_group(moments_all, g)[:, 0, :], mv[:, 3, :, 0])
                dve.tensor_copy(of_group(moments_all, g)[:, 1, :], rstd[:, 3, :]).then_inc(s["saved"], 1)

            def b_qk(g, n):
                dve.wait_ge(s["qk_mm"], g * 2 + n + 1)
                dve.tensor_tensor(qk[:, 2 * n:2 * n + 2, :], bank[4 + n][:, :].rearrange("p (u c) -> p u c", u=2),
                                  bqk[:, :].unsqueeze(1).broadcast_to([P, 2, 2 * D]), ALU.add).then_inc(s["qk"], 1)

            def b_values(g):
                dve.wait_ge(s["v_mm"], g + 1)
                for n in range(2):
                    at = slice(n * S, (n + 1) * S)
                    dve.tensor_tensor(vx[at, :, :, n, 0:HD],
                                      bank[6][at, :].rearrange("p (b j d) -> p b j d", b=GB, d=HD),
                                      bv[at, :].rearrange("p (j d) -> p j d", d=HD).unsqueeze(1)
                                      .broadcast_to([S, GB, H // 2, HD]), ALU.add).then_inc(s["vx"], 1)

            def b_rope(g):
                dve.wait_ge(s["qk"], (g + 1) * 2)
                dve.tensor_tensor(rope_a[:, :, :].rearrange("p u (c f) -> p (u c) f", f=4),
                                  qk[:, :, :].rearrange("p u (c f) -> p (u c) f", f=4),
                                  cos.unsqueeze(1).broadcast_to([P, U * 4 * H, 4]), ALU.mult)\
                    .then_inc(s["rope_a"], 1)

            def b_rope_sum(g):
                dve.wait_ge(s["rope_a"], g + 1)
                dve.wait_ge(s["rope_b"], (g + 1) * 2)
                dve.tensor_tensor(qkr[:, :, :], rope_a[:, :, :], rope_b[:, :, :], ALU.add).then_inc(s["qkr"], 1)

            def b_keys(g, n):
                dve.wait_ge(s["kT"], (g + 1) * 2)
                for j in range(HH_DVE):
                    dve.tensor_scalar(kx[:, 2 * n:2 * n + 2, :, j, :], kT[:, 2 * n:2 * n + 2, :, :],
                                      head_mask[:, j:j + 1], None, ALU.mult).then_inc(s["kx"], 1)

            def b_shift(g, u):
                dve.wait_ge(s["s_mm"], g * U + u + 1)
                for n in range(2):
                    dve.tensor_reduce(mxs[:, u % 2, n * HH:(n + 1) * HH],
                                      bank[3 + n][:, :].rearrange("p (h k) -> p h k", h=HH), X, ALU.max)\
                        .then_inc(s["smax"], 1)
                dve.wait_ge(s["smax"], (g * U + u + 1) * 2)
                if u >= 2:
                    dve.wait_ge(s["pT_mm"], (g * U + u - 1) * 2)
                for n in range(2):
                    ins = dve.tensor_tensor(
                        probs[:, u % 2, n * 512:(n + 1) * 512].rearrange("p (h k) -> p h k", h=HH),
                        bank[3 + n][:, :].rearrange("p (h k) -> p h k", h=HH),
                        mxs[:, u % 2, n * HH:(n + 1) * HH].unsqueeze(2).broadcast_to([P, HH, S]), ALU.subtract)
                ins.then_inc(s["ssub"], 1)

            def b_attention(g, u):
                dve.wait_ge(s["pv_mm"], g * U + u + 1)
                if u == 0:
                    wait_past(dve, s["attnT_mm"], g)
                pv = bank[6][:, 0:H // 2 * TB * 2 * VW].rearrange("p (j b h c) -> p j b h c", b=TB, h=2, c=VW)
                for b in range(TB):
                    at = slice(b * S, (b + 1) * S)
                    dve.reciprocal(rsum[at, u, :].rearrange("p (j h) -> p j h", h=2), pv[at, :, b, :, HD])\
                        .then_inc(s["rsum"], 1)
                for b in range(TB):
                    at = slice(b * S, (b + 1) * S)
                    dve.wait_ge(s["rsum"], (g * U + u) * TB + b + 1)
                    dve.tensor_tensor(
                        attn[at, u, :].rearrange("p (j h c) -> p j h c", h=2, c=HD), pv[at, :, b, :, 0:HD],
                        rsum[at, u, :].rearrange("p (j h) -> p j h", h=2).unsqueeze(3)
                        .broadcast_to([S, H // 2, 2, HD]), ALU.mult).then_inc(s["attn"], 1)

            def c_z2(g):
                dve.wait_ge(s["saved"], g + 1)
                for u in range(U):
                    m = moments_all[:, bass.ds(g, 1), :, u].rearrange("p g a -> p (g a)")
                    dve.tensor_scalar(z2[:, u, :], x2_tile(g, u), m[:, 0:1], m[:, 1:2], ALU.subtract, ALU.mult)\
                        .then_inc(s["z2"], 1)

            def c_xp(g):
                dve.wait_ge(s["proj_mm"], g + 1)
                dve.wait_ge(s["resid"], g + 1)
                dve.wait_ge(s["z2"], (g + 1) * U)
                dve.tensor_tensor(xp[:, :, :], per_tile(bank[7]), z2[:, :, :], ALU.add).then_inc(s["xp"], 1)
                dve.wait_ge(s["xp"], g + 1)
                stats(g, 4, s["ln4"], lambda u: xp[:, u, :])

            def c_norm(g):
                dve.wait_ge(s["root4"], g + 1)
                dve.wait_ge(s["scattered"], g * (U * 2 * 16) + ZERO_STORES * 16)
                normalise(h2, 4, 5, lambda u: xp[:, u, :], s["h2n"])
                dve.wait_ge(s["row_id"], g + 1)
                dve.tensor_scalar(row_id, row_id, float(P * U), None, ALU.add).then_inc(s["row_id"], 1)

            route_steps = 25
            step = [0]

            def link(g, ins):
                step[0] += 1
                ins.then_inc(s["route"], 1)
                dve.wait_ge(s["route"], g * route_steps + step[0])

            def over_experts(ap):
                return ap.unsqueeze(2).broadcast_to([P, U, E])

            def c_select(g):
                step[0] = 0
                dve.wait_ge(s["logit_mm"], g + 1)
                link(g, dve.tensor_copy(lg[:, 0, :, :], bank[7][:, 0:U * E].rearrange("p (u e) -> p u e", u=U)))
                for k in range(2):
                    link(g, dve.tensor_reduce(first[:, k, :], lg[:, k, :, :], X, ALU.max))
                    link(g, dve.tensor_tensor(tie[:, k, :, :], lg[:, k, :, :], over_experts(first[:, k, :]),
                                              ALU.is_equal))
                    link(g, dve.tensor_tensor(tie[:, k, :, :], tie[:, k, :, :], over_tiles(rank, E), ALU.mult))
                    link(g, dve.tensor_reduce(tie_max[:, k, :], tie[:, k, :, :], X, ALU.max))
                    link(g, dve.tensor_tensor(sel[:, k, :, :], over_tiles(rank, E), over_experts(tie_max[:, k, :]),
                                              ALU.is_equal))
                    if k == 0:
                        link(g, dve.scalar_tensor_tensor(out=lg[:, 1, :, :], in0=sel[:, 0, :, :], scalar=-3e38,
                                                         in1=lg[:, 0, :, :], op0=ALU.mult, op1=ALU.add))
                dve.tensor_tensor(sel_l[:, :, :], sel[:, 0, :, :], sel[:, 1, :, :], ALU.add).then_inc(s["selected"], 1)
                dve.tensor_tensor(shifted[:, :, 0:E], lg[:, 0, :, :], over_experts(first[:, 0, :]), ALU.subtract)
                dve.tensor_tensor(shifted[:, :, E], first[:, 1, :], first[:, 0, :], ALU.subtract)\
                    .then_inc(s["expd"], 1)

            def c_slots(g):
                dve.wait_ge(s["pos_mm"], g + 1)
                link(g, dve.tensor_tensor(pos[:, 0, :, :], bank[7][:, 64:64 + U * E].rearrange("p (u e) -> p u e", u=U),
                                          over_tiles(count[:, 0, :], E), ALU.add))
                link(g, dve.tensor_tensor(count[:, 1, :], count[:, 0, :], bank[7][:, 128:128 + E], ALU.add))
                link(g, dve.tensor_copy(count[:, 0, :], count[:, 1, :]))
                link(g, dve.tensor_scalar(kept[:, :, :], pos[:, 0, :, :], float(CAP), None, ALU.is_le))
                link(g, dve.tensor_tensor(pos[:, 1, :, :], pos[:, 0, :, :], over_tiles(eoff, E), ALU.add))
                for k in range(2):
                    dve.tensor_tensor(picked[:, k, :, :], sel[:, k, :, :], pos[:, 1, :, :], ALU.mult)
                    last = dve.tensor_tensor(picked[:, 2 + k, :, :], sel[:, k, :, :], kept[:, :, :], ALU.mult)
                link(g, last)
                link(g, dve.tensor_reduce(slot[:, 0:2, :, :], picked[:, :, :, :], X, ALU.add))
                link(g, dve.tensor_tensor(slot[:, 2, :, :], slot[:, 0, :, :], slot[:, 1, :, :], ALU.mult))
                link(g, dve.tensor_scalar(slot[:, 3, :, :], slot[:, 1, :, :], -float(4 * SLOTS), float(4 * SLOTS),
                                          ALU.mult, ALU.add))
                link(g, dve.tensor_tensor(slot[:, 4, :, :], slot[:, 2, :, :], slot[:, 3, :, :], ALU.add))
                dve.tensor_copy(scatter_idx[:, :, :], slot[:, 4, :, :]).then_inc(s["slots"], 1)
                dve.wait_ge(s["expd"], (g + 1) * 2)
                link(g, dve.tensor_reduce(esum[:, :], expd[:, :, 0:E], X, ALU.add))
                link(g, dve.reciprocal(gate[:, 0, :], esum[:, :]))
                link(g, dve.tensor_tensor(gate[:, 1, :], gate[:, 0, :], expd[:, :, E], ALU.mult))
                dve.tensor_tensor(of_group(gates_all, g), gate[:, :, :], slot[:, 1, :, :], ALU.mult)\
                    .then_inc(s["d_done"], 1)
                assert step[0] == route_steps, step

            def iteration(group):
                run(b_shift, group[2], 3)
                run(b_attention, group[2], 1)
                run(a_state, group[1], 1)
                run(a_stats2, group[1])
                run(a_norm2, group[1])
                run(b_attention, group[2], 2)
                run(a_x2, group[1])
                run(a_stats0, group[0])
                run(b_attention, group[2], 3)
                run(b_stats, group[1])
                run(a_norm0, group[0])
                run(b_norm, group[1])
                run(c_z2, group[2])
                run(c_xp, group[2])
                run(b_qk, group[1], 0)
                run(b_qk, group[1], 1)
                run(b_rope, group[1])
                run(b_values, group[1])
                run(a_v0, group[0])
                run(b_rope_sum, group[1])
                run(a_softmax, group[0])
                run(c_norm, group[2])
                run(b_keys, group[1], 0)
                run(c_select, group[2])
                run(a_rsum0, group[0])
                run(b_keys, group[1], 1)
                run(b_shift, group[1], 0)
                run(a_x1, group[0])
                run(a_norm1, group[0])
                run(b_shift, group[1], 1)
                run(c_slots, group[2])
                run(a_kv, group[0], 0)
                run(a_kv, group[0], 1)
                run(b_shift, group[1], 2)
                run(a_kv, group[0], 2)
                run(b_attention, group[1], 0)
                run(a_kv, group[0], 3)
                run(a_state, group[0], 0)

            pipeline(dve, iteration)

            with dve.Fori(0, E // 2) as i:
                for n in range(2):
                    wait_apart(dve, s[f"contributed{n}"], (i + 1) * (8 * 16))
                    dve.wait_ge((s["rows_in0"], s["rows_in1"])[n], (i + 1) * 16)
                    dve.tensor_copy(y_idx[n][:, :], rows[n][:, :, D]).then_inc(s["y_idx"], 1)
                    for c in range(2):
                        dve.wait_ge(s["tok_mm"], i * 4 + (2 * n + c + 1))
                        dve.tensor_copy(tokT[:, c, :], bank[c][:, :]).then_inc(s["tok"], 1)
                    for c in range(2):
                        dve.wait_ge(s["exp_mm"], i * 4 + (2 * n + c + 1))
                        dve.tensor_tensor(y_sb[n][:, 4 * c:4 * c + 4, :], per_tile(bank[6 + c]),
                                          b2[:, bass.ds(i * 2 + n, 1), :].broadcast_to([P, 4, D]), ALU.add)\
                            .then_inc(s["expert_out"], 1)
            dve.wait_ge(s["resid"], GROUPS + 1)
            for g in range(GROUPS):
                dve.wait_ge(s[f"joined{g}"], 16)
                for k in range(2):
                    for u in range(U):
                        if k == 1:
                            dve.wait_ge(s["partial"], g * U + u + 1)
                        dve.scalar_tensor_tensor(
                            out=resid[:, g, u, :], in0=joined[g][:, k, u, :], scalar=gates_all[:, g, k, u:u + 1],
                            in1=resid[:, g, u, :], op0=ALU.mult, op1=ALU.add)\
                            .then_inc(s["partial"] if k == 0 else s["result"], 1)

        @block.tensor
        def _(pe):
            pe.wait_ge(s["weights_in"], 16 * len(LOADS))
            for k in range(3):
                pe.matmul(bank[0][:, k * HD:(k + 1) * HD], xw_T[:, k, :], xw_h[:, k, :], start=True, stop=True)
            pe.wait_ge(s["prep_cast"], 9)
            pe.matmul(bank[1][:, 0:3 * D], bcols[:, 1, :], wqkv[:, :], start=True, stop=True)
            pe.matmul(bank[2][:, 0:D], bcols[:, 0, :], wo1[:, :], start=True, stop=True).then_inc(s["prep_mm"], 1)
            pe.wait_ge(s["prepared"], 1)
            pe.wait_ge(s["presets"], 6)

            def transposes(dst, src, sem, ready, counts):
                for u in range(U):
                    pe.wait_ge(ready, counts + u + 1)
                    mm = pe.transpose(dst[:, u * P:(u + 1) * P], src[:, u, :], ident)
                mm.then_inc(sem, 1)

            def a_context(g, n):
                pe.wait_ge(s["ctx_in"], (g + 1) * 16)
                wait_past(pe, s["x2"], g)
                for b in range(n * 4, n * 4 + 4):
                    mm = pe.transpose(bank[n][:, b % 4 * KEYS:(b % 4 + 1) * KEYS], ctx_sb[:, b, :], ident)
                mm.then_inc(s["ctxT_mm"], 1)

            def a_z0T(g):
                transposes(bank[2], z, s["z0T_mm"], s["z0"], g * U)

            def a_keys(g, n):
                pe.wait_ge(s["ctxT"], g * 2 + n + 1)
                pe.matmul(bank[n][0:HD, :], xw[:, 1, :], ctxT[:, n * 512:(n + 1) * 512], start=True,
                          stop=True).then_inc(s["k0_mm"], 1)

            def a_queries(g):
                pe.wait_ge(s["z0T"], g + 1)
                pe.matmul(bank[2][0:HD, :], xw[:, 0, :], zT[:, :], start=True, stop=True).then_inc(s["q0_mm"], 1)

            def a_v0(g):
                pe.wait_ge(s["k0"], g * 2 + 1)
                for b in range(GB):
                    mm = pe.matmul(bank[0][:, b * HD:(b + 1) * HD], ctxT[:, b * KEYS:(b + 1) * KEYS], xw[:, 2, :],
                                   start=True, stop=True)
                mm.then_inc(s["v0_mm"], 1)

            def a_scores(g):
                pe.wait_ge(s["q0"], g + 1)
                pe.wait_ge(s["k0"], (g + 1) * 2)
                for b in range(GB):
                    u, w = b // TB, b % TB
                    mm = pe.matmul(bank[1][w * S:(w + 1) * S, u * KEYS:(u + 1) * KEYS], q0T[:, b * S:(b + 1) * S],
                                   k0T[:, b * KEYS:(b + 1) * KEYS], start=True, stop=True)
                mm.then_inc(s["s0_mm"], 1)

            def a_p0T(g):
                transposes(bank[2], p0, s["p0T_mm"], s["p0"], g * U)

            def a_values(g):
                pe.wait_ge(s["p0T"], g + 1)
                pe.wait_ge(s["v0"], g + 1)
                for b in range(GB):
                    mm = pe.matmul(bank[0][0:HD, b * S:(b + 1) * S], v0[:, b, :], p0T[:, b * S:(b + 1) * S],
                                   start=True, stop=True)
                mm.then_inc(s["o0_mm"], 1)

            def a_y0(g):
                pe.wait_ge(s["o0"], g + 1)
                for u in range(U):
                    mm = pe.matmul(bank[1][:, u * D:(u + 1) * D], o0T[:, u * P:(u + 1) * P], wo_sum[:, :],
                                   start=True, stop=True)
                mm.then_inc(s["y0_mm"], 1)

            def a_z1T(g):
                transposes(bank[2], z, s["z1T_mm"], s["z1"], g * U)

            def a_kv(g, u):
                if u == 0:
                    pe.wait_ge(s["z1T"], g + 1)
                if u == U - 1:
                    pe.wait_ge(s["kv"], g * U + 1)
                pe.matmul(bank[KV_BANK[u]][:, :], zT[:, u * P:(u + 1) * P], wkv[:, :], start=True, stop=True)\
                    .then_inc(s["kv_mm"], 1)

            def a_q1(g):
                pe.wait_ge(s["kv"], g * U + 2)
                pe.matmul(bank[1][:, :], wq1[:, :], zT[:, :], start=True, stop=True).then_inc(s["q1_mm"], 1)

            def a_states(g, pair):
                if pair == 0:
                    pe.wait_ge(s["kv"], (g + 1) * U)
                else:
                    pe.wait_ge(s["q1"], g + 1)
                    pe.wait_ge(s["state"], g * 2 * TB + TB)
                for v in range(2):
                    u = 2 * pair + v
                    for k in range(2):
                        for b in range(TB):
                            at = slice(b * S, (b + 1) * S)
                            o = (2 * v + k) * D
                            mm = pe.matmul(bank[STATE_BANK[pair][b]][:, o:o + D],
                                           kv[at, u, 2 * k * D:(2 * k + 1) * D],
                                           kv[at, u, (2 * k + 1) * D:(2 * k + 2) * D], start=True, stop=True)
                mm.then_inc(s["state_mm"], 1)

            def a_read_states(g):
                for u in range(U):
                    for b in range(TB):
                        pe.wait_ge(s["state"], (g * 2 + u // 2) * TB + b + 1)
                        mm = pe.matmul(bank[2][b * S:(b + 1) * S, u * D:(u + 1) * D],
                                       q1T[:, u * P + b * S:u * P + (b + 1) * S], state[:, u // 2, b, u % 2, :],
                                       start=True, stop=True)
                mm.then_inc(s["o1_mm"], 1)

            def a_n1T(g):
                transposes(bank[1], z, s["n1T_mm"], s["n1"], g * U)

            def a_y1(g):
                pe.wait_ge(s["n1T"], g + 1)
                for u in range(U):
                    mm = pe.matmul(bank[0][:, u * D:(u + 1) * D], zT[:, u * P:(u + 1) * P], wo1_g[:, :],
                                   start=True, stop=True)
                mm.then_inc(s["y1_mm"], 1)

            def b_hT(g):
                wait_past(pe, s["attn"], g * (U * TB))
                transposes(bank[3], h, s["h_T_mm"], s["h"], g * U)

            def b_qk(g, n):
                pe.wait_ge(s["hT"], g + 1)
                for u in (2 * n, 2 * n + 1):
                    mm = pe.matmul(bank[4 + n][:, u % 2 * 2 * D:(u % 2 + 1) * 2 * D], hT[:, u * P:(u + 1) * P],
                                   wqkv_g[:, 0:2 * D], start=True, stop=True)
                mm.then_inc(s["qk_mm"], 1)

            def b_values(g):
                for b in range(GB):
                    for n in range(2):
                        mm = pe.matmul(bank[6][n * S:(n + 1) * S, b * 64:(b + 1) * 64], hT[:, b * S:(b + 1) * S],
                                       wqkv_g[:, 2 * D + n * 64:2 * D + (n + 1) * 64], start=True, stop=True)
                mm.then_inc(s["v_mm"], 1)

            def b_qkT(g):
                wait_apart(pe, s["qkr"], g + 1)
                pe.wait_ge(s["vx"], (g + 1) * 2)
                for u in range(U):
                    for c in range(2):
                        for n in range(2):
                            o = (c * 2 + n) * P
                            mm = pe.transpose(bank[3 + u][0:64, o:o + P],
                                              qkr[:, u, c * D + n * 64:c * D + (n + 1) * 64], ident)
                    mm.then_inc(s["qkT_mm"], 1)

            def b_scores(g, u):
                if u % 2 == 0:
                    pe.wait_ge(s["kx"], g * (2 * HH_DVE) + (u // 2 + 1) * HH_DVE)
                    pe.wait_ge(s["kx_act"], g * (2 * (HH - HH_DVE)) + (u // 2 + 1) * (HH - HH_DVE))
                if u == 0:
                    pe.wait_ge(s["qT"], (g + 1) * 2 * U)
                else:
                    pe.wait_ge(s["ssub"], g * U + u)
                for n in range(2):
                    pe.matmul(bank[3 + n][:, :], qblk[:, u, n, :],
                              kx[:, u, n, :, :].rearrange("p h k -> p (h k)"), start=True, stop=False)
                    mm = pe.matmul(bank[3 + n][:, :], ident_l, causal_l, start=False, stop=True)
                mm.then_inc(s["s_mm"], 1)

            def b_probs_T(g, u, n):
                pe.wait_ge(s["probs"], g * U + u + 1)
                wait_past(pe, s["pT"], (g * U + u) * 2 + n)
                for j in range(4 * n, 4 * n + 4):
                    mm = pe.transpose(bank[5][:, j % 4 * P:(j % 4 + 1) * P], probs[:, u % 2, j * P:(j + 1) * P], ident)
                mm.then_inc(s["pT_mm"], 1)

            def b_attend(g, u):
                pe.wait_ge(s["pT"], (g * U + u + 1) * 2)
                if u >= 1:
                    pe.wait_ge(s["attn"], (g * U + u) * TB)
                w = TB * 2 * VW
                for j in range(H // 2):
                    mm = pe.matmul(bank[6][:, j * w:(j + 1) * w], pT[:, u % 2, j, :],
                                   vx[:, TB * u:TB * u + TB, j, :, :].rearrange("p b h c -> p b (h c)"),
                                   start=True, stop=True)
                mm.then_inc(s["pv_mm"], 1)

            def c_attnT(g):
                wait_past(pe, s["d_done"], g + 1)
                for u in range(U):
                    pe.wait_ge(s["attn"], (g * U + u + 1) * TB)
                    mm = pe.transpose(bank[7][:, u * P:(u + 1) * P], attn[:, u, :], ident)
                mm.then_inc(s["attnT_mm"], 1)

            def c_project(g):
                pe.wait_ge(s["attnT"], g + 1)
                for u in range(U):
                    mm = pe.matmul(bank[7][:, u * D:(u + 1) * D], attnT[:, u * P:(u + 1) * P], wproj[:, :],
                                   start=True, stop=True)
                mm.then_inc(s["proj_mm"], 1)

            def c_h2T(g):
                pe.wait_ge(s["h2"], g + 1)
                for u in range(U):
                    mm = pe.transpose(bank[7][:, u * P:(u + 1) * P], h2[:, u, :], ident)
                mm.then_inc(s["h2T_mm"], 1)

            def c_logits(g):
                pe.wait_ge(s["h2T"], g + 1)
                for u in range(U):
                    mm = pe.matmul(bank[7][:, u * E:(u + 1) * E], h2T[:, u * P:(u + 1) * P], wgate[:, :],
                                   start=True, stop=True)
                mm.then_inc(s["logit_mm"], 1)

            def c_count(g):
                pe.wait_ge(s["selected"], g + 1)
                for v in range(U):
                    o = 64 + v * E
                    pe.matmul(bank[7][:, o:o + E], tri_l, sel_l[:, v, :], start=True, stop=(v == 0))
                    for u in range(v):
                        pe.matmul(bank[7][:, o:o + E], ones_l, sel_l[:, u, :], start=False, stop=(u == v - 1))
                for u in range(U):
                    mm = pe.matmul(bank[7][:, 128:128 + E], ones_l, sel_l[:, u, :], start=(u == 0),
                                   stop=(u == U - 1))
                mm.then_inc(s["pos_mm"], 1)

            def iteration(group):
                run(a_n1T, group[1])
                run(a_y1, group[1])
                run(b_attend, group[2], 3)
                run(a_context, group[0], 0)
                run(a_context, group[0], 1)
                run(c_attnT, group[2])
                run(a_keys, group[0], 0)
                run(a_keys, group[0], 1)
                run(a_z0T, group[0])
                run(b_hT, group[1])
                run(c_project, group[2])
                run(b_qk, group[1], 0)
                run(a_v0, group[0])
                run(b_qk, group[1], 1)
                run(a_queries, group[0])
                run(b_values, group[1])
                run(a_scores, group[0])
                run(b_qkT, group[1])
                run(c_h2T, group[2])
                run(c_logits, group[2])
                run(a_p0T, group[0])
                run(b_scores, group[1], 0)
                run(a_values, group[0])
                run(c_count, group[2])
                run(a_y0, group[0])
                run(b_scores, group[1], 1)
                run(a_z1T, group[0])
                run(b_probs_T, group[1], 0, 0)
                run(a_kv, group[0], 0)
                run(a_kv, group[0], 1)
                run(b_probs_T, group[1], 0, 1)
                run(b_scores, group[1], 2)
                run(b_attend, group[1], 0)
                run(a_kv, group[0], 2)
                run(a_kv, group[0], 3)
                run(b_probs_T, group[1], 1, 0)
                run(b_scores, group[1], 3)
                run(a_q1, group[0])
                run(b_probs_T, group[1], 1, 1)
                run(a_states, group[0], 0)
                run(b_probs_T, group[1], 2, 0)
                run(b_attend, group[1], 1)
                run(a_states, group[0], 1)
                run(b_probs_T, group[1], 2, 1)
                run(a_read_states, group[0])
                run(b_probs_T, group[1], 3, 0)
                run(b_attend, group[1], 2)
                run(b_probs_T, group[1], 3, 1)

            pipeline(pe, iteration)

            with pe.Fori(0, E // 2) as i:
                for n in range(2):
                    pe.wait_ge((s["w_in0"], s["w_in1"])[n], (i + 1) * 32)
                    pe.wait_ge((s["rows_in0"], s["rows_in1"])[n], (i + 1) * 16)
                    for c in range(2):
                        for r in range(4):
                            mm = pe.transpose(bank[c][:, r * P:(r + 1) * P], rows[n][:, 4 * c + r, 0:D], ident)
                        mm.then_inc(s["tok_mm"], 1)
                    for c in range(2):
                        pe.wait_ge(s["tok"], i * 4 + (2 * n + c + 1))
                        for f in range(FC):
                            if c == 1:
                                pe.wait_ge(s["hid"], i * (4 * FC) + (2 * FC * n + f + 1))
                            pe.matmul(bank[2 + f][:, :], w1_sb[n][:, f * P:(f + 1) * P], tokT[:, c, :], start=True,
                                      stop=True).then_inc(s["hid_mm"], 1)
                    for c in range(2):
                        pe.wait_ge(s["hid"], i * (4 * FC) + (2 * FC * n + (c + 1) * FC))
                        for r in range(4):
                            for f in range(FC):
                                mm = pe.matmul(bank[6 + c][:, r * D:(r + 1) * D], hid[:, c, f, r * P:(r + 1) * P],
                                               w2_sb[n][:, f, :], start=(f == 0), stop=(f == FC - 1))
                        mm.then_inc(s["exp_mm"], 1)


def constants():
    import numpy as np

    f = np.zeros((P, C_WIDTH), np.float32)
    p = np.arange(P)
    f[:, C_IDENT:C_IDENT + P] = np.eye(P)
    inv_freq = (1.0 / 10000.0 ** (np.arange(0, HD, 2, dtype=np.float32) / np.float32(HD))).astype(np.float32)
    ang = ((p % S).astype(np.float32)[:, None] * inv_freq).astype(np.float32)
    f[:, C_COS:C_COS + 4] = np.cos(ang)
    f[:, C_SIN:C_SIN + 4] = np.sin(ang)
    f[:, C_NSIN:C_NSIN + 4] = -np.sin(ang)
    f[:, C_BLOCK:C_BLOCK + D] = (p[:, None] // HD == np.arange(D)[None, :] // HD) * 2.0 ** -18
    f[:, C_HEAD:C_HEAD + HH] = (p[:, None] // HD) % HH == np.arange(HH)[None, :]
    f[:, C_RANK:C_RANK + E] = E - np.arange(E)
    f[:, C_EOFF:C_EOFF + E] = np.arange(E) * CAP - 1
    place = np.arange(2)[None, :, None] * TOKENS + p[:, None, None] * U + np.arange(U)[None, None, :] - P * U
    f[:, C_ROWID:C_ROWID + 2 * U] = place.reshape(P, 2 * U)
    b = np.zeros((P, L_WIDTH), np.float32)
    b[:, L_IDENT:L_IDENT + P] = np.eye(P)
    b[:, L_TRI:L_TRI + P] = p[:, None] <= p[None, :]
    b[:, L_ONES:L_ONES + P] = 1.0
    key = np.arange(HH * S) % S
    b[:, L_CAUSAL:] = np.where(key[None, :] <= (p % S)[:, None], 0.0, -(2.0 ** 32))
    return f, b


def kernel(**inputs):
    import numpy as np
    import concourse.bacc as bacc
    from concourse.bass_utils import run_bass_kernel_spmd

    a = {k: np.asarray(v) for k, v in inputs.items()}
    f, b = constants()
    qkv = a["L0_ffn_Wqkv"].reshape(D, H, 3, HD)
    awk, awv = a["L0_attn_Wk"], a["L0_attn_Wv"]
    abk, abv = a["L0_attn_bk"], a["L0_attn_bv"]
    arrays = {
        "x": a["x"],
        "ctx_1024": a["ctx_1024"],
        "mask": a["mask_SxS2_bk1"].view(np.uint8),
        "const_f32": f,
        "const_low": b,
        "xw_T": np.stack([a["L0_xattn_Wq"].T, a["L0_xattn_Wk"].T, a["L0_xattn_Wv"].T], 1),
        "xw_h": np.stack([a["L0_xattn_wq_h"], a["L0_xattn_wk_h"], a["L0_xattn_wv_h"]], 1),
        "xwo_heads": a["L0_xattn_Wo"].reshape(H, HD, D).transpose(1, 0, 2),
        "xb_qk": np.stack([a["L0_xattn_bq_h"], a["L0_xattn_bk_h"]], 1),
        "xb_v": a["L0_xattn_bv_h"],
        "awq": a["L0_attn_Wq"],
        "abq": a["L0_attn_bq"][:, None],
        "awkv": np.concatenate([awk[0], awv[0], awk[1], awv[1]], 1),
        "abkv": np.concatenate([abk[0], abv[0], abk[1], abv[1]]),
        "awo": a["L0_attn_Wo"],
        "abo": a["L0_attn_bo"],
        "cols": np.stack([a["L0_attn_ln_g"], a["L0_attn_ln_b"], a["L0_ffn_ln1_g"], a["L0_ffn_ln1_b"]], 1),
        "wqkv": np.concatenate([qkv[:, :, 0].reshape(D, D), qkv[:, :, 1].reshape(D, D),
                                qkv[:, 0::2, 2].reshape(D, D // 2), qkv[:, 1::2, 2].reshape(D, D // 2)], 1),
        "wproj": a["L0_ffn_Wproj"],
        "g2": a["L0_ffn_ln2_g"],
        "b2ln": a["L0_ffn_ln2_b"],
        "wgate": a["L0_ffn_Wgate"],
        "w1": a["L0_ffn_W1"],
        "b1c": a["L0_ffn_b1"].reshape(E, FC, P).transpose(2, 0, 1).reshape(P, E * FC),
        "w2": a["L0_ffn_W2"],
        "b2": a["L0_ffn_b2"],
    }
    arrays = {k: np.ascontiguousarray(v) for k, v in arrays.items()}
    nc = bacc.Bacc("TRN2", target_bir_lowering=False, num_devices=1)
    t = {
        n: nc.dram_tensor("in_" + n, list(v.shape), mybir.dt.from_np(v.dtype), kind="ExternalInput").ap()
        for n, v in arrays.items()}
    out = nc.dram_tensor("out", [B, S, D], F32, kind="ExternalOutput").ap()
    build_program(nc, t, out)
    r = run_bass_kernel_spmd(nc, [{"in_" + n: v for n, v in arrays.items()}], core_ids=[0])
    return r.results[0]["out"]
```

```python
from contextlib import ExitStack

import concourse.bass as bass
from concourse import mybir

ALU = mybir.AluOpType
ACT = mybir.ActivationFunctionType
F32 = mybir.dt.float32
BF16 = mybir.dt.bfloat16
U32 = mybir.dt.uint32
U8 = mybir.dt.uint8
X = mybir.AxisListType.X

P = 128
D = 128
B, S = 64, 64
KEYS = 128
H, HD = 16, 8
HH = H // 2
HH_DVE = 5
E, CAP = 8, 1024
FF = 512
FC = FF // P
U = 4
GROUPS = B * S // (U * P)
TB = 2
GB = U * TB
EPS = 1e-5
LN_STEPS = 2 * U + 1
SCALE = float(HD) ** -0.5
SLOTS = E * CAP
TOKENS = B * S
ZERO_STORES = 4
PRESETS = 11
ROW = D + 1
EMPTY = 65536.0
KV_BANK = (0, 1, 2, 0)
STATE_BANK = ((2, 0), (1, 0))
VW = HD + 1

C_IDENT = 0
C_COS = C_IDENT + P
C_SIN = C_COS + HD // 2
C_NSIN = C_SIN + HD // 2
C_BLOCK = C_NSIN + HD // 2
C_HEAD = C_BLOCK + D
C_RANK = C_HEAD + HH
C_EOFF = C_RANK + E
C_ROWID = C_EOFF + E
C_WIDTH = C_ROWID + 2 * U
L_IDENT = 0
L_TRI = L_IDENT + P
L_ONES = L_TRI + P
L_CAUSAL = L_ONES + P
L_WIDTH = L_CAUSAL + HH * S

WEIGHTS = (("xw_T", 3 * D), ("xw_h", 3 * HD), ("cols", 4), ("bq1", 1), ("wqkv", 3 * D), ("wo1", D),
           ("wq1", D), ("wkv", 4 * D), ("wproj", D), ("wgate", E), ("b1c", E * FC))
FIRST_WEIGHTS = sum(width for _, width in WEIGHTS[:6])
ROWS = (("bv_h", HD), ("bkv", 4 * D), ("bo1", D), ("g2", D), ("b2ln", D))


def build_program(nc, t, out):
    xs = nc.dram_tensor("expert_in", [SLOTS, ROW], F32, kind="Internal").ap()
    contributions = nc.dram_tensor("contributions", [2 * TOKENS, D], F32, kind="Internal").ap()
    contributions_of = contributions.rearrange("(k g p u) d -> g p k u d", k=2, g=GROUPS, p=P)
    x_groups = t["x"].rearrange("(g u w) s d -> g (w s) u d", u=U, w=TB)
    out_groups = out.rearrange("(g u w) s d -> g (w s) u d", u=U, w=TB)
    ctx_groups = t["ctx_1024"].rearrange("(g b) k d -> g k b d", b=GB)
    xs_rows = xs.rearrange("(e p r) d -> e p r d", e=E, p=P)
    w1_rows = t["w1"]
    w2_rows = t["w2"].rearrange("e (c p) d -> e p c d", p=P)

    with ExitStack() as ctx:
        def sb(name, shape, dt=F32):
            return ctx.enter_context(nc.sbuf_tensor(name, shape, dt))

        names = """const_in weights_in prep prep_mm prep_cast presets prepared x_in ctx_in
            ln0 z0 z0T_mm ctxT_mm z0T ctxT q0_mm k0_mm v0_mm q0 k0 v0 s0_mm s0_step nmax0 p0 p0T_mm p0T o0_mm o0 y0_mm
            rsum0 x1 ln1 z1 z1T_mm z1T q1_mm q1 kv_mm kv state_mm state_half state o1_mm ln2 n1 n1T_mm n1T y1_mm x1c x2
            ln3 h h_T_mm hT qk_mm qk v_mm vx rope_a rope_b qkr qkT_mm qT kT kx kx_act
            s_mm smax ssub probs pT_mm pT pv_mm rsum attn attnT_mm attnT proj_mm z2 xp ln4 h2n h2g h2 h2T_mm h2T
            logit_mm route shift expd selected pos_mm slots scattered resid saved d_done
            w_in0 w_in1 rows_in0 rows_in1 tok_mm tok hid_mm hid exp_mm expert_out expert_stored
            root0 root1 root2 root3 root4 prep_pool b2_in blank_done row_id h2_twin y_idx
            contributed0 contributed1 weighted partial result result_stored""".split()
        names += [f"joined{g}" for g in range(GROUPS)]
        s = {n: ctx.enter_context(nc.semaphore(n)) for n in names}

        cf = sb("const_f32", [P, C_WIDTH])
        cl = sb("const_bf16", [P, L_WIDTH], BF16)
        ident = cf[:, C_IDENT:C_IDENT + P]
        cos = cf[:, C_COS:C_COS + 4]
        sin = cf[:, C_SIN:C_SIN + 4]
        nsin = cf[:, C_NSIN:C_NSIN + 4]
        block_scale = cf[:, C_BLOCK:C_BLOCK + D]
        head_mask = cf[:, C_HEAD:C_HEAD + HH]
        rank = cf[:, C_RANK:C_RANK + E]
        eoff = cf[:, C_EOFF:C_EOFF + E]
        row_id0 = cf[:, C_ROWID:C_ROWID + 2 * U].rearrange("p (k u) -> p k u", k=2)
        ident_l = cl[:, L_IDENT:L_IDENT + P]
        tri_l = cl[:, L_TRI:L_TRI + P]
        ones_l = cl[:, L_ONES:L_ONES + P]
        causal_l = cl[:, L_CAUSAL:L_CAUSAL + HH * S]
        def parts(name, columns):
            whole = sb(name, [P, sum(width for _, width in columns)])
            found, at = {}, 0
            for part, width in columns:
                found[part] = whole[:, at:at + width]
                at += width
            return whole, found
        weights, w = parts("weights", WEIGHTS)
        row_params, r = parts("row_params", ROWS)
        xw_T = w["xw_T"].rearrange("p (c d) -> p c d", c=3)
        xw_h = w["xw_h"].rearrange("p (c d) -> p c d", c=3)
        cols = w["cols"]
        bq1, wqkv, wo1, wq1, wkv = w["bq1"], w["wqkv"], w["wo1"], w["wq1"], w["wkv"]
        wproj, wgate, b1c = w["wproj"], w["wgate"], w["b1c"]
        bv_h, bkv, bo1, g2, b2ln = r["bv_h"], r["bkv"], r["bo1"], r["g2"], r["b2ln"]
        by_head = sb("by_head", [HD, H * D + 2])
        wo_heads = by_head[:, 0:H * D].rearrange("p (h d) -> p h d", h=H)
        bqk_h = by_head[:, H * D:H * D + 2]
        xw = sb("xw", [P, 3, HD])
        wo_sum = sb("wo_sum", [P, D])
        mask_u8 = sb("mask_u8", [P, KEYS], U8)
        keep = sb("keep", [P, KEYS])
        fill = sb("fill", [P, KEYS])
        wo1_g = sb("wo1_g", [P, D])
        c1 = sb("c1", [P, D])
        bcols = sb("bcols", [P, 2, P])
        wqkv_g = sb("wqkv_g", [P, 3 * D])
        bqk = sb("bqk", [P, 2 * D])
        bv = sb("bv", [P, D // 2])
        b2 = sb("b2", [P, E, D])
        blank = sb("blank", [P, 8, ROW])

        x_sb = sb("x_sb", [P, U, D])
        ctx_sb = sb("ctx_sb", [P, GB, D])
        ln_parts = sb("ln_parts", [P, 5, U, 6])
        mv = sb("mv", [P, 5, U, 2])
        var_eps = sb("var_eps", [P, 6, U])
        rstd = sb("rstd", [P, 8, U])
        minus_half = sb("minus_half", [P, 2, U])
        z = sb("z", [P, U, D])
        zT = sb("zT", [P, U * P])
        ctxT = sb("ctxT", [P, GB * KEYS])
        q0T = sb("q0T", [P, U * P])
        k0T = sb("k0T", [P, GB * KEYS])
        v0 = sb("v0", [P, GB, HD])
        s0 = sb("s0", [P, U, KEYS])
        smax0 = sb("smax0", [P, U])
        nmax0 = sb("nmax0", [P, U])
        sum0 = sb("sum0", [P, U])
        rsum0 = sb("rsum0", [P, U])
        p0 = sb("p0", [P, U, KEYS])
        p0T = sb("p0T", [P, U * P])
        o0T = sb("o0T", [P, U * P])
        x1 = sb("x1", [P, U, D])
        x1c = sb("x1c", [P, U, D])
        q1T = sb("q1T", [P, U * P])
        k1 = sb("k1", [P, U, 2, D])
        v1 = sb("v1", [P, U, 2, TB, D])
        half_state = sb("half_state", [P, 2, 2, TB, D])
        state = sb("state", [P, 2, 2, TB, D])
        z2 = sb("z2", [P, U, D])
        h = sb("h", [P, U, D])
        hT = sb("hT", [P, U * P])
        qk = sb("qk", [P, U, 2 * D])
        rope_space = [sb(f"rope_space{n}", [P, 8, ROW]) for n in range(2)]
        rope_a, rope_b = [b[:, :, :].rearrange("p r d -> p (r d)")[:, 0:U * 2 * D]
                          .rearrange("p (u c) -> p u c", u=U) for b in rope_space]
        qkr = sb("qkr", [P, U, 2 * D])
        vx = sb("vx", [P, GB, H // 2, 2, VW])
        qblk = sb("qblk", [P, U, 2, P])
        kT = sb("kT", [P, U, 2, S])
        kx = sb("kx", [P, U, 2, HH, S])
        cl_f32 = kx[:, :, :, :, :].rearrange("p u c j k -> p (u c j k)")[:, 0:L_WIDTH]
        mxs = sb("mxs", [P, 2, H])
        probs = sb("probs", [P, 2, H * S])
        pT = sb("pT", [P, 2, H // 2, P])
        rsum = sb("rsum", [P, U, H])
        attn = sb("attn", [P, U, D])
        attnT = sb("attnT", [P, U * P])
        xp = sb("xp", [P, U, D])
        h2_rows = sb("h2_rows", [P, 2, U, ROW])
        h2 = h2_rows[:, 0, :, 0:D]
        row_id = h2_rows[:, :, :, D]
        h2T = sb("h2T", [P, U * P])
        lg = sb("lg", [P, 2, U, E])
        first = sb("first", [P, 2, U])
        tie = sb("tie", [P, 2, U, E])
        tie_max = sb("tie_max", [P, 2, U])
        sel = sb("sel", [P, 2, U, E])
        sel_l = sb("sel_l", [P, U, E], BF16)
        shifted = sb("shifted", [P, U, E + 1])
        expd = sb("expd", [P, U, E + 1])
        gate = sb("gate", [P, 2, U])
        esum = sb("esum", [P, U])
        count = sb("count", [P, 2, E])
        pos = sb("pos", [P, 2, U, E])
        kept = sb("kept", [P, U, E])
        picked = sb("picked", [P, 4, U, E])
        slot = sb("slot", [P, 6, 2, U])
        scatter_idx = sb("scatter_idx", [P, 2, U], U32)
        resid = sb("resid", [P, GROUPS, U, D])
        moments_all = sb("moments_all", [P, GROUPS, 2, U])
        gates_all = sb("gates_all", [P, GROUPS, 2, U])
        w1_sb = [sb(f"w1_sb{n}", [P, FF]) for n in range(2)]
        w2_sb = [sb(f"w2_sb{n}", [P, FC, D]) for n in range(2)]
        rows = rope_space
        tokT = sb("tokT", [P, 2, 512])
        hid = kx[:, :, :, :, :].rearrange("p (c v) h j k -> p c (v h) (j k)", c=2)
        y_sb = [v1[:, 2 * n:2 * n + 2, :, :, :].rearrange("p u k b d -> p (u k b) d") for n in range(2)]
        y_idx = [sb(f"y_idx{n}", [P, 8], U32) for n in range(2)]
        joined = [b[:, :, :].rearrange("p (k v) (r d) -> p k (v r) d", k=2, r=2) for b in (qk, qkr)]
        joined += [b[:, :, :].rearrange("p (k u) d -> p k u d", k=2) for b in (ctx_sb,)]
        joined += [ctxT[:, :].rearrange("p (k u d) -> p k u d", k=2, u=U)]
        joined += [b[:, :, :, :, :].rearrange("p k b u d -> p k (b u) d") for b in (half_state, state)]
        joined += [probs[:, n, :].rearrange("p (k u d) -> p k u d", k=2, u=U) for n in range(2)]

        bank = [ctx.enter_context(nc.psum_tensor(f"bank{n}", [P, 512], F32)) for n in range(8)]

        block = ctx.enter_context(nc.Block())

        def wait_apart(eng, sem, count):
            count = eng.compute_val(count)
            eng.wait_ge(s["weights_in"], 16 * len(LOADS))
            eng.wait_ge(sem, count)

        def wait_past(eng, sem, count):
            if not (isinstance(count, int) and count <= 0):
                eng.wait_ge(sem, count)

        def of_group(kept, g):
            return kept[:, bass.ds(g, 1), :, :].rearrange("p g a b -> p (g a) b")

        def pipeline(eng, iteration):
            lags = 4
            for t in range(lags - 1):
                iteration([t - lag if t >= lag else None for lag in range(lags)])
            with eng.Fori(0, GROUPS - (lags - 1)) as g:
                iteration([g + (lags - 1 - lag) for lag in range(lags)])
            for t in range(GROUPS, GROUPS + lags - 1):
                iteration([t - lag if t - lag < GROUPS else None for lag in range(lags)])

        def run(step, g, *more):
            if g is not None:
                step(g, *more)

        def over_tiles(ap, width):
            return ap.unsqueeze(1).broadcast_to([P, U, width])

        def per_tile(b):
            return b[:, :].rearrange("p (u n) -> p u n", u=U)

        LOADS = [(cf[:, :], t["const_f32"]),
                 (weights[:, 0:FIRST_WEIGHTS], t["weights"][:, 0:FIRST_WEIGHTS]),
                 (by_head[:, :], t["by_head"]), (row_params[:, :], t["row_params"].partition_broadcast(P)),
                 (weights[:, FIRST_WEIGHTS:], t["weights"][:, FIRST_WEIGHTS:]), (cl_f32, t["const_low"]),
                 (mask_u8[0:S, :], t["mask"]), (mask_u8[S:P, :], t["mask"])]

        @block.sync
        def _(sp):
            for dst, src in LOADS:
                sp.dma_start(dst, src).then_inc(s["weights_in"], 16)
            sp.dma_start(ctx_sb[:, :, :], ctx_groups[0]).then_inc(s["ctx_in"], 16)
            sp.dma_start(x_sb[:, :, :], x_groups[0]).then_inc(s["x_in"], 16)
            sp.dma_start(b2[:, :, :], t["b2"].partition_broadcast(P)).then_inc(s["b2_in"], 16)
            with sp.Fori(0, GROUPS - 1) as g:
                sp.wait_ge(s["ctxT_mm"], (g + 1) * 2)
                sp.dma_start(ctx_sb[:, :, :], ctx_groups[bass.ds(g + 1, 1)].rearrange("a k b d -> (a k) b d"))\
                    .then_inc(s["ctx_in"], 16)
                sp.wait_ge(s["x1"], (g + 1) * U)
                sp.dma_start(x_sb[:, :, :], x_groups[bass.ds(g + 1, 1)].rearrange("a k b d -> (a k) b d"))\
                    .then_inc(s["x_in"], 16)

            def load_rows(e, n):
                sp.dma_start(rows[n][:, :, :], xs_rows[bass.ds(e, 1)].rearrange("a p r d -> (a p) r d"))\
                    .then_inc((s["rows_in0"], s["rows_in1"])[n], 16)

            def load_weights(e, n):
                w_in = (s["w_in0"], s["w_in1"])[n]
                sp.dma_start(w1_sb[n][:, :], w1_rows[bass.ds(e, 1)].rearrange("a p f -> (a p) f"))\
                    .then_inc(w_in, 16)
                sp.dma_start(w2_sb[n][:, :, :], w2_rows[bass.ds(e, 1)].rearrange("a p c d -> (a p) c d"))\
                    .then_inc(w_in, 16)

            for n in range(2):
                load_weights(n, n)
            sp.wait_ge(s["scattered"], (GROUPS * U * 2 + ZERO_STORES) * 16)
            for n in range(2):
                load_rows(n, n)
            with sp.Fori(0, E // 2 - 1) as i:
                for n in range(2):
                    sp.wait_ge(s["tok_mm"], i * 4 + (2 * n + 2))
                    sp.wait_ge(s["y_idx"], i * 2 + (n + 1))
                    load_rows(i * 2 + (n + 2), n)
                    sp.wait_ge(s["exp_mm"], i * 4 + (2 * n + 2))
                    load_weights(i * 2 + (n + 2), n)
            for n in range(2):
                sp.wait_ge(s[f"contributed{n}"], (GROUPS + SLOTS // P // 2) * 16)
            for g in range(GROUPS):
                sp.dma_start(joined[g], contributions_of[g]).then_inc(s[f"joined{g}"], 16)
            with sp.Fori(0, GROUPS) as g:
                sp.wait_ge(s["result"], g + 1)
                sp.dma_start(out_groups[bass.ds(g, 1)].rearrange("a p u d -> (a p) u d"),
                             resid[:, bass.ds(g, 1), :, :].rearrange("p a u d -> p (a u) d"))\
                    .then_inc(s["result_stored"], 16)
            sp.wait_ge(s["result_stored"], GROUPS * 16)

        @block.gpsimd
        def _(pool):
            pool.memset(blank[:, :, :], 0.0).then_inc(s["blank_done"], 1)
            pool.wait_ge(s["blank_done"], 1)
            pool.memset(blank[:, :, D:ROW], EMPTY).then_inc(s["blank_done"], 1)
            for padded in (wo_sum, q0T, k0T, o0T):
                pool.memset(padded[:, :], 0.0).then_inc(s["presets"], 1)
            pool.memset(qblk[:, :, :, :], 0.0).then_inc(s["presets"], 1)
            pool.memset(v1[:, :, :, :, :], 0.0).then_inc(s["presets"], 1)
            pool.memset(vx[:, :, :, :, :], 0.0).then_inc(s["presets"], 1)
            pool.memset(count[:, :, :], 0.0).then_inc(s["presets"], 1)
            pool.memset(xp[:, :, :], 0.0).then_inc(s["resid"], 1)
            pool.memset(minus_half[:, :, :], -0.5).then_inc(s["presets"], 1)
            pool.wait_ge(s["presets"], 9)
            pool.memset(vx[0:S, :, :, 0, HD:VW], 1.0).then_inc(s["presets"], 1)
            pool.memset(vx[S:P, :, :, 1, HD:VW], 1.0).then_inc(s["presets"], 1)
            pool.wait_ge(s["presets"], PRESETS)
            pool.wait_ge(s["weights_in"], 16 * len(LOADS))
            pool.tensor_tensor(wq1[:, :], wq1[:, :], ident, ALU.add).then_inc(s["prep_pool"], 1)
            wkv_parts = wkv.rearrange("p (k d) -> p k d", k=4)
            pool.tensor_tensor(wkv_parts, wkv_parts, ident.unsqueeze(1).broadcast_to([P, 4, D]), ALU.add)\
                .then_inc(s["prep_pool"], 1)
            pool.wait_ge(s["blank_done"], 2)
            for n in range(ZERO_STORES):
                pool.dma_start(xs.rearrange("(n p a r) d -> n p a r d", n=ZERO_STORES, p=P, r=8)[n],
                               blank[:, :, :].unsqueeze(1).broadcast_to([P, SLOTS // (ZERO_STORES * P * 8), 8, ROW]))\
                    .then_inc(s["scattered"], 16)
            pool.wait_ge(s["prepared"], 1)

            def root(g, ln, steps, first, many, done):
                pool.wait_ge(ln, (g + 1) * steps)
                pool.tensor_tensor(rstd[:, first:first + many, :], var_eps[:, first:first + many, :],
                                   minus_half[:, 0:many, :], ALU.pow).then_inc(done, 1)

            def a_offset(g):
                pool.wait_ge(s["x1"], (g + 1) * U)
                pool.tensor_tensor(x1c[:, :, :], x1[:, :, :], over_tiles(c1[:, :], D), ALU.add)\
                    .then_inc(s["x1c"], 1)

            def b_rope(g):
                pool.wait_ge(s["qk"], (g + 1) * 2)
                halves = qk[:, :, :].rearrange("p u (c k f) -> p (u c) k f", k=2, f=4)
                crossed = rope_b[:, :, :].rearrange("p u (c k f) -> p (u c) k f", k=2, f=4)
                for k, table in ((0, nsin), (1, sin)):
                    pool.tensor_tensor(crossed[:, :, k, :], halves[:, :, 1 - k, :],
                                       table.unsqueeze(1).broadcast_to([P, U * 2 * H, 4]), ALU.mult)\
                        .then_inc(s["rope_b"], 1)

            def c_norm(g):
                pool.wait_ge(s["h2n"], (g + 1) * U)
                pool.tensor_tensor(h2, h2, over_tiles(g2[:, :], D), ALU.mult).then_inc(s["h2g"], 1)
                pool.wait_ge(s["h2g"], g + 1)
                pool.tensor_tensor(h2, h2, over_tiles(b2ln[:, :], D), ALU.add).then_inc(s["h2"], 1)

            def c_blank(g):
                for k in range(2):
                    pool.dma_start(contributions_of[bass.ds(g, 1)].rearrange("a p k u d -> (a p) k u d")[:, k],
                                   blank[:, 0:U, 0:D]).then_inc(s[f"contributed{k}"], 16)

            def c_residual(g):
                pool.wait_ge(s["xp"], g + 1)
                pool.tensor_tensor(of_group(resid, g), of_group(resid, g), xp[:, :, :], ALU.add)\
                    .then_inc(s["resid"], 1)

            def c_scatter(g, k):
                if k == 0:
                    wait_apart(pool, s["slots"], g + 1)
                    pool.wait_ge(s["h2"], g + 1)
                    pool.wait_ge(s["row_id"], g + 2)
                else:
                    wait_apart(pool, s["h2_twin"], g + 1)
                for u in range(U):
                    pool.indirect_dma_start(
                        xs, bass.IndirectOffsetOnAxis(scatter_idx[:, k, u:u + 1], 0), h2_rows[:, k, u, :], None,
                        bounds_check=SLOTS - 1, oob_is_err=False).then_inc(s["scattered"], 16)

            def iteration(group):
                run(root, group[2], s["ln3"], LN_STEPS + 1, 3, 2, s["root3"])
                run(b_rope, group[2])
                run(root, group[3], s["ln4"], LN_STEPS, 5, 1, s["root4"])
                run(c_norm, group[3])
                run(c_blank, group[3])
                run(root, group[1], s["ln1"], LN_STEPS, 1, 1, s["root1"])
                run(c_residual, group[3])
                run(c_scatter, group[3], 0)
                run(c_scatter, group[3], 1)
                run(a_offset, group[1])
                run(root, group[1], s["ln2"], LN_STEPS, 2, 1, s["root2"])
                run(root, group[0], s["ln0"], LN_STEPS, 0, 1, s["root0"])

            pipeline(pool, iteration)

            for n in range(2):
                pool.wait_ge(s[f"contributed{n}"], GROUPS * 16)
            with pool.Fori(0, E // 2) as i:
                for n in range(2):
                    wait_apart(pool, s["y_idx"], i * 2 + (n + 1))
                    for c in range(2):
                        wait_apart(pool, s["expert_out"], i * 4 + (2 * n + c + 1))
                        for r in range(4 * c, 4 * c + 4):
                            pool.indirect_dma_start(
                                contributions, bass.IndirectOffsetOnAxis(y_idx[n][:, r:r + 1], 0), y_sb[n][:, r, :],
                                None, bounds_check=2 * TOKENS - 1, oob_is_err=False)\
                                .then_inc(s[f"contributed{n}"], 16)

        @block.scalar
        def _(act):
            act.wait_ge(s["weights_in"], 16 * len(LOADS))
            act.wait_ge(s["prepared"], 1)
            act.wait_ge(s["presets"], PRESETS)
            def a_context(g, n):
                act.wait_ge(s["ctxT_mm"], g * 2 + n + 1)
                act.activation(ctxT[:, n * 512:(n + 1) * 512], bank[n][:, :], ACT.Copy).then_inc(s["ctxT"], 1)

            def a_z0T(g):
                act.wait_ge(s["z0T_mm"], g + 1)
                act.activation(zT[:, :], bank[2][:, :], ACT.Copy).then_inc(s["z0T"], 1)

            def a_keys(g, n):
                act.wait_ge(s["k0_mm"], g * 2 + n + 1)
                act.activation(k0T[0:HD, n * 512:(n + 1) * 512], bank[n][0:HD, :], ACT.Identity,
                               bias=bqk_h[:, 1:2]).then_inc(s["k0"], 1)

            def a_queries(g):
                act.wait_ge(s["q0_mm"], g + 1)
                act.activation(q0T[0:HD, :], bank[2][0:HD, :], ACT.Identity, bias=bqk_h[:, 0:1]).then_inc(s["q0"], 1)

            def a_softmax(g):
                act.wait_ge(s["nmax0"], g + 1)
                for u in range(U):
                    act.activation(p0[:, u, :], s0[:, u, :], ACT.Exp, bias=nmax0[:, u:u + 1], scale=SCALE,
                                   accum_out=sum0[:, u:u + 1]).then_inc(s["p0"], 1)

            def a_p0T(g):
                act.wait_ge(s["p0T_mm"], g + 1)
                act.activation(p0T[:, :], bank[2][:, :], ACT.Copy).then_inc(s["p0T"], 1)

            def a_values(g):
                act.wait_ge(s["o0_mm"], g + 1)
                act.activation(o0T[0:HD, :], bank[0][0:HD, :], ACT.Copy).then_inc(s["o0"], 1)

            def a_z1T(g):
                act.wait_ge(s["z1T_mm"], g + 1)
                act.activation(zT[:, :], bank[2][:, :], ACT.Copy).then_inc(s["z1T"], 1)

            def a_q1(g):
                act.wait_ge(s["q1_mm"], g + 1)
                act.activation(q1T[:, :], bank[1][:, :], ACT.Identity, bias=bq1[:, 0:1]).then_inc(s["q1"], 1)

            def a_n1T(g):
                act.wait_ge(s["n1T_mm"], g + 1)
                act.activation(zT[:, :], bank[1][:, :], ACT.Copy).then_inc(s["n1T"], 1)

            def b_hT(g):
                act.wait_ge(s["h_T_mm"], g + 1)
                act.activation(hT[:, :], bank[3][:, :], ACT.Copy).then_inc(s["hT"], 1)

            def b_qkT(g):
                act.wait_ge(s["qkT_mm"], (g + 1) * U)
                for n in range(2):
                    for u in range(U):
                        src = bank[3 + u][0:HH * HD, :].rearrange("p (c h b t) -> p c h b t", c=2, h=2, b=TB)
                        act.activation(kT[n * 64:(n + 1) * 64, u, :, :], src[:, 1, :, n, :], ACT.Copy)\
                            .then_inc(s["kT"] if u == U - 1 else s["shift"], 1)
                for n in range(2):
                    for u in range(U):
                        src = bank[3 + u][0:HH * HD, :].rearrange("p (c h b t) -> p c h b t", c=2, h=2, b=TB)
                        act.activation(qblk[n * 64:(n + 1) * 64, u, :, n * S:(n + 1) * S], src[:, 0, :, n, :],
                                       ACT.Copy).then_inc(s["qT"], 1)

            def b_keys(g, n):
                act.wait_ge(s["kT"], (g + 1) * 2)
                for j in range(HH_DVE, HH):
                    act.activation(kx[:, 2 * n:2 * n + 2, :, j, :], kT[:, 2 * n:2 * n + 2, :, :], ACT.Copy,
                                   scale=head_mask[:, j:j + 1]).then_inc(s["kx_act"], 1)

            def b_exp(g, u):
                act.wait_ge(s["ssub"], g * U + u + 1)
                act.activation(probs[:, u % 2, :], probs[:, u % 2, :], ACT.Exp, scale=SCALE)\
                    .then_inc(s["probs"], 1)

            def b_probs_T(g, u, n):
                act.wait_ge(s["pT_mm"], (g * U + u) * 2 + n + 1)
                act.activation(pT[:, u % 2, 4 * n:4 * n + 4, :],
                               bank[5][:, :].rearrange("p (j t) -> p j t", j=4), ACT.Copy).then_inc(s["pT"], 1)

            def c_attnT(g):
                act.wait_ge(s["attnT_mm"], g + 1)
                act.activation(attnT[:, :], bank[7][:, :], ACT.Copy).then_inc(s["attnT"], 1)

            def c_h2T(g):
                act.wait_ge(s["h2T_mm"], g + 1)
                act.activation(h2T[:, :], bank[7][:, :], ACT.Copy).then_inc(s["h2T"], 1)

            def c_twin(g):
                act.wait_ge(s["h2"], g + 1)
                act.activation(h2_rows[:, 1, :, 0:D], h2, ACT.Copy).then_inc(s["h2_twin"], 1)

            def c_gates(g):
                act.wait_ge(s["expd"], g * 2 + 1)
                act.activation(expd[:, :, :], shifted[:, :, :], ACT.Exp).then_inc(s["expd"], 1)

            def iteration(group):
                run(a_n1T, group[1])
                run(a_context, group[0], 0)
                run(a_context, group[0], 1)
                run(c_attnT, group[2])
                run(b_hT, group[1])
                run(a_keys, group[0], 0)
                run(a_keys, group[0], 1)
                run(a_z0T, group[0])
                run(a_queries, group[0])
                run(b_qkT, group[1])
                run(a_softmax, group[0])
                run(c_h2T, group[2])
                run(c_twin, group[2])
                run(b_keys, group[1], 0)
                run(a_p0T, group[0])
                run(a_values, group[0])
                run(b_keys, group[1], 1)
                run(b_exp, group[1], 0)
                run(a_z1T, group[0])
                run(b_probs_T, group[1], 0, 0)
                run(b_exp, group[1], 1)
                run(c_gates, group[2])
                run(b_probs_T, group[1], 0, 1)
                run(b_probs_T, group[1], 1, 0)
                run(b_exp, group[1], 2)
                run(b_probs_T, group[1], 1, 1)
                run(b_probs_T, group[1], 2, 0)
                run(a_q1, group[0])
                run(b_exp, group[1], 3)
                run(b_probs_T, group[1], 2, 1)
                run(b_probs_T, group[1], 3, 0)
                run(b_probs_T, group[1], 3, 1)

            pipeline(act, iteration)
            with act.Fori(0, E // 2) as i:
                for n in range(2):
                    for c in range(2):
                        for f in range(FC):
                            wait_apart(act, s["hid_mm"], i * (4 * FC) + (2 * FC * n + c * FC + f + 1))
                            act.activation(hid[:, c, f, :], bank[2 + f][:, :], ACT.Gelu,
                                           bias=b1c[:, bass.ds(i * (2 * FC) + (n * FC + f), 1)])\
                                .then_inc(s["hid"], 1)
            act.wait_ge(s["d_done"], GROUPS + 1)
            for g in range(GROUPS):
                act.wait_ge(s[f"joined{g}"], 16)
                for u in range(U):
                    act.activation(joined[g][:, 1, u, :], joined[g][:, 1, u, :], ACT.Copy,
                                   scale=gates_all[:, g, 1, u:u + 1]).then_inc(s["weighted"], 1)

        @block.vector
        def _(dve):
            dve.wait_ge(s["weights_in"], 16 * len(LOADS))
            for n in range(2):
                dve.tensor_scalar(bcols[:, n, :], ident, 0.0, cols[:, 2 * n + 1:2 * n + 2], ALU.mult, ALU.add)\
                    .then_inc(s["prep_cast"], 1)
            dve.tensor_copy(cl[:, :], cl_f32).then_inc(s["prep_cast"], 1)
            dve.tensor_copy(fill[:, :], mask_u8[:, :]).then_inc(s["prep_cast"], 1)
            dve.wait_ge(s["prep_cast"], 4)
            dve.tensor_scalar(keep[:, :], fill[:, :], -1.0, 1.0, ALU.mult, ALU.add).then_inc(s["prep_cast"], 1)
            dve.wait_ge(s["prep_cast"], 5)
            dve.tensor_scalar(fill[:, :], fill[:, :], -1e9 / SCALE, None, ALU.mult).then_inc(s["prep"], 1)
            dve.tensor_scalar(wo1_g[:, :], wo1[:, :], cols[:, 0:1], None, ALU.mult).then_inc(s["prep"], 1)
            dve.tensor_scalar(wqkv_g[:, :], wqkv[:, :], cols[:, 2:3], None, ALU.mult).then_inc(s["prep"], 1)
            dve.wait_ge(s["presets"], PRESETS)
            dve.tensor_reduce(wo_sum[0:HD, :], wo_heads[:, :, :].rearrange("p h d -> p d h"), X, ALU.add)\
                .then_inc(s["prep"], 1)
            dve.wait_ge(s["prep_mm"], 1)
            dve.tensor_copy(xw[:, :, :], bank[0][:, 0:3 * HD].rearrange("p (c d) -> p c d", c=3))\
                .then_inc(s["prep"], 1)
            dve.tensor_copy(bqk[:, :], bank[1][:, 0:2 * D]).then_inc(s["prep"], 1)
            dve.tensor_copy(bv[0:S, :], bank[1][0:S, 2 * D:2 * D + D // 2]).then_inc(s["prep_cast"], 1)
            dve.tensor_copy(bv[S:P, :], bank[1][S:P, 2 * D + D // 2:3 * D]).then_inc(s["prep"], 1)
            dve.wait_ge(s["prep_cast"], 6)
            dve.tensor_tensor(c1[:, :], bank[2][:, 0:D], bo1[:, :], ALU.add).then_inc(s["prep"], 1)
            dve.wait_ge(s["prep"], 8)
            dve.memset(smax0[:, :], 0.0).then_inc(s["d_done"], 1)
            dve.memset(rsum0[:, :], 0.0).then_inc(s["prepared"], 1)
            dve.tensor_copy(row_id, row_id0).then_inc(s["row_id"], 1)
            dve.wait_ge(s["presets"], PRESETS)

            def stats(g, n, sem, src, steps=LN_STEPS):
                at = 5 if n == 4 else n
                for u in range(U):
                    dve.bn_stats(ln_parts[:, n, u, :], src(u)).then_inc(sem, 1)
                wait_apart(dve, sem, g * steps + U)
                for u in range(U):
                    dve.bn_aggr(mv[:, n, u, :], ln_parts[:, n, u, :]).then_inc(sem, 1)
                dve.wait_ge(sem, g * steps + 2 * U)
                dve.tensor_scalar(var_eps[:, at, :], mv[:, n, :, 1], EPS, None, ALU.add).then_inc(sem, 1)

            def normalise(dst, n, k, src, sem):
                for u in range(U):
                    dve.tensor_scalar(dst[:, u, :], src(u), mv[:, n, u, 0:1], rstd[:, k, u:u + 1],
                                      ALU.subtract, ALU.mult).then_inc(sem, 1)

            def x2_tile(g, u):
                return resid[:, bass.ds(g, 1), u, :].rearrange("p a d -> p (a d)")

            def a_stats0(g):
                dve.wait_ge(s["x_in"], (g + 1) * 16)
                stats(g, 0, s["ln0"], lambda u: x_sb[:, u, :])

            def a_norm0(g):
                dve.wait_ge(s["root0"], g + 1)
                normalise(z, 0, 0, lambda u: x_sb[:, u, :], s["z0"])

            def a_v0(g):
                dve.wait_ge(s["v0_mm"], g + 1)
                dve.tensor_tensor(v0[:, :, :], bank[0][:, 0:GB * HD].rearrange("p (b d) -> p b d", b=GB),
                                  bv_h[:, :].unsqueeze(1).broadcast_to([P, GB, HD]), ALU.add).then_inc(s["v0"], 1)

            def a_softmax(g):
                dve.wait_ge(s["s0_mm"], g + 1)
                dve.tensor_tensor(s0[:, :, :], per_tile(bank[1]), over_tiles(keep[:, :], KEYS), ALU.mult)\
                    .then_inc(s["s0_step"], 1)
                dve.wait_ge(s["s0_step"], g * 3 + 1)
                dve.tensor_tensor(s0[:, :, :], s0[:, :, :], over_tiles(fill[:, :], KEYS), ALU.add)\
                    .then_inc(s["s0_step"], 1)
                dve.wait_ge(s["s0_step"], g * 3 + 2)
                dve.tensor_reduce(smax0[:, :], s0[:, :, :], X, ALU.max).then_inc(s["s0_step"], 1)
                dve.wait_ge(s["s0_step"], g * 3 + 3)
                dve.tensor_scalar(nmax0[:, :], smax0[:, :], -SCALE, None, ALU.mult).then_inc(s["nmax0"], 1)

            def a_rsum0(g):
                dve.wait_ge(s["p0"], (g + 1) * U)
                dve.reciprocal(rsum0[:, :], sum0[:, :]).then_inc(s["rsum0"], 1)

            def a_x1(g):
                dve.wait_ge(s["rsum0"], g + 1)
                dve.wait_ge(s["y0_mm"], g + 1)
                for u in range(U):
                    dve.scalar_tensor_tensor(out=x1[:, u, :], in0=bank[1][:, u * D:(u + 1) * D],
                                             scalar=rsum0[:, u:u + 1], in1=x_sb[:, u, :], op0=ALU.mult,
                                             op1=ALU.add).then_inc(s["x1"], 1)
                dve.wait_ge(s["x1"], (g + 1) * U)
                stats(g, 1, s["ln1"], lambda u: x1[:, u, :])

            def a_norm1(g):
                dve.wait_ge(s["root1"], g + 1)
                normalise(z, 1, 1, lambda u: x1[:, u, :], s["z1"])

            def a_kv(g, u):
                dve.wait_ge(s["kv_mm"], g * U + u + 1)
                kv, bias = [ap[:, :].rearrange("p (k c e) -> p k c e", k=2, c=2) for ap in (bank[KV_BANK[u]], bkv)]
                dve.tensor_tensor(k1[:, u, :, :], kv[:, :, 0, :], bias[:, :, 0, :], ALU.add)
                for b in range(TB):
                    at = slice(b * S, (b + 1) * S)
                    ins = dve.tensor_tensor(v1[at, u, :, b, :], kv[at, :, 1, :], bias[at, :, 1, :], ALU.add)
                ins.then_inc(s["kv"], 1)

            def a_state(g, pair):
                dve.wait_ge(s["state_mm"], g * 2 + pair + 1)
                def products(v):
                    return bank[STATE_BANK[pair][v]][:, :].rearrange("p (k b e) -> p k b e", k=2, b=TB)
                for v in range(2):
                    dve.tensor_tensor(half_state[:, pair, v, :, :], products(v)[:, 0, :, :],
                                      block_scale.unsqueeze(1).broadcast_to([P, TB, D]), ALU.mult)\
                        .then_inc(s["state_half"], 1)
                for v in range(2):
                    dve.wait_ge(s["state_half"], g * U + 2 * pair + v + 1)
                    dve.tensor_tensor(state[:, pair, v, :, :], half_state[:, pair, v, :, :],
                                      products(v)[:, 1, :, :], ALU.mult).then_inc(s["state"], 1)

            def a_stats2(g):
                dve.wait_ge(s["o1_mm"], g + 1)
                stats(g, 2, s["ln2"], lambda u: bank[2][:, u * D:(u + 1) * D])

            def a_norm2(g):
                dve.wait_ge(s["root2"], g + 1)
                normalise(z, 2, 2, lambda u: bank[2][:, u * D:(u + 1) * D], s["n1"])

            def a_x2(g):
                dve.wait_ge(s["y1_mm"], g + 1)
                dve.wait_ge(s["x1c"], g + 1)
                dve.tensor_tensor(of_group(resid, g), per_tile(bank[0]), x1c[:, :, :], ALU.add)\
                    .then_inc(s["x2"], 1)

            def b_stats(g):
                wait_apart(dve, s["x2"], g + 1)
                stats(g, 3, s["ln3"], lambda u: x2_tile(g, u), LN_STEPS + 1)
                dve.wait_ge(s["ln3"], g * (LN_STEPS + 1) + LN_STEPS)
                dve.scalar_tensor_tensor(out=var_eps[:, 4, :], in0=var_eps[:, 3, :], scalar=EPS,
                                         in1=mv[:, 3, :, 1], op0=ALU.mult, op1=ALU.add).then_inc(s["ln3"], 1)

            def b_norm(g):
                dve.wait_ge(s["root3"], g + 1)
                normalise(h, 3, 4, lambda u: x2_tile(g, u), s["h"])
                dve.tensor_copy(of_group(moments_all, g)[:, 0, :], mv[:, 3, :, 0])
                dve.tensor_copy(of_group(moments_all, g)[:, 1, :], rstd[:, 3, :]).then_inc(s["saved"], 1)

            def b_qk(g, n):
                dve.wait_ge(s["qk_mm"], g * 2 + n + 1)
                dve.tensor_tensor(qk[:, 2 * n:2 * n + 2, :], bank[4 + n][:, :].rearrange("p (u c) -> p u c", u=2),
                                  bqk[:, :].unsqueeze(1).broadcast_to([P, 2, 2 * D]), ALU.add).then_inc(s["qk"], 1)

            def b_values(g):
                dve.wait_ge(s["v_mm"], g + 1)
                for n in range(2):
                    at = slice(n * S, (n + 1) * S)
                    dve.tensor_tensor(vx[at, :, :, n, 0:HD],
                                      bank[6][at, :].rearrange("p (b j d) -> p b j d", b=GB, d=HD),
                                      bv[at, :].rearrange("p (j d) -> p j d", d=HD).unsqueeze(1)
                                      .broadcast_to([S, GB, H // 2, HD]), ALU.add).then_inc(s["vx"], 1)

            def b_rope(g):
                dve.wait_ge(s["qk"], (g + 1) * 2)
                dve.tensor_tensor(rope_a[:, :, :].rearrange("p u (c f) -> p (u c) f", f=4),
                                  qk[:, :, :].rearrange("p u (c f) -> p (u c) f", f=4),
                                  cos.unsqueeze(1).broadcast_to([P, U * 4 * H, 4]), ALU.mult)\
                    .then_inc(s["rope_a"], 1)

            def b_rope_sum(g):
                dve.wait_ge(s["rope_a"], g + 1)
                dve.wait_ge(s["rope_b"], (g + 1) * 2)
                dve.tensor_tensor(qkr[:, :, :], rope_a[:, :, :], rope_b[:, :, :], ALU.add).then_inc(s["qkr"], 1)

            def b_keys(g, n):
                dve.wait_ge(s["kT"], (g + 1) * 2)
                for j in range(HH_DVE):
                    dve.tensor_scalar(kx[:, 2 * n:2 * n + 2, :, j, :], kT[:, 2 * n:2 * n + 2, :, :],
                                      head_mask[:, j:j + 1], None, ALU.mult).then_inc(s["kx"], 1)

            def b_shift(g, u):
                dve.wait_ge(s["s_mm"], g * U + u + 1)
                for n in range(2):
                    dve.tensor_reduce(mxs[:, u % 2, n * HH:(n + 1) * HH],
                                      bank[3 + n][:, :].rearrange("p (h k) -> p h k", h=HH), X, ALU.max)\
                        .then_inc(s["smax"], 1)
                dve.wait_ge(s["smax"], (g * U + u + 1) * 2)
                if u >= 2:
                    dve.wait_ge(s["pT_mm"], (g * U + u - 1) * 2)
                for n in range(2):
                    ins = dve.tensor_tensor(
                        probs[:, u % 2, n * 512:(n + 1) * 512].rearrange("p (h k) -> p h k", h=HH),
                        bank[3 + n][:, :].rearrange("p (h k) -> p h k", h=HH),
                        mxs[:, u % 2, n * HH:(n + 1) * HH].unsqueeze(2).broadcast_to([P, HH, S]), ALU.subtract)
                ins.then_inc(s["ssub"], 1)

            def b_attention(g, u):
                dve.wait_ge(s["pv_mm"], g * U + u + 1)
                if u == 0:
                    wait_past(dve, s["attnT_mm"], g)
                pv = bank[6][:, 0:H // 2 * TB * 2 * VW].rearrange("p (j b h c) -> p j b h c", b=TB, h=2, c=VW)
                for b in range(TB):
                    at = slice(b * S, (b + 1) * S)
                    dve.reciprocal(rsum[at, u, :].rearrange("p (j h) -> p j h", h=2), pv[at, :, b, :, HD])\
                        .then_inc(s["rsum"], 1)
                for b in range(TB):
                    at = slice(b * S, (b + 1) * S)
                    dve.wait_ge(s["rsum"], (g * U + u) * TB + b + 1)
                    dve.tensor_tensor(
                        attn[at, u, :].rearrange("p (j h c) -> p j h c", h=2, c=HD), pv[at, :, b, :, 0:HD],
                        rsum[at, u, :].rearrange("p (j h) -> p j h", h=2).unsqueeze(3)
                        .broadcast_to([S, H // 2, 2, HD]), ALU.mult).then_inc(s["attn"], 1)

            def c_z2(g):
                dve.wait_ge(s["saved"], g + 1)
                for u in range(U):
                    m = moments_all[:, bass.ds(g, 1), :, u].rearrange("p g a -> p (g a)")
                    dve.tensor_scalar(z2[:, u, :], x2_tile(g, u), m[:, 0:1], m[:, 1:2], ALU.subtract, ALU.mult)\
                        .then_inc(s["z2"], 1)

            def c_xp(g):
                dve.wait_ge(s["proj_mm"], g + 1)
                dve.wait_ge(s["resid"], g + 1)
                dve.wait_ge(s["z2"], (g + 1) * U)
                dve.tensor_tensor(xp[:, :, :], per_tile(bank[7]), z2[:, :, :], ALU.add).then_inc(s["xp"], 1)
                dve.wait_ge(s["xp"], g + 1)
                stats(g, 4, s["ln4"], lambda u: xp[:, u, :])

            def c_norm(g):
                dve.wait_ge(s["root4"], g + 1)
                dve.wait_ge(s["scattered"], g * (U * 2 * 16) + ZERO_STORES * 16)
                normalise(h2, 4, 5, lambda u: xp[:, u, :], s["h2n"])
                dve.wait_ge(s["row_id"], g + 1)
                dve.tensor_scalar(row_id, row_id, float(P * U), None, ALU.add).then_inc(s["row_id"], 1)

            route_steps = 25
            step = [0]

            def link(g, ins):
                step[0] += 1
                ins.then_inc(s["route"], 1)
                dve.wait_ge(s["route"], g * route_steps + step[0])

            def over_experts(ap):
                return ap.unsqueeze(2).broadcast_to([P, U, E])

            def c_select(g):
                step[0] = 0
                dve.wait_ge(s["logit_mm"], g + 1)
                link(g, dve.tensor_copy(lg[:, 0, :, :], bank[7][:, 0:U * E].rearrange("p (u e) -> p u e", u=U)))
                for k in range(2):
                    link(g, dve.tensor_reduce(first[:, k, :], lg[:, k, :, :], X, ALU.max))
                    link(g, dve.tensor_tensor(tie[:, k, :, :], lg[:, k, :, :], over_experts(first[:, k, :]),
                                              ALU.is_equal))
                    link(g, dve.tensor_tensor(tie[:, k, :, :], tie[:, k, :, :], over_tiles(rank, E), ALU.mult))
                    link(g, dve.tensor_reduce(tie_max[:, k, :], tie[:, k, :, :], X, ALU.max))
                    link(g, dve.tensor_tensor(sel[:, k, :, :], over_tiles(rank, E), over_experts(tie_max[:, k, :]),
                                              ALU.is_equal))
                    if k == 0:
                        link(g, dve.scalar_tensor_tensor(out=lg[:, 1, :, :], in0=sel[:, 0, :, :], scalar=-3e38,
                                                         in1=lg[:, 0, :, :], op0=ALU.mult, op1=ALU.add))
                dve.tensor_tensor(sel_l[:, :, :], sel[:, 0, :, :], sel[:, 1, :, :], ALU.add).then_inc(s["selected"], 1)
                dve.tensor_tensor(shifted[:, :, 0:E], lg[:, 0, :, :], over_experts(first[:, 0, :]), ALU.subtract)
                dve.tensor_tensor(shifted[:, :, E], first[:, 1, :], first[:, 0, :], ALU.subtract)\
                    .then_inc(s["expd"], 1)

            def c_slots(g):
                dve.wait_ge(s["pos_mm"], g + 1)
                link(g, dve.tensor_tensor(pos[:, 0, :, :], bank[7][:, 64:64 + U * E].rearrange("p (u e) -> p u e", u=U),
                                          over_tiles(count[:, 0, :], E), ALU.add))
                link(g, dve.tensor_tensor(count[:, 1, :], count[:, 0, :], bank[7][:, 128:128 + E], ALU.add))
                link(g, dve.tensor_copy(count[:, 0, :], count[:, 1, :]))
                link(g, dve.tensor_scalar(kept[:, :, :], pos[:, 0, :, :], float(CAP), None, ALU.is_le))
                link(g, dve.tensor_tensor(pos[:, 1, :, :], pos[:, 0, :, :], over_tiles(eoff, E), ALU.add))
                for k in range(2):
                    dve.tensor_tensor(picked[:, k, :, :], sel[:, k, :, :], pos[:, 1, :, :], ALU.mult)
                    last = dve.tensor_tensor(picked[:, 2 + k, :, :], sel[:, k, :, :], kept[:, :, :], ALU.mult)
                link(g, last)
                link(g, dve.tensor_reduce(slot[:, 0:2, :, :], picked[:, :, :, :], X, ALU.add))
                link(g, dve.tensor_tensor(slot[:, 2, :, :], slot[:, 0, :, :], slot[:, 1, :, :], ALU.mult))
                link(g, dve.tensor_scalar(slot[:, 3, :, :], slot[:, 1, :, :], -float(4 * SLOTS), float(4 * SLOTS),
                                          ALU.mult, ALU.add))
                link(g, dve.tensor_tensor(slot[:, 4, :, :], slot[:, 2, :, :], slot[:, 3, :, :], ALU.add))
                dve.tensor_copy(scatter_idx[:, :, :], slot[:, 4, :, :]).then_inc(s["slots"], 1)
                dve.wait_ge(s["expd"], (g + 1) * 2)
                link(g, dve.tensor_reduce(esum[:, :], expd[:, :, 0:E], X, ALU.add))
                link(g, dve.reciprocal(gate[:, 0, :], esum[:, :]))
                link(g, dve.tensor_tensor(gate[:, 1, :], gate[:, 0, :], expd[:, :, E], ALU.mult))
                dve.tensor_tensor(of_group(gates_all, g), gate[:, :, :], slot[:, 1, :, :], ALU.mult)\
                    .then_inc(s["d_done"], 1)
                assert step[0] == route_steps, step

            def iteration(group):
                run(b_shift, group[2], 3)
                run(b_attention, group[2], 1)
                run(a_state, group[1], 1)
                run(a_stats2, group[1])
                run(a_norm2, group[1])
                run(b_attention, group[2], 2)
                run(a_x2, group[1])
                run(a_stats0, group[0])
                run(b_attention, group[2], 3)
                run(b_stats, group[1])
                run(a_norm0, group[0])
                run(b_norm, group[1])
                run(c_z2, group[2])
                run(c_xp, group[2])
                run(b_qk, group[1], 0)
                run(b_qk, group[1], 1)
                run(b_rope, group[1])
                run(b_values, group[1])
                run(a_v0, group[0])
                run(b_rope_sum, group[1])
                run(a_softmax, group[0])
                run(c_norm, group[2])
                run(b_keys, group[1], 0)
                run(c_select, group[2])
                run(a_rsum0, group[0])
                run(b_keys, group[1], 1)
                run(b_shift, group[1], 0)
                run(a_x1, group[0])
                run(a_norm1, group[0])
                run(b_shift, group[1], 1)
                run(c_slots, group[2])
                run(a_kv, group[0], 0)
                run(a_kv, group[0], 1)
                run(b_shift, group[1], 2)
                run(a_kv, group[0], 2)
                run(b_attention, group[1], 0)
                run(a_kv, group[0], 3)
                run(a_state, group[0], 0)

            pipeline(dve, iteration)

            def take_rows(i, n):
                for c in range(2):
                    dve.wait_ge(s["tok_mm"], i * 4 + (2 * n + c + 1))
                    if c == 0:
                        wait_past(dve, s["hid_mm"], i * (4 * FC) + 2 * FC * n)
                    dve.tensor_copy(tokT[:, c, :], bank[c][:, :]).then_inc(s["tok"], 1)
                wait_apart(dve, s[f"contributed{n}"], (i + 1) * (8 * 16))
                dve.tensor_copy(y_idx[n][:, :], rows[n][:, :, D]).then_inc(s["y_idx"], 1)

            def add_offset(i, n):
                for c in range(2):
                    dve.wait_ge(s["exp_mm"], i * 4 + (2 * n + c + 1))
                    dve.tensor_tensor(y_sb[n][:, 4 * c:4 * c + 4, :], per_tile(bank[6 + c]),
                                      b2[:, bass.ds(i * 2 + n, 1), :].broadcast_to([P, 4, D]), ALU.add)\
                        .then_inc(s["expert_out"], 1)

            dve.wait_ge(s["b2_in"], 16)
            take_rows(0, 0)
            with dve.Fori(0, E // 2 - 1) as i:
                take_rows(i, 1)
                add_offset(i, 0)
                take_rows(i + 1, 0)
                add_offset(i, 1)
            take_rows(E // 2 - 1, 1)
            add_offset(E // 2 - 1, 0)
            add_offset(E // 2 - 1, 1)
            dve.wait_ge(s["resid"], GROUPS + 1)
            for g in range(GROUPS):
                dve.wait_ge(s[f"joined{g}"], 16)
                for u in range(U):
                    dve.scalar_tensor_tensor(
                        out=resid[:, g, u, :], in0=joined[g][:, 0, u, :], scalar=gates_all[:, g, 0, u:u + 1],
                        in1=resid[:, g, u, :], op0=ALU.mult, op1=ALU.add).then_inc(s["partial"], 1)
                dve.wait_ge(s["partial"], (g + 1) * U)
                dve.wait_ge(s["weighted"], (g + 1) * U)
                dve.tensor_tensor(resid[:, g, :, :], resid[:, g, :, :], joined[g][:, 1, :, :], ALU.add)\
                    .then_inc(s["result"], 1)

        @block.tensor
        def _(pe):
            pe.wait_ge(s["weights_in"], 16 * len(LOADS))
            for k in range(3):
                pe.matmul(bank[0][:, k * HD:(k + 1) * HD], xw_T[:, k, :], xw_h[:, k, :], start=True, stop=True)
            pe.wait_ge(s["prep_cast"], 2)
            pe.matmul(bank[1][:, 0:3 * D], bcols[:, 1, :], wqkv[:, :], start=True, stop=True)
            pe.matmul(bank[2][:, 0:D], bcols[:, 0, :], wo1[:, :], start=True, stop=True).then_inc(s["prep_mm"], 1)
            pe.wait_ge(s["prepared"], 1)
            pe.wait_ge(s["prep_pool"], 2)
            pe.wait_ge(s["presets"], PRESETS)

            def transposes(dst, src, sem, ready, counts):
                for u in range(U):
                    pe.wait_ge(ready, counts + u + 1)
                    mm = pe.transpose(dst[:, u * P:(u + 1) * P], src[:, u, :], ident)
                mm.then_inc(sem, 1)

            def a_context(g, n):
                pe.wait_ge(s["ctx_in"], (g + 1) * 16)
                wait_past(pe, s["x2"], g)
                for b in range(n * 4, n * 4 + 4):
                    mm = pe.transpose(bank[n][:, b % 4 * KEYS:(b % 4 + 1) * KEYS], ctx_sb[:, b, :], ident)
                mm.then_inc(s["ctxT_mm"], 1)

            def a_z0T(g):
                transposes(bank[2], z, s["z0T_mm"], s["z0"], g * U)

            def a_keys(g, n):
                pe.wait_ge(s["ctxT"], g * 2 + n + 1)
                pe.matmul(bank[n][0:HD, :], xw[:, 1, :], ctxT[:, n * 512:(n + 1) * 512], start=True,
                          stop=True).then_inc(s["k0_mm"], 1)

            def a_queries(g):
                pe.wait_ge(s["z0T"], g + 1)
                pe.matmul(bank[2][0:HD, :], xw[:, 0, :], zT[:, :], start=True, stop=True).then_inc(s["q0_mm"], 1)

            def a_v0(g):
                pe.wait_ge(s["k0"], g * 2 + 1)
                for b in range(GB):
                    mm = pe.matmul(bank[0][:, b * HD:(b + 1) * HD], ctxT[:, b * KEYS:(b + 1) * KEYS], xw[:, 2, :],
                                   start=True, stop=True)
                mm.then_inc(s["v0_mm"], 1)

            def a_scores(g):
                pe.wait_ge(s["q0"], g + 1)
                pe.wait_ge(s["k0"], (g + 1) * 2)
                for b in range(GB):
                    u, w = b // TB, b % TB
                    mm = pe.matmul(bank[1][w * S:(w + 1) * S, u * KEYS:(u + 1) * KEYS], q0T[:, b * S:(b + 1) * S],
                                   k0T[:, b * KEYS:(b + 1) * KEYS], start=True, stop=True)
                mm.then_inc(s["s0_mm"], 1)

            def a_p0T(g):
                transposes(bank[2], p0, s["p0T_mm"], s["p0"], g * U)

            def a_values(g):
                pe.wait_ge(s["p0T"], g + 1)
                pe.wait_ge(s["v0"], g + 1)
                for b in range(GB):
                    mm = pe.matmul(bank[0][0:HD, b * S:(b + 1) * S], v0[:, b, :], p0T[:, b * S:(b + 1) * S],
                                   start=True, stop=True)
                mm.then_inc(s["o0_mm"], 1)

            def a_y0(g):
                pe.wait_ge(s["o0"], g + 1)
                for u in range(U):
                    mm = pe.matmul(bank[1][:, u * D:(u + 1) * D], o0T[:, u * P:(u + 1) * P], wo_sum[:, :],
                                   start=True, stop=True)
                mm.then_inc(s["y0_mm"], 1)

            def a_z1T(g):
                transposes(bank[2], z, s["z1T_mm"], s["z1"], g * U)

            def a_kv(g, u):
                if u == 0:
                    pe.wait_ge(s["z1T"], g + 1)
                if u == U - 1:
                    pe.wait_ge(s["kv"], g * U + 1)
                pe.matmul(bank[KV_BANK[u]][:, :], zT[:, u * P:(u + 1) * P], wkv[:, :], start=True, stop=True)\
                    .then_inc(s["kv_mm"], 1)

            def a_q1(g):
                pe.wait_ge(s["kv"], g * U + 2)
                pe.matmul(bank[1][:, :], wq1[:, :], zT[:, :], start=True, stop=True).then_inc(s["q1_mm"], 1)

            def a_states(g, pair):
                if pair == 0:
                    pe.wait_ge(s["kv"], (g + 1) * U)
                else:
                    pe.wait_ge(s["q1"], g + 1)
                    pe.wait_ge(s["state"], g * U + 2)
                for v in range(2):
                    for k in range(2):
                        mm = pe.matmul(bank[STATE_BANK[pair][v]][:, k * TB * D:(k + 1) * TB * D],
                                       k1[:, 2 * pair + v, k, :],
                                       v1[:, 2 * pair + v, k, :, :].rearrange("p b e -> p (b e)"), start=True,
                                       stop=True)
                mm.then_inc(s["state_mm"], 1)

            def a_read_states(g):
                for u in range(U):
                    pe.wait_ge(s["state"], g * U + u + 1)
                    for b in range(TB):
                        mm = pe.matmul(bank[2][b * S:(b + 1) * S, u * D:(u + 1) * D],
                                       q1T[:, u * P + b * S:u * P + (b + 1) * S], state[:, u // 2, u % 2, b, :],
                                       start=True, stop=True)
                mm.then_inc(s["o1_mm"], 1)

            def a_n1T(g):
                transposes(bank[1], z, s["n1T_mm"], s["n1"], g * U)

            def a_y1(g):
                pe.wait_ge(s["n1T"], g + 1)
                for u in range(U):
                    mm = pe.matmul(bank[0][:, u * D:(u + 1) * D], zT[:, u * P:(u + 1) * P], wo1_g[:, :],
                                   start=True, stop=True)
                mm.then_inc(s["y1_mm"], 1)

            def b_hT(g):
                wait_past(pe, s["attn"], g * (U * TB))
                transposes(bank[3], h, s["h_T_mm"], s["h"], g * U)

            def b_qk(g, n):
                pe.wait_ge(s["hT"], g + 1)
                for u in (2 * n, 2 * n + 1):
                    mm = pe.matmul(bank[4 + n][:, u % 2 * 2 * D:(u % 2 + 1) * 2 * D], hT[:, u * P:(u + 1) * P],
                                   wqkv_g[:, 0:2 * D], start=True, stop=True)
                mm.then_inc(s["qk_mm"], 1)

            def b_values(g):
                for b in range(GB):
                    for n in range(2):
                        mm = pe.matmul(bank[6][n * S:(n + 1) * S, b * 64:(b + 1) * 64], hT[:, b * S:(b + 1) * S],
                                       wqkv_g[:, 2 * D + n * 64:2 * D + (n + 1) * 64], start=True, stop=True)
                mm.then_inc(s["v_mm"], 1)

            def b_qkT(g):
                wait_apart(pe, s["qkr"], g + 1)
                pe.wait_ge(s["vx"], (g + 1) * 2)
                for u in range(U):
                    for c in range(2):
                        for n in range(2):
                            o = (c * 2 + n) * P
                            mm = pe.transpose(bank[3 + u][0:64, o:o + P],
                                              qkr[:, u, c * D + n * 64:c * D + (n + 1) * 64], ident)
                    mm.then_inc(s["qkT_mm"], 1)

            def b_scores(g, u):
                if u % 2 == 0:
                    pe.wait_ge(s["kx"], g * (2 * HH_DVE) + (u // 2 + 1) * HH_DVE)
                    pe.wait_ge(s["kx_act"], g * (2 * (HH - HH_DVE)) + (u // 2 + 1) * (HH - HH_DVE))
                if u == 0:
                    pe.wait_ge(s["qT"], (g + 1) * 2 * U)
                else:
                    pe.wait_ge(s["ssub"], g * U + u)
                for n in range(2):
                    pe.matmul(bank[3 + n][:, :], qblk[:, u, n, :],
                              kx[:, u, n, :, :].rearrange("p h k -> p (h k)"), start=True, stop=False)
                    mm = pe.matmul(bank[3 + n][:, :], ident_l, causal_l, start=False, stop=True)
                mm.then_inc(s["s_mm"], 1)

            def b_probs_T(g, u, n):
                pe.wait_ge(s["probs"], g * U + u + 1)
                wait_past(pe, s["pT"], (g * U + u) * 2 + n)
                for j in range(4 * n, 4 * n + 4):
                    mm = pe.transpose(bank[5][:, j % 4 * P:(j % 4 + 1) * P], probs[:, u % 2, j * P:(j + 1) * P], ident)
                mm.then_inc(s["pT_mm"], 1)

            def b_attend(g, u):
                pe.wait_ge(s["pT"], (g * U + u + 1) * 2)
                if u >= 1:
                    pe.wait_ge(s["attn"], (g * U + u) * TB)
                w = TB * 2 * VW
                for j in range(H // 2):
                    mm = pe.matmul(bank[6][:, j * w:(j + 1) * w], pT[:, u % 2, j, :],
                                   vx[:, TB * u:TB * u + TB, j, :, :].rearrange("p b h c -> p b (h c)"),
                                   start=True, stop=True)
                mm.then_inc(s["pv_mm"], 1)

            def c_attnT(g):
                wait_past(pe, s["d_done"], g + 1)
                for u in range(U):
                    pe.wait_ge(s["attn"], (g * U + u + 1) * TB)
                    mm = pe.transpose(bank[7][:, u * P:(u + 1) * P], attn[:, u, :], ident)
                mm.then_inc(s["attnT_mm"], 1)

            def c_project(g):
                pe.wait_ge(s["attnT"], g + 1)
                for u in range(U):
                    mm = pe.matmul(bank[7][:, u * D:(u + 1) * D], attnT[:, u * P:(u + 1) * P], wproj[:, :],
                                   start=True, stop=True)
                mm.then_inc(s["proj_mm"], 1)

            def c_h2T(g):
                pe.wait_ge(s["h2"], g + 1)
                for u in range(U):
                    mm = pe.transpose(bank[7][:, u * P:(u + 1) * P], h2[:, u, :], ident)
                mm.then_inc(s["h2T_mm"], 1)

            def c_logits(g):
                pe.wait_ge(s["h2T"], g + 1)
                for u in range(U):
                    mm = pe.matmul(bank[7][:, u * E:(u + 1) * E], h2T[:, u * P:(u + 1) * P], wgate[:, :],
                                   start=True, stop=True)
                mm.then_inc(s["logit_mm"], 1)

            def c_count(g):
                pe.wait_ge(s["selected"], g + 1)
                for v in range(U):
                    o = 64 + v * E
                    pe.matmul(bank[7][:, o:o + E], tri_l, sel_l[:, v, :], start=True, stop=(v == 0))
                    for u in range(v):
                        pe.matmul(bank[7][:, o:o + E], ones_l, sel_l[:, u, :], start=False, stop=(u == v - 1))
                for u in range(U):
                    mm = pe.matmul(bank[7][:, 128:128 + E], ones_l, sel_l[:, u, :], start=(u == 0),
                                   stop=(u == U - 1))
                mm.then_inc(s["pos_mm"], 1)

            def iteration(group):
                run(a_n1T, group[1])
                run(a_y1, group[1])
                run(b_attend, group[2], 3)
                run(a_context, group[0], 0)
                run(a_context, group[0], 1)
                run(c_attnT, group[2])
                run(a_keys, group[0], 0)
                run(a_keys, group[0], 1)
                run(a_z0T, group[0])
                run(b_hT, group[1])
                run(c_project, group[2])
                run(b_qk, group[1], 0)
                run(a_v0, group[0])
                run(b_qk, group[1], 1)
                run(a_queries, group[0])
                run(b_values, group[1])
                run(a_scores, group[0])
                run(b_qkT, group[1])
                run(c_h2T, group[2])
                run(c_logits, group[2])
                run(a_p0T, group[0])
                run(b_scores, group[1], 0)
                run(a_values, group[0])
                run(c_count, group[2])
                run(a_y0, group[0])
                run(b_scores, group[1], 1)
                run(a_z1T, group[0])
                run(b_probs_T, group[1], 0, 0)
                run(a_kv, group[0], 0)
                run(a_kv, group[0], 1)
                run(b_probs_T, group[1], 0, 1)
                run(b_scores, group[1], 2)
                run(b_attend, group[1], 0)
                run(a_kv, group[0], 2)
                run(a_kv, group[0], 3)
                run(b_probs_T, group[1], 1, 0)
                run(b_scores, group[1], 3)
                run(a_q1, group[0])
                run(b_probs_T, group[1], 1, 1)
                run(a_states, group[0], 0)
                run(b_probs_T, group[1], 2, 0)
                run(b_attend, group[1], 1)
                run(a_states, group[0], 1)
                run(b_probs_T, group[1], 2, 1)
                run(a_read_states, group[0])
                run(b_probs_T, group[1], 3, 0)
                run(b_attend, group[1], 2)
                run(b_probs_T, group[1], 3, 1)

            pipeline(pe, iteration)

            def rows_T(i, n):
                pe.wait_ge((s["rows_in0"], s["rows_in1"])[n], (i + 1) * 16)
                for c in range(2):
                    for r in range(4):
                        mm = pe.transpose(bank[c][:, r * P:(r + 1) * P], rows[n][:, 4 * c + r, 0:D], ident)
                    mm.then_inc(s["tok_mm"], 1)

            def first_products(i, n):
                pe.wait_ge((s["w_in0"], s["w_in1"])[n], (i + 1) * 32)
                for c in range(2):
                    pe.wait_ge(s["tok"], i * 4 + (2 * n + c + 1))
                    for f in range(FC):
                        if c == 1:
                            pe.wait_ge(s["hid"], i * (4 * FC) + (2 * FC * n + f + 1))
                        pe.matmul(bank[2 + f][:, :], w1_sb[n][:, f * P:(f + 1) * P], tokT[:, c, :], start=True,
                                  stop=True).then_inc(s["hid_mm"], 1)

            def second_products(i, n):
                wait_past(pe, s["expert_out"], i * 4 + 2 * n)
                for c in range(2):
                    pe.wait_ge(s["hid"], i * (4 * FC) + (2 * FC * n + (c + 1) * FC))
                    for r in range(4):
                        for f in range(FC):
                            mm = pe.matmul(bank[6 + c][:, r * D:(r + 1) * D], hid[:, c, f, r * P:(r + 1) * P],
                                           w2_sb[n][:, f, :], start=(f == 0), stop=(f == FC - 1))
                    mm.then_inc(s["exp_mm"], 1)

            rows_T(0, 0)
            first_products(0, 0)
            rows_T(0, 1)
            second_products(0, 0)
            with pe.Fori(0, E // 2 - 1) as i:
                first_products(i, 1)
                rows_T(i + 1, 0)
                second_products(i, 1)
                first_products(i + 1, 0)
                rows_T(i + 1, 1)
                second_products(i + 1, 0)
            first_products(E // 2 - 1, 1)
            second_products(E // 2 - 1, 1)


def constants():
    import numpy as np

    f = np.zeros((P, C_WIDTH), np.float32)
    p = np.arange(P)
    f[:, C_IDENT:C_IDENT + P] = np.eye(P)
    inv_freq = (1.0 / 10000.0 ** (np.arange(0, HD, 2, dtype=np.float32) / np.float32(HD))).astype(np.float32)
    ang = ((p % S).astype(np.float32)[:, None] * inv_freq).astype(np.float32)
    f[:, C_COS:C_COS + 4] = np.cos(ang)
    f[:, C_SIN:C_SIN + 4] = np.sin(ang)
    f[:, C_NSIN:C_NSIN + 4] = -np.sin(ang)
    f[:, C_BLOCK:C_BLOCK + D] = (p[:, None] // HD == np.arange(D)[None, :] // HD) * 2.0 ** -18
    f[:, C_HEAD:C_HEAD + HH] = (p[:, None] // HD) % HH == np.arange(HH)[None, :]
    f[:, C_RANK:C_RANK + E] = E - np.arange(E)
    f[:, C_EOFF:C_EOFF + E] = np.arange(E) * CAP - 1
    place = np.arange(2)[None, :, None] * TOKENS + p[:, None, None] * U + np.arange(U)[None, None, :] - P * U
    f[:, C_ROWID:C_ROWID + 2 * U] = place.reshape(P, 2 * U)
    b = np.zeros((P, L_WIDTH), np.float32)
    b[:, L_IDENT:L_IDENT + P] = np.eye(P)
    b[:, L_TRI:L_TRI + P] = p[:, None] <= p[None, :]
    b[:, L_ONES:L_ONES + P] = 1.0
    key = np.arange(HH * S) % S
    b[:, L_CAUSAL:] = np.where(key[None, :] <= (p % S)[:, None], 0.0, -(2.0 ** 32))
    return f, b


def kernel(**inputs):
    import numpy as np
    import concourse.bacc as bacc
    from concourse.bass_utils import run_bass_kernel_spmd

    a = {k: np.asarray(v) for k, v in inputs.items()}
    f, b = constants()
    qkv = a["L0_ffn_Wqkv"].reshape(D, H, 3, HD)
    awk, awv = a["L0_attn_Wk"], a["L0_attn_Wv"]
    abk, abv = a["L0_attn_bk"], a["L0_attn_bv"]
    packed = {
        "xw_T": np.stack([a["L0_xattn_Wq"].T, a["L0_xattn_Wk"].T, a["L0_xattn_Wv"].T], 1),
        "xw_h": np.stack([a["L0_xattn_wq_h"], a["L0_xattn_wk_h"], a["L0_xattn_wv_h"]], 1),
        "cols": np.stack([a["L0_attn_ln_g"], a["L0_attn_ln_b"], a["L0_ffn_ln1_g"], a["L0_ffn_ln1_b"]], 1),
        "bq1": a["L0_attn_bq"],
        "wqkv": np.concatenate([qkv[:, :, 0].reshape(D, D), qkv[:, :, 1].reshape(D, D),
                                qkv[:, 0::2, 2].reshape(D, D // 2), qkv[:, 1::2, 2].reshape(D, D // 2)], 1),
        "wo1": a["L0_attn_Wo"],
        "wq1": a["L0_attn_Wq"],
        "wkv": np.concatenate([awk[0], awv[0], awk[1], awv[1]], 1),
        "wproj": a["L0_ffn_Wproj"],
        "wgate": a["L0_ffn_Wgate"],
        "b1c": a["L0_ffn_b1"].reshape(E, FC, P).transpose(2, 0, 1),
    }
    arrays = {
        "x": a["x"],
        "ctx_1024": a["ctx_1024"],
        "mask": a["mask_SxS2_bk1"].view(np.uint8),
        "const_f32": f,
        "const_low": b,
        "weights": np.concatenate([packed[name].reshape(P, width) for name, width in WEIGHTS], 1),
        "row_params": np.concatenate([a["L0_xattn_bv_h"], abk[0], abv[0], abk[1], abv[1], a["L0_attn_bo"],
                                      a["L0_ffn_ln2_g"], a["L0_ffn_ln2_b"]]),
        "by_head": np.concatenate([a["L0_xattn_Wo"].reshape(H, HD, D).transpose(1, 0, 2).reshape(HD, H * D),
                                   np.stack([a["L0_xattn_bq_h"], a["L0_xattn_bk_h"]], 1)], 1),
        "w1": a["L0_ffn_W1"],
        "w2": a["L0_ffn_W2"],
        "b2": a["L0_ffn_b2"],
    }
    arrays = {k: np.ascontiguousarray(v) for k, v in arrays.items()}
    nc = bacc.Bacc("TRN2", target_bir_lowering=False, num_devices=1)
    t = {
        n: nc.dram_tensor("in_" + n, list(v.shape), mybir.dt.from_np(v.dtype), kind="ExternalInput").ap()
        for n, v in arrays.items()}
    out = nc.dram_tensor("out", [B, S, D], F32, kind="ExternalOutput").ap()
    build_program(nc, t, out)
    r = run_bass_kernel_spmd(nc, [{"in_" + n: v for n, v in arrays.items()}], core_ids=[0])
    return r.results[0]["out"]
```
